# Optimizing a Trainium2 kernel written in Bass

```python
import numpy as np
import jax
import jax.numpy as jnp

def _softmax(x, axis=-1):
    return jax.nn.softmax(x, axis=axis)

def _gelu(x):
    return jax.nn.gelu(x, approximate=True)

def _silu(x):
    return jax.nn.silu(x)

def _sigmoid(x):
    return jax.nn.sigmoid(x)

def _layernorm(x, axis=-1, eps=1e-05):
    m = jnp.mean(x, axis=axis, keepdims=True)
    v = jnp.var(x, axis=axis, keepdims=True)
    return (x - m) / jnp.sqrt(v + eps)

def _scatter_add(tgt, idx, src, axis=0):
    return tgt.at[idx].add(src)

def _segment_sum(src, seg, n):
    return jax.ops.segment_sum(src, seg, n)
kernel_name = 'mk_gnn_ffn_d1_gnn_r8_314423'

def setup_inputs(seed: int=0):
    np.random.seed(seed)
    _w = jnp.asarray

    def _rec_inputs():
        import jax
        import jax.numpy as jnp
        _gk = jax.random.key(seed)
        x = -0.0003713 + 1 * jax.random.normal(jax.random.fold_in(_gk, 1), (6250, 256), jnp.float32)
        _s = jax.random.randint(jax.random.fold_in(_gk, 2), (50000,), 0, 6250, jnp.int32)
        _d = jax.random.randint(jax.random.fold_in(_gk, 3), (50000,), 0, 6250, jnp.int32)
        _loop = jnp.arange(6250, dtype=jnp.int32)
        src = jnp.concatenate([_s, _d, _loop])
        dst = jnp.concatenate([_d, _s, _loop])
        _o = jnp.argsort(dst, stable=True)
        src = src[_o]
        dst = dst[_o]
        return (x, src, dst)
    x, src, dst = _rec_inputs()

    def _L0_gnn_setup():
        import jax, jax.numpy as jnp
        import numpy as np
        H, C, D = (4, 16, 256)
        HC = H * C
        N_NODES, N_EDGES = (6250, 200000)

        def _lin_params(key, out_dim, in_dim):
            k1, k2 = jax.random.split(key)
            s = 1.0 / np.sqrt(in_dim).astype(np.float32)
            W = jax.random.uniform(k1, (out_dim, in_dim), minval=-s, maxval=s, dtype=jnp.float32)
            b = jax.random.uniform(k2, (out_dim,), minval=-s, maxval=s, dtype=jnp.float32)
            return (W, b)

        def _transformer_conv(x, edge_index, Wq, bq, Wk, bk, Wv, bv, Ws, bs):
            N = x.shape[0]
            src, dst = (edge_index[0], edge_index[1])
            q = (x @ Wq.T + bq).reshape(N, H, C)
            k = (x @ Wk.T + bk).reshape(N, H, C)
            v = (x @ Wv.T + bv).reshape(N, H, C)
            logits = (q[dst] * k[src]).sum(-1) * (1.0 / np.sqrt(C).astype(np.float32))
            m = jax.ops.segment_max(logits, dst, num_segments=N)
            e = jnp.exp(logits - m[dst])
            denom = jax.ops.segment_sum(e, dst, num_segments=N)
            alpha = e / (denom[dst] + 1e-16)
            msg = v[src] * alpha[..., None]
            out = jax.ops.segment_sum(msg, dst, num_segments=N).reshape(N, HC)
            return out + x @ Ws.T + bs
        key = jax.random.key(seed)
        ks = jax.random.split(key, 12)
        x = jax.random.normal(ks[0], (N_NODES, D), dtype=jnp.float32)
        edge_index = jax.random.randint(ks[1], (2, N_EDGES), 0, N_NODES, dtype=jnp.int32)
        Wq1, bq1 = _lin_params(ks[2], HC, D)
        Wk1, bk1 = _lin_params(ks[3], HC, D)
        Wv1, bv1 = _lin_params(ks[4], HC, D)
        Ws1, bs1 = _lin_params(ks[5], HC, D)
        Wq2, bq2 = _lin_params(ks[6], HC, HC)
        Wk2, bk2 = _lin_params(ks[7], HC, HC)
        Wv2, bv2 = _lin_params(ks[8], HC, HC)
        Ws2, bs2 = _lin_params(ks[9], HC, HC)
        Wo, bo = _lin_params(ks[10], D, HC)
        return dict(x=x, edge_index=edge_index, Wq1=Wq1, bq1=bq1, Wk1=Wk1, bk1=bk1, Wv1=Wv1, bv1=bv1, Ws1=Ws1, bs1=bs1, Wq2=Wq2, bq2=bq2, Wk2=Wk2, bk2=bk2, Wv2=Wv2, bv2=bv2, Ws2=Ws2, bs2=bs2, Wo=Wo, bo=bo)
    _L0_gnn_all = _L0_gnn_setup()
    _L0_gnn_in = {k: v for k, v in _L0_gnn_all.items() if k in ('Wq1', 'bq1', 'Wk1', 'bk1', 'Wv1', 'bv1', 'Ws1', 'bs1', 'Wq2', 'bq2', 'Wk2', 'bk2', 'Wv2', 'bv2', 'Ws2', 'bs2', 'Wo', 'bo')}
    del _L0_gnn_all

    def _L0_ffn_setup():
        import jax, jax.numpy as jnp
        import numpy as np
        BN_EPS = 0.001

        def _bn(h, g, b, m, v):
            return g * (h - m) * jax.lax.rsqrt(v + BN_EPS) + b
        key = jax.random.key(seed)
        ks = jax.random.split(key, 8)
        B, F, Df = (256, 64, 256)
        E, H, D = (8, 256, 256)
        s1 = 1.0 / np.sqrt(Df)
        s2 = 1.0 / np.sqrt(H)
        return {'x': jax.random.normal(ks[0], (B, F, Df), jnp.float32), 'Wr': jax.random.normal(ks[1], (Df, E), jnp.float32) * s1, 'br': jnp.zeros((E,), jnp.float32), 'W1': jax.random.normal(ks[2], (E, Df, H), jnp.float32) * s1, 'b1': jnp.zeros((E, H), jnp.float32), 'g1': jnp.ones((E, H), jnp.float32), 'be1': jnp.zeros((E, H), jnp.float32), 'm1': jnp.zeros((E, H), jnp.float32), 'v1': jnp.ones((E, H), jnp.float32), 'W2': jax.random.normal(ks[3], (E, H, H), jnp.float32) * s2, 'b2': jnp.zeros((E, H), jnp.float32), 'g2': jnp.ones((E, H), jnp.float32), 'be2': jnp.zeros((E, H), jnp.float32), 'm2': jnp.zeros((E, H), jnp.float32), 'v2': jnp.ones((E, H), jnp.float32), 'Wo': jax.random.normal(ks[4], (E, H, D), jnp.float32) * s2, 'bo': jnp.zeros((E, D), jnp.float32)}
    _L0_ffn_all = _L0_ffn_setup()
    _L0_ffn_in = {k: v for k, v in _L0_ffn_all.items() if k in ('Wr', 'br', 'W1', 'b1', 'g1', 'be1', 'm1', 'v1', 'W2', 'b2', 'g2', 'be2', 'm2', 'v2', 'Wo', 'bo')}
    del _L0_ffn_all
    return {'x': x, 'src': src, 'dst': dst, 'L0_gnn_Wq1': _L0_gnn_in['Wq1'], 'L0_gnn_bq1': _L0_gnn_in['bq1'], 'L0_gnn_Wk1': _L0_gnn_in['Wk1'], 'L0_gnn_bk1': _L0_gnn_in['bk1'], 'L0_gnn_Wv1': _L0_gnn_in['Wv1'], 'L0_gnn_bv1': _L0_gnn_in['bv1'], 'L0_gnn_Ws1': _L0_gnn_in['Ws1'], 'L0_gnn_bs1': _L0_gnn_in['bs1'], 'L0_gnn_Wq2': _L0_gnn_in['Wq2'], 'L0_gnn_bq2': _L0_gnn_in['bq2'], 'L0_gnn_Wk2': _L0_gnn_in['Wk2'], 'L0_gnn_bk2': _L0_gnn_in['bk2'], 'L0_gnn_Wv2': _L0_gnn_in['Wv2'], 'L0_gnn_bv2': _L0_gnn_in['bv2'], 'L0_gnn_Ws2': _L0_gnn_in['Ws2'], 'L0_gnn_bs2': _L0_gnn_in['bs2'], 'L0_gnn_Wo': _L0_gnn_in['Wo'], 'L0_gnn_bo': _L0_gnn_in['bo'], 'L0_ffn_Wr': _L0_ffn_in['Wr'], 'L0_ffn_br': _L0_ffn_in['br'], 'L0_ffn_W1': _L0_ffn_in['W1'], 'L0_ffn_b1': _L0_ffn_in['b1'], 'L0_ffn_g1': _L0_ffn_in['g1'], 'L0_ffn_be1': _L0_ffn_in['be1'], 'L0_ffn_m1': _L0_ffn_in['m1'], 'L0_ffn_v1': _L0_ffn_in['v1'], 'L0_ffn_W2': _L0_ffn_in['W2'], 'L0_ffn_b2': _L0_ffn_in['b2'], 'L0_ffn_g2': _L0_ffn_in['g2'], 'L0_ffn_be2': _L0_ffn_in['be2'], 'L0_ffn_m2': _L0_ffn_in['m2'], 'L0_ffn_v2': _L0_ffn_in['v2'], 'L0_ffn_Wo': _L0_ffn_in['Wo'], 'L0_ffn_bo': _L0_ffn_in['bo']}

def reference(x, src, dst, L0_gnn_Wq1, L0_gnn_bq1, L0_gnn_Wk1, L0_gnn_bk1, L0_gnn_Wv1, L0_gnn_bv1, L0_gnn_Ws1, L0_gnn_bs1, L0_gnn_Wq2, L0_gnn_bq2, L0_gnn_Wk2, L0_gnn_bk2, L0_gnn_Wv2, L0_gnn_bv2, L0_gnn_Ws2, L0_gnn_bs2, L0_gnn_Wo, L0_gnn_bo, L0_ffn_Wr, L0_ffn_br, L0_ffn_W1, L0_ffn_b1, L0_ffn_g1, L0_ffn_be1, L0_ffn_m1, L0_ffn_v1, L0_ffn_W2, L0_ffn_b2, L0_ffn_g2, L0_ffn_be2, L0_ffn_m2, L0_ffn_v2, L0_ffn_Wo, L0_ffn_bo):
    import jax
    import jax.numpy as jnp

    def _L0_gnn_ref(x, edge_index, Wq1, bq1, Wk1, bk1, Wv1, bv1, Ws1, bs1, Wq2, bq2, Wk2, bk2, Wv2, bv2, Ws2, bs2, Wo, bo):
        import jax, jax.numpy as jnp
        import numpy as np
        H, C, D = (4, 16, 256)
        HC = H * C
        N_NODES, N_EDGES = (6250, 200000)

        def _lin_params(key, out_dim, in_dim):
            k1, k2 = jax.random.split(key)
            s = 1.0 / np.sqrt(in_dim).astype(np.float32)
            W = jax.random.uniform(k1, (out_dim, in_dim), minval=-s, maxval=s, dtype=jnp.float32)
            b = jax.random.uniform(k2, (out_dim,), minval=-s, maxval=s, dtype=jnp.float32)
            return (W, b)

        def _transformer_conv(x, edge_index, Wq, bq, Wk, bk, Wv, bv, Ws, bs):
            N = x.shape[0]
            src, dst = (edge_index[0], edge_index[1])
            q = (x @ Wq.T + bq).reshape(N, H, C)
            k = (x @ Wk.T + bk).reshape(N, H, C)
            v = (x @ Wv.T + bv).reshape(N, H, C)
            logits = (q[dst] * k[src]).sum(-1) * (1.0 / np.sqrt(C).astype(np.float32))
            m = jax.ops.segment_max(logits, dst, num_segments=N)
            e = jnp.exp(logits - m[dst])
            denom = jax.ops.segment_sum(e, dst, num_segments=N)
            alpha = e / (denom[dst] + 1e-16)
            msg = v[src] * alpha[..., None]
            out = jax.ops.segment_sum(msg, dst, num_segments=N).reshape(N, HC)
            return out + x @ Ws.T + bs
        h = jax.nn.relu(_transformer_conv(x, edge_index, Wq1, bq1, Wk1, bk1, Wv1, bv1, Ws1, bs1))
        h = jax.nn.relu(_transformer_conv(h, edge_index, Wq2, bq2, Wk2, bk2, Wv2, bv2, Ws2, bs2))
        return jax.nn.sigmoid(h @ Wo.T + bo)

    def _L0_ffn_ref(x, Wr, br, W1, b1, g1, be1, m1, v1, W2, b2, g2, be2, m2, v2, Wo, bo):
        import jax, jax.numpy as jnp
        import numpy as np
        BN_EPS = 0.001

        def _bn(h, g, b, m, v):
            return g * (h - m) * jax.lax.rsqrt(v + BN_EPS) + b
        feat = jnp.mean(x, axis=0)
        w = jax.nn.softmax(feat @ Wr + br, axis=-1)
        h = jnp.einsum('bfd,edh->bfeh', x, W1) + b1
        h = jax.nn.relu(_bn(h, g1, be1, m1, v1))
        h = jnp.einsum('bfeh,ehk->bfek', h, W2) + b2
        h = jax.nn.relu(_bn(h, g2, be2, m2, v2))
        y = jnp.einsum('bfeh,ehd->bfed', h, Wo) + bo
        return jnp.einsum('bfed,fe->bfd', y, w)
    edge_index = jnp.stack([src, dst])
    x = x + _L0_gnn_ref(_layernorm(x, axis=-1), edge_index, L0_gnn_Wq1, L0_gnn_bq1, L0_gnn_Wk1, L0_gnn_bk1, L0_gnn_Wv1, L0_gnn_bv1, L0_gnn_Ws1, L0_gnn_bs1, L0_gnn_Wq2, L0_gnn_bq2, L0_gnn_Wk2, L0_gnn_bk2, L0_gnn_Wv2, L0_gnn_bv2, L0_gnn_Ws2, L0_gnn_bs2, L0_gnn_Wo, L0_gnn_bo)
    x = x + _L0_ffn_ref(_layernorm(x, axis=-1)[None], L0_ffn_Wr, L0_ffn_br, L0_ffn_W1, L0_ffn_b1, L0_ffn_g1, L0_ffn_be1, L0_ffn_m1, L0_ffn_v1, L0_ffn_W2, L0_ffn_b2, L0_ffn_g2, L0_ffn_be2, L0_ffn_m2, L0_ffn_v2, L0_ffn_Wo, L0_ffn_bo)[0]
    return x

_drawn_inputs = setup_inputs


def setup_inputs(seed=0):
    import zlib

    import numpy as np

    out = dict(_drawn_inputs(seed))
    spreads = {'L0_ffn_br': (0.0, 0.269),
     'L0_ffn_b1': (0.0, 0.357),
     'L0_ffn_g1': (1.0, 0.2),
     'L0_ffn_be1': (0.0, 0.364),
     'L0_ffn_m1': (0.0, 0.357),
     'L0_ffn_v1': (1.0, 0.6),
     'L0_ffn_b2': (0.0, 0.1),
     'L0_ffn_g2': (1.0, 0.2),
     'L0_ffn_be2': (0.0, 0.1),
     'L0_ffn_m2': (0.0, 0.1),
     'L0_ffn_v2': (1.0, 0.6),
     'L0_ffn_bo': (0.0, 0.1)}
    factors = {'L0_gnn_Wq1': 8.0,
     'L0_gnn_bq1': 8.0,
     'L0_gnn_Wk1': 8.0,
     'L0_gnn_bk1': 8.0,
     'L0_gnn_Wv1': 8.0,
     'L0_gnn_bv1': 8.0,
     'L0_gnn_Ws1': 3.428,
     'L0_gnn_bs1': 8.0,
     'L0_gnn_Wq2': 8.0,
     'L0_gnn_bq2': 8.0,
     'L0_gnn_Wk2': 8.0,
     'L0_gnn_bk2': 8.0,
     'L0_gnn_Wv2': 4.583,
     'L0_gnn_bv2': 8.0,
     'L0_gnn_Ws2': 2.886,
     'L0_gnn_bs2': 8.0,
     'L0_gnn_bo': 3.532}
    for name, (base, spread) in spreads.items():
        noise = np.random.default_rng([zlib.crc32(name.encode()), seed]).standard_normal(out[name].shape)
        drawn = base * np.exp(spread * noise) if base else spread * noise
        out[name] = jnp.asarray(drawn.astype(out[name].dtype))
    for name, factor in factors.items():
        out[name] = (out[name] * factor).astype(out[name].dtype)
    return out
```

```python
from contextlib import ExitStack

import numpy as np

import concourse.bass as bass
from concourse import mybir

F32 = mybir.dt.float32
BF16 = mybir.dt.bfloat16
I32 = mybir.dt.int32
ALU = mybir.AluOpType
ACT = mybir.ActivationFunctionType
AX = mybir.AxisListType
ts = bass.ts

P = 128
N, E, D = 6250, 106250, 256
HEADS, CH = 4, 16
HC = HEADS * CH
EXPERTS, HID = 8, 256
KC = D // P
LN_EPS, BN_EPS, DEN_EPS = 1e-5, 1e-3, 1e-16

NT = -(-N // P)
NP = NT * P
GROUP = 7
NG = NT // GROUP
assert NG * GROUP == NT

STREAMS = 2
STEP = 512
TPB = STEP // P
UNROLL = 4
BLOCKS = -(-E // (STREAMS * STEP * UNROLL)) * UNROLL
STEPS = BLOCKS // UNROLL
HALF = BLOCKS * STEP
EP = STREAMS * HALF
ROW = HC + 2 * HEADS
DEN, MAX = HC, HC + HEADS

SROWS, SCOLS = 425, 250
assert SROWS * SCOLS == E
NEG = -3.0e38
SKIP = float(1 << 22)

Q0, K0, S0 = 0, HC, 3 * HC
PROJ = 4 * HC
HTOK = GROUP * P // 2


def each_group(eng, body):
    body(0)
    with eng.Fori(1, NG) as g:
        body(g)


class Steps:

    def __init__(self, eng, done, at=0):
        self.eng, self.done, self.at = eng, done, at

    def __call__(self, instruction):
        self.at = self.at + 1
        instruction.then_inc(self.done, 1)
        self.eng.wait_ge(self.done, self.at)


def build(nc, d):
    kv_t = nc.dram_tensor("kv_table", [NP, 2 * HC], F32, kind="Internal").ap()
    q_t = nc.dram_tensor("q_table", [NP, HC], F32, kind="Internal").ap()
    qz_t = nc.dram_tensor("q_at_starts", [EP, HC], F32, kind="Internal").ap()
    sum_t = nc.dram_tensor("running_sums", [EP, ROW], F32, kind="Internal").ap()
    mask_t = nc.dram_tensor("masks", [STREAMS, BLOCKS, 2 * STEP], BF16, kind="Internal").ap()
    qz_blocks = qz_t.rearrange("(b j p s) c -> b p j (s c)", j=TPB, p=P, s=STREAMS)
    sum_blocks = sum_t.rearrange("(b j p s) c -> b p j (s c)", j=TPB, p=P, s=STREAMS)
    kv_nodes = kv_t.rearrange("(i p) c -> p i c", p=P)
    q_nodes = q_t.rearrange("(i p) c -> p i c", p=P)

    with ExitStack() as whole:
        def keep(name, shape, dt=F32):
            return whole.enter_context(nc.sbuf_tensor(name, shape, dt))

        x_sb = keep("x_sb", [P, NT, D])
        proj = keep("proj", [P, NT, PROJ])
        yT = proj[:, :, :].rearrange("p i c -> p (i c)").rearrange("p (k n) -> p k n", k=KC)
        identity = keep("identity", [P, P])
        head_sum = keep("head_sum", [P, P])
        pick = keep("pick", [P, STREAMS * HEADS])
        start_row = keep("start_row", [P, NT], I32)
        end_row = keep("end_row", [P, NT], I32)
        span_bias = keep("span_bias", [P, NT])
        present = keep("present", [P, NT])
        cut_ix = keep("cut_ix", [16, 1], I32)
        cut_q = keep("cut_q", [16, HC])
        eps = keep("eps", [P, 1])
        mv = keep("mv", [P, NT, 2])
        rstd = keep("rstd", [P, NT])
        stat = keep("stat", [P, NT, 6])
        gate = keep("gate", [P, NT, EXPERTS])

        def scatter_q(pool, done, projected):
            for i in range(NT):
                pool.wait_ge(projected, i + 1)
                pool.indirect_dma_start(qz_t, bass.IndirectOffsetOnAxis(start_row[:, i:i + 1], 0),
                                        proj[:, i, Q0:Q0 + HC], None,
                                        bounds_check=EP - 1, oob_is_err=False).then_inc(done, 16)

        def scatter_cut(pool, done, stored, got, cut_done):
            pool.wait_ge(stored, 16 * 2 * NG)
            pool.indirect_dma_start(cut_q[:, :], None, q_t, bass.IndirectOffsetOnAxis(cut_ix[:, :], 0),
                                    bounds_check=NP - 1, oob_is_err=False).then_inc(got, 16)
            pool.wait_ge(got, 16)
            pool.wait_ge(done, 16 * NT)
            pool.dma_start(qz_t[1:2, :], cut_q[0:1, :]).then_inc(cut_done, 16)
            pool.wait_ge(cut_done, 16)

        def store_tables(sp, projected, stored):
            with sp.Fori(0, NG) as g:
                sp.wait_ge(projected, GROUP * g + GROUP)
                sp.dma_start(kv_nodes[:, ts(g, GROUP), :], proj[:, ts(g, GROUP), K0:S0]).then_inc(stored, 16)
                sp.dma_start(q_nodes[:, ts(g, GROUP), :], proj[:, ts(g, GROUP), Q0:K0]).then_inc(stored, 16)
            sp.wait_ge(stored, 16 * 2 * NG)

        def layer_norm_stats(dve, done, aggregated, rooted):
            with dve.Fori(0, NG) as g:
                for u in range(GROUP):
                    ins = dve.bn_stats(stat[:, ts(GROUP * g + u, 1), :].rearrange("p i c -> p (i c)"), x_sb[:, GROUP * g + u, :])
                ins.then_inc(done, 1)
            dve.wait_ge(done, NG)
            step = Steps(dve, done, NG)
            mean, var = mv[:, :, 0], mv[:, :, 1]
            step(dve.tensor_tensor(mean, stat[:, :, 1], stat[:, :, 4], ALU.subtract))
            step(dve.tensor_tensor(var, mean, mean, ALU.mult))
            step(dve.scalar_tensor_tensor(var, var, D / 4.0, stat[:, :, 2], ALU.mult, ALU.add))
            step(dve.tensor_tensor(var, var, stat[:, :, 5], ALU.add))
            step(dve.tensor_scalar(var, var, 1.0 / D, None, ALU.mult))
            step(dve.tensor_tensor(mean, stat[:, :, 1], stat[:, :, 4], ALU.add))
            step(dve.tensor_scalar(mean, mean, 0.5, None, ALU.mult))
            dve.sem_inc(aggregated, 1)
            dve.wait_ge(rooted, 1)
            step(dve.reciprocal(rstd[:, :], rstd[:, :]))

        def root_variance(act, aggregated, rooted):
            act.wait_ge(aggregated, 1)
            act.activation(rstd[:, :], mv[:, :, 1], ACT.Sqrt, bias=eps[:, 0:1]).then_inc(rooted, 1)

        with ExitStack() as phase:
            def sb(name, shape, dt=F32):
                return phase.enter_context(nc.sbuf_tensor(name, shape, dt))

            def pb(name):
                return phase.enter_context(nc.psum_tensor(name, [P, 512], F32))

            def sem(name):
                return whole.enter_context(nc.semaphore(name))

            node_i = sb("node_i", [P, NT], I32)
            node = sb("node", [P, NT])
            samples_i = sb("samples_i", [P, SROWS], I32)
            samples = sb("samples", [P, SROWS])
            below = sb("below", [P, GROUP, SROWS], BF16)
            found = sb("found", [P, NT])
            chunk_no = sb("chunk_no", [P, NT])
            chunk_ix = sb("chunk_ix", [P, NT], I32)
            chunk = sb("chunk", [P, NT, SCOLS], I32)
            start = sb("start", [P, NT + 1])
            nxt = sb("nxt", [P, NT])
            t0 = sb("t0", [P, NT])
            t1 = sb("t1", [P, NT])
            shift = sb("shift", [P, P])
            wrap = sb("wrap", [P, P])
            zeros = sb("zeros", [P, EP * HC // P // 32])
            dst_b = sb("dst_b", [BLOCKS, STREAMS, STEP], I32)
            prev_b = sb("prev_b", [BLOCKS, STREAMS, STEP], I32)
            mask_b = sb("mask_b", [BLOCKS, STREAMS, 2, STEP], BF16)
            w1t = sb("w1t", [P, KC, PROJ])
            b1 = sb("b1", [P, PROJ])
            xh = sb("xh", [P, 2, D])
            xT = sb("xT", [P, 2, KC, P])
            psT = [pb(f"psT{i}") for i in range(2)]
            psP = [pb(f"psP{i}") for i in range(2)]
            psN = pb("psN")

            x_in, w_in, edges_in, samples_in, cut_in = (sem(n) for n in (
                "x_in", "w_in", "edges_in", "samples_in", "cut_in"))
            zeroed, filled, constants, numbered, made = (sem(n) for n in (
                "zeroed", "filled", "constants", "numbered", "made"))
            chunk_in = [sem(f"chunk_in{g}") for g in range(NG)]
            chunk_wanted, chunk_ready, started, shifted = (sem(n) for n in (
                "chunk_wanted", "chunk_ready", "started", "shifted"))
            dve_step, stats_done, aggregated, rooted, eps_set = (sem(n) for n in (
                "dve_step", "stats_done", "aggregated", "rooted", "eps_set"))
            rows_ready, masks_made, masks_out = sem("rows_ready"), sem("masks_made"), sem("masks_out")
            xhat_ready, turned, xT_ready, product, projected = (sem(n) for n in (
                "xhat_ready", "turned", "xT_ready", "product", "projected"))
            stored, scattered, cut_got, cut_done = (sem(n) for n in ("stored", "scattered", "cut_got", "cut_done"))
            block = phase.enter_context(nc.Block())

            @block.sync
            def _(sp):
                sp.dma_start(samples_i[:, :], d["samples"].partition_broadcast(P)).then_inc(samples_in, 16)
                sp.dma_start(x_sb[:, :, :], d["x"].rearrange("(i p) c -> p i c", p=P)).then_inc(x_in, 16)
                sp.dma_start(w1t[:, :, :], d["proj1_w"].rearrange("(k p) c -> p k c", p=P)).then_inc(w_in, 16)
                sp.dma_start(b1[:, :], d["proj1_b"].partition_broadcast(P)).then_inc(w_in, 16)
                sp.dma_start(dst_b[:, :, :], d["dst"].rearrange("(s b c) -> b s c", s=STREAMS, c=STEP)).then_inc(edges_in, 16)
                sp.dma_start(prev_b[:, :, :], d["prev"].rearrange("(s b c) -> b s c", s=STREAMS, c=STEP)).then_inc(edges_in, 16)
                sp.dma_start(cut_ix[:, :], d["cut"]).then_inc(cut_in, 16)
                sp.wait_ge(masks_made, 1)
                for s in range(STREAMS):
                    sp.dma_start(mask_t[s], mask_b[:, s, :, :].rearrange("b m c -> b (m c)")).then_inc(masks_out, 16)
                store_tables(sp, projected, stored)
                sp.wait_ge(masks_out, 16 * STREAMS)

            @block.gpsimd
            def _(pool):
                pool.iota(node_i[:, :], pattern=[[P, NT]], base=0, channel_multiplier=1).then_inc(numbered, 1)
                pool.memset(zeros[:, :], 0.0).then_inc(zeroed, 1)
                for m, v in ((identity, 0.0), (shift, 0.0), (wrap, 0.0), (head_sum, CH ** -0.5), (pick, 0.0)):
                    pool.memset(m[:, :], v).then_inc(made, 1)
                pool.wait_ge(made, 5)
                pool.affine_select(out=identity[:, :], in_=identity[:, :], compare_op=ALU.not_equal, fill=1.0,
                                   base=0, pattern=[[-1, P]], channel_multiplier=1).then_inc(constants, 1)
                pool.affine_select(out=shift[:, :], in_=shift[:, :], compare_op=ALU.not_equal, fill=1.0,
                                   base=-1, pattern=[[-1, P]], channel_multiplier=1).then_inc(constants, 1)
                pool.memset(wrap[0:1, P - 1:P], 1.0).then_inc(constants, 1)
                pool.affine_select(out=pick[:, :], in_=pick[:, :], compare_op=ALU.not_equal, fill=1.0,
                                   base=0, pattern=[[-CH, STREAMS * HEADS]], channel_multiplier=1).then_inc(constants, 1)
                blocks = head_sum[:, :].rearrange("p (j c) -> p j c", c=CH)
                pool.affine_select(out=blocks, in_=blocks, compare_op=ALU.is_ge, fill=0.0, base=0,
                                   pattern=[[-CH, P // CH], [0, CH]], channel_multiplier=1).then_inc(made, 1)
                pool.wait_ge(made, 6)
                pool.affine_select(out=blocks, in_=blocks, compare_op=ALU.is_ge, fill=0.0, base=CH - 1,
                                   pattern=[[CH, P // CH], [0, CH]], channel_multiplier=-1).then_inc(constants, 1)
                for g in range(NG):
                    pool.wait_ge(chunk_wanted, g + 1)
                    for i in range(GROUP * g, GROUP * (g + 1)):
                        pool.indirect_dma_start(chunk[:, i, :], None, d["edge_rows"],
                                                bass.IndirectOffsetOnAxis(chunk_ix[:, i:i + 1], 0),
                                                bounds_check=SROWS - 1, oob_is_err=False).then_inc(chunk_in[g], 16)
                pool.wait_ge(rows_ready, 1)
                pool.wait_ge(filled, 16 * 4)
                scatter_q(pool, scattered, projected)
                pool.wait_ge(cut_in, 16)
                scatter_cut(pool, scattered, stored, cut_got, cut_done)

            @block.scalar
            def _(act):
                act.wait_ge(zeroed, 1)
                fill = qz_t.rearrange("(p r) c -> p (r c)", p=P).rearrange("p (m k n) -> m p k n", m=4, k=8)
                for m in range(4):
                    act.dma_start(fill[m], zeros[:, :].unsqueeze(1).to_broadcast([P, 8, EP * HC // P // 32])).then_inc(filled, 16)
                act.wait_ge(eps_set, 1)
                root_variance(act, aggregated, rooted)
                def group(g):
                    for u in range(GROUP):
                        t = GROUP * g + u
                        act.wait_ge(turned, t + 1)
                        act.wait_ge(product, t if u == 0 else t - 1)
                        act.activation(xT[:, u % 2, :, :].rearrange("p k n -> p (k n)"), psT[u % 2][:, 0:D],
                                       ACT.Copy).then_inc(xT_ready, 1)
                each_group(act, group)
                act.wait_ge(filled, 16 * 4)

            @block.tensor
            def _(pe):
                pe.wait_ge(constants, 5)
                pe.wait_ge(started, 1)
                pe.matmul(psN[:, 0:NT], shift[:, :], start[:, 0:NT], start=True, stop=False)
                pe.matmul(psN[:, 0:NT], wrap[:, :], start[:, 1:NT + 1], start=False, stop=True).then_inc(shifted, 1)
                pe.wait_ge(w_in, 32)
                def group(g):
                    for k in range(GROUP + 1):
                        if k < GROUP:
                            t = GROUP * g + k
                            pe.wait_ge(xhat_ready, t + 1)
                            pe.wait_ge(xT_ready, t if k == 0 else t - 1)
                            for c in range(KC):
                                ins = pe.transpose(psT[k % 2][:, P * c:P * (c + 1)], xh[:, k % 2, P * c:P * (c + 1)], identity[:, :])
                            ins.then_inc(turned, 1)
                        if k >= 1:
                            u, t = k - 1, GROUP * g + k - 1
                            pe.wait_ge(xT_ready, t + 1)
                            pe.wait_ge(projected, t if u == 0 else t - 1)
                            for c in range(KC):
                                ins = pe.matmul(psP[u % 2][:, 0:PROJ], xT[:, u % 2, c, :], w1t[:, c, :],
                                                start=(c == 0), stop=(c == KC - 1))
                            ins.then_inc(product, 1)

                each_group(pe, group)
            @block.vector
            def _(dve):
                dve.memset(eps[:, :], LN_EPS).then_inc(eps_set, 1)
                step = Steps(dve, dve_step)
                dve.wait_ge(numbered, 1)
                step(dve.tensor_copy(node[:, :], node_i[:, :]))
                dve.wait_ge(samples_in, 16)
                step(dve.tensor_copy(samples[:, :], samples_i[:, :]))
                for g in range(NG):
                    of = slice(GROUP * g, GROUP * (g + 1))
                    step(dve.tensor_tensor(below[:, :, :], samples[:, :].unsqueeze(1).to_broadcast([P, GROUP, SROWS]),
                                           node[:, of].unsqueeze(2).to_broadcast([P, GROUP, SROWS]), ALU.is_lt))
                    step(dve.tensor_reduce(found[:, of], below[:, :, :], AX.X, ALU.add))
                    step(dve.tensor_scalar(chunk_no[:, of], found[:, of], -1.0, 0.0, ALU.add, ALU.max))
                    dve.tensor_copy(chunk_ix[:, of], chunk_no[:, of]).then_inc(chunk_wanted, 1)
                dve.wait_ge(edges_in, 32)
                step(dve.tensor_tensor(mask_b[:, :, 0, :], dst_b[:, :, :], prev_b[:, :, :], ALU.is_equal))
                step(dve.memset(mask_b[0:1, 1, 0, 0:1], 0.0))
                step(dve.tensor_scalar(mask_b[:, :, 1, :], mask_b[:, :, 0, :], -NEG, NEG, ALU.mult, ALU.add))
                dve.sem_inc(masks_made, 1)
                dve.wait_ge(x_in, 16)
                layer_norm_stats(dve, stats_done, aggregated, rooted)
                for g in range(NG):
                    of = slice(GROUP * g, GROUP * (g + 1))
                    dve.wait_ge(chunk_in[g], 16 * GROUP)
                    step(dve.tensor_tensor(below[:, :, 0:SCOLS], chunk[:, of, :],
                                           node[:, of].unsqueeze(2).to_broadcast([P, GROUP, SCOLS]), ALU.is_lt))
                    step(dve.tensor_reduce(found[:, of], below[:, :, 0:SCOLS], AX.X, ALU.add))
                step(dve.memset(start[:, NT:NT + 1], float(E)))
                step(dve.scalar_tensor_tensor(start[:, 0:NT], chunk_no[:, :], float(SCOLS), found[:, :], ALU.mult, ALU.add))
                dve.sem_inc(started, 1)
                dve.wait_ge(shifted, 1)
                step(dve.tensor_copy(nxt[:, :], psN[:, 0:NT]))
                first = start[:, 0:NT]
                step(dve.tensor_tensor(present[:, :], nxt[:, :], first, ALU.is_gt))
                step(dve.tensor_scalar(t0[:, :], first, float(HALF), 1.0 - 2 * HALF, ALU.is_ge, ALU.mult))
                step(dve.scalar_tensor_tensor(t0[:, :], first, 2.0, t0[:, :], ALU.mult, ALU.add))
                step(dve.tensor_scalar(t1[:, :], present[:, :], -SKIP, SKIP, ALU.mult, ALU.add))
                step(dve.tensor_tensor(start_row[:, :], t0[:, :], t1[:, :], ALU.add))
                dve.sem_inc(rows_ready, 1)
                step(dve.tensor_scalar(t0[:, :], first, float(HALF), None, ALU.is_lt))
                step(dve.scalar_tensor_tensor(t0[:, :], nxt[:, :], float(HALF), t0[:, :], ALU.is_gt, ALU.mult))
                step(dve.tensor_scalar(span_bias[:, :], t0[:, :], -NEG, NEG, ALU.mult, ALU.add))
                step(dve.tensor_scalar(nxt[:, :], nxt[:, :], -1.0, 0.0, ALU.add, ALU.max))
                step(dve.tensor_scalar(t0[:, :], nxt[:, :], float(HALF), 1.0 - 2 * HALF, ALU.is_ge, ALU.mult))
                step(dve.scalar_tensor_tensor(end_row[:, :], nxt[:, :], 2.0, t0[:, :], ALU.mult, ALU.add))
                dve.wait_ge(w_in, 32)
                def group(g):
                    for k in range(GROUP + 2):
                        if k < GROUP:
                            t = GROUP * g + k
                            dve.wait_ge(turned, t if k == 0 else t - 1)
                            dve.tensor_scalar(xh[:, k % 2, :], x_sb[:, t, :], mv[:, t, 0:1], rstd[:, ts(t, 1)],
                                              ALU.subtract, ALU.mult).then_inc(xhat_ready, 1)
                        if k >= 2:
                            t = GROUP * g + k - 2
                            dve.wait_ge(product, t + 1)
                            dve.tensor_tensor(proj[:, t, :], psP[(k - 2) % 2][:, 0:PROJ], b1[:, :],
                                              ALU.add).then_inc(projected, 1)

                each_group(dve, group)
        def edge_sem(name):
            return whole.enter_context(nc.semaphore(name))

        ix_in = [edge_sem(f"ix_in{u}") for u in range(UNROLL)]
        kv_in = [edge_sem(f"kv_in{u}") for u in range(UNROLL)]
        q_in = [edge_sem(f"q_in{u}") for u in range(UNROLL)]
        mask_in = [edge_sem(f"mask_in{u}") for u in range(UNROLL)]
        rows_out = [edge_sem(f"rows_out{i}") for i in range(2)]
        cleared, kq_turned, v_turned, out_turned = (edge_sem(n) for n in ("cleared", "kq_turned", "v_turned", "out_turned"))
        q_held, kq_ready, logits_ready, carried, top_ready = (edge_sem(n) for n in (
            "q_held", "kq_ready", "logits_ready", "carried", "top_ready"))
        grown, gaps_ready, ex_ready, weighted, v_summed, d_summed, copied, gathering = (edge_sem(n) for n in (
            "grown", "gaps_ready", "ex_ready", "weighted", "v_summed", "d_summed", "copied", "gathering"))

        def edge_phase(layer):
            with ExitStack() as phase:
                def sb(name, shape, dt=F32):
                    return phase.enter_context(nc.sbuf_tensor(f"{name}_{layer}", shape, dt))

                def pb(name):
                    return phase.enter_context(nc.psum_tensor(f"{name}_{layer}", [P, STEP], F32))

                U = UNROLL
                ix = sb("ix", [P, U, TPB * STREAMS], I32)
                kv = sb("kv", [P, U, TPB, STREAMS * 2 * HC])
                qz = sb("qz", [P, U, TPB, STREAMS * HC])
                mask = sb("mask", [P, U, 2, STEP], BF16)
                held_q = sb("held_q", [P, 2, STEP])
                kq = sb("kq", [P, 2, STEP])
                top = sb("top", [P, U, 1 + STEP])
                gap = sb("gap", [P, 2, 2, STEP])
                ex = sb("ex", [P, 2, 2, STEP])
                wv = sb("wv", [P, 2, STEP])
                run_v = sb("run_v", [P, U, STEP])
                run_d = sb("run_d", [P, U, STEP])
                rows = sb("rows", [P, 2, TPB, STREAMS, ROW])
                kT = [pb(f"kT{i}") for i in range(2)]
                qT = [pb(f"qT{i}") for i in range(2)]
                vT, logit, outT = pb("vT"), pb("logit"), pb("outT")
                restT = pb("restT")[:, 0:2 * TPB * STREAMS * HEADS].rearrange("p (m j h) -> p m j h", m=2, j=TPB)

                block = phase.enter_context(nc.Block())

                past = STEPS * layer

                def each_step(eng, body):
                    if layer == 0:
                        body(0, False)
                    with eng.Fori(past + (layer == 0), past + STEPS) as i:
                        body(i, True)

                @block.sync
                def _(sp):
                    def body(i, again):
                        for u in range(U):
                            b = U * i + u
                            if again:
                                sp.wait_ge(kq_turned, b - U + 1)
                                sp.wait_ge(gaps_ready, b - U + 1)
                                sp.wait_ge(v_turned, b - U + 1)
                            sp.dma_start(ix[:, u, :], d["src"][b - BLOCKS * layer]).then_inc(ix_in[u], 16)
                            sp.dma_start(qz[:, u, :, :], qz_blocks[b - BLOCKS * layer]).then_inc(q_in[u], 16)
                            for s in range(STREAMS):
                                sp.dma_start(mask[HC * s:HC * (s + 1), u, :, :].rearrange("p m c -> p (m c)"),
                                             mask_t[s, b - BLOCKS * layer].partition_broadcast(HC)).then_inc(mask_in[u], 16)
                    each_step(sp, body)

                @block.gpsimd
                def _(pool):
                    def body(i, again):
                        for u in range(U):
                            pool.wait_ge(ix_in[u], 16 * i + 16)
                            pool.sem_inc(gathering, 1)
                            for j in range(TPB):
                                for s in range(STREAMS):
                                    n = STREAMS * j + s
                                    pool.indirect_dma_start(kv[:, u, j, 2 * HC * s:2 * HC * (s + 1)], None, kv_t,
                                                            bass.IndirectOffsetOnAxis(ix[:, u, n:n + 1], 0),
                                                            bounds_check=NP - 1, oob_is_err=False).then_inc(kv_in[u], 16)
                    each_step(pool, body)

                @block.tensor
                def _(pe):
                    def body(i, again):
                        for stage in range(U + 3):
                            if stage < U:
                                u, b = stage, U * i + stage
                                pe.wait_ge(kv_in[u], 16 * TPB * STREAMS * (i + 1))
                                pe.wait_ge(q_in[u], 16 * i + 16)
                                if again or u >= 2:
                                    pe.wait_ge(kq_ready, b - 1)
                                for j in range(TPB):
                                    pe.transpose(kT[u % 2][:, P * j:P * (j + 1)], kv[:, u, j, 0::2], identity[:, :])
                                    ins = pe.transpose(qT[u % 2][:, P * j:P * (j + 1)], qz[:, u, j, :], identity[:, :])
                                ins.then_inc(kq_turned, 1)
                            if 1 <= stage <= U:
                                u, b = stage - 1, U * i + stage - 1
                                pe.wait_ge(kq_ready, b + 1)
                                pe.wait_ge(gaps_ready, b)
                                pe.matmul(logit[:, :], head_sum[:, :], kq[:, u % 2, :], start=True, stop=True)\
                                    .then_inc(logits_ready, 1)
                            if 2 <= stage <= U + 1:
                                u, b = stage - 2, U * i + stage - 2
                                pe.wait_ge(weighted, b)
                                for j in range(TPB):
                                    ins = pe.transpose(vT[:, P * j:P * (j + 1)], kv[:, u, j, 1::2], identity[:, :])
                                ins.then_inc(v_turned, 1)
                            if stage >= 3:
                                u, b = stage - 3, U * i + stage - 3
                                pe.wait_ge(v_summed, b + 1)
                                pe.wait_ge(d_summed, b + 1)
                                pe.wait_ge(copied, 3 * b)
                                for j in range(TPB):
                                    of = slice(P * j, P * (j + 1))
                                    pe.transpose(outT[:, of], run_v[:, u, of], identity[:, :])
                                    pe.matmul(restT[:, 0, j, :], run_d[:, u, of], pick[:, :], start=True, stop=True)
                                    ins = pe.matmul(restT[:, 1, j, :], top[:, u, 1 + P * j:1 + P * (j + 1)], pick[:, :],
                                                    start=True, stop=True)
                                ins.then_inc(out_turned, 1)
                    each_step(pe, body)

                @block.vector
                def _(dve):
                    dve.memset(held_q[:, 1, STEP - 1:STEP], 0.0).then_inc(cleared, 1)
                    dve.memset(top[:, U - 1, STEP:STEP + 1], 0.0).then_inc(cleared, 1)
                    dve.memset(run_v[:, U - 1, STEP - 1:STEP], 0.0).then_inc(cleared, 1)
                    dve.memset(run_d[:, U - 1, STEP - 1:STEP], 0.0).then_inc(cleared, 1)
                    dve.wait_ge(cleared, 4 * layer + 4)

                    def body(i, again):
                        for stage in range(U + 2):
                            if stage < U:
                                u, b, h = stage, U * i + stage, stage % 2
                                dve.wait_ge(kq_turned, b + 1)
                                dve.wait_ge(mask_in[u], 32 * i + 32)
                                dve.wait_ge(q_held, b)
                                dve.tensor_tensor_scan(held_q[:, h, :], mask[:, u, 0, :], qT[h][:, :],
                                                       held_q[:, 1 - h, STEP - 1:STEP], ALU.mult, ALU.add).then_inc(q_held, 1)
                                dve.wait_ge(q_held, b + 1)
                                if again or u >= 2:
                                    dve.wait_ge(logits_ready, b - 1)
                                dve.tensor_tensor(kq[:, h, :], kT[h][:, :], held_q[:, h, :], ALU.mult).then_inc(kq_ready, 1)
                            if 1 <= stage <= U:
                                u, b, h = stage - 1, U * i + stage - 1, (stage - 1) % 2
                                before, now = top[:, u, 0:STEP], top[:, u, 1:1 + STEP]
                                last = top[:, (u - 1) % U, STEP:STEP + 1]
                                dve.wait_ge(top_ready, b)
                                if again:
                                    dve.wait_ge(out_turned, b - U + 1)
                                dve.tensor_copy(top[:, u, 0:1], last).then_inc(carried, 1)
                                dve.wait_ge(logits_ready, b + 1)
                                dve.tensor_tensor_scan(now, mask[:, u, 1, :], logit[:, :], last,
                                                       ALU.add, ALU.max).then_inc(top_ready, 1)
                                dve.wait_ge(top_ready, b + 1)
                                dve.wait_ge(carried, b + 1)
                                if again or u >= 2:
                                    dve.wait_ge(ex_ready, b - 1)
                                dve.tensor_tensor(gap[:, h, 1, :], before, now, ALU.subtract).then_inc(grown, 1)
                                dve.tensor_tensor(gap[:, h, 0, :], logit[:, :], now, ALU.subtract).then_inc(grown, 1)
                                dve.wait_ge(grown, 2 * b + 2)
                                dve.tensor_tensor(gap[:, h, 1, :], gap[:, h, 1, :], mask[:, u, 1, :], ALU.add).then_inc(gaps_ready, 1)
                            if stage >= 2:
                                u, b, h = stage - 2, U * i + stage - 2, stage % 2
                                dve.wait_ge(ex_ready, b + 1)
                                dve.wait_ge(v_turned, b + 1)
                                dve.tensor_tensor(wv[:, h, :], vT[:, :], ex[:, h, 0, :], ALU.mult).then_inc(weighted, 1)
                                if again:
                                    dve.wait_ge(out_turned, b - U + 1)
                                dve.wait_ge(d_summed, b)
                                dve.tensor_tensor_scan(run_d[:, u, :], ex[:, h, 1, :], ex[:, h, 0, :],
                                                       run_d[:, (u - 1) % U, STEP - 1:STEP], ALU.mult, ALU.add).then_inc(d_summed, 1)
                                dve.wait_ge(weighted, b + 1)
                                dve.wait_ge(v_summed, b)
                                dve.tensor_tensor_scan(run_v[:, u, :], ex[:, h, 1, :], wv[:, h, :],
                                                       run_v[:, (u - 1) % U, STEP - 1:STEP], ALU.mult, ALU.add).then_inc(v_summed, 1)
                    each_step(dve, body)

                @block.scalar
                def _(act):
                    def body(i, again):
                        for stage in range(1, U + 3):
                            if stage <= U:
                                u, b, h = stage - 1, U * i + stage - 1, (stage - 1) % 2
                                act.wait_ge(gaps_ready, b + 1)
                                if again or u >= 2:
                                    act.wait_ge(v_summed, b - 1)
                                act.activation(ex[:, h, :, :].rearrange("p m c -> p (m c)"),
                                               gap[:, h, :, :].rearrange("p m c -> p (m c)"), ACT.Exp).then_inc(ex_ready, 1)
                            if stage >= 3:
                                u, b, h = stage - 3, U * i + stage - 3, (stage - 3) % 2
                                act.wait_ge(out_turned, b + 1)
                                act.wait_ge(rows_out[h], 16 * (U // 2 * i + u // 2))
                                flat = rows[:, h, :, :, :].rearrange("p j s c -> p (j s) c")
                                act.activation(flat[:, :, 0:HC], outT[:, :].rearrange("p (r c) -> p r c", c=HC),
                                               ACT.Copy).then_inc(copied, 1)
                                for m, at in enumerate((DEN, MAX)):
                                    act.activation(flat[:, :, at:at + HEADS],
                                                   restT[:, m, :, :].rearrange("p j (s h) -> p (j s) h", h=HEADS),
                                                   ACT.Copy).then_inc(copied, 1)
                                act.wait_ge(copied, 3 * b + 3)
                                act.dma_start(sum_blocks[b - BLOCKS * layer], rows[:, h, :, :, :].rearrange("p j s c -> p j (s c)"))\
                                    .then_inc(rows_out[h], 16)
                    each_step(act, body)
                    for h in range(2):
                        act.wait_ge(rows_out[h], 16 * BLOCKS // 2 * (layer + 1))

        def node_phase(layer):
            last = layer == 1
            with ExitStack() as phase:
                def sb(name, shape, dt=F32):
                    return phase.enter_context(nc.sbuf_tensor(f"{name}_n{layer}", shape, dt))

                def pb(name):
                    return phase.enter_context(nc.psum_tensor(f"{name}_n{layer}", [P, 512], F32))

                def sem(name):
                    return whole.enter_context(nc.semaphore(f"{name}_n{layer}"))

                G = GROUP
                fin = sb("fin", [P, NT, ROW])
                cut = sb("cut", [P, ROW])
                h = sb("h", [P, NT, HC])
                mb = sb("mb", [P, G, HEADS])
                mm = sb("mm", [P, G, HEADS])
                wt = sb("wt", [P, G, 2, HEADS])
                wx = sb("wx", [P, G, 2, HEADS])
                den = sb("den", [P, G, HEADS])
                part = sb("part", [P, G, HEADS])
                ov = sb("ov", [P, G, HC])
                hs = sb("hs", [P, 2, HC])
                hT = sb("hT", [HC, 2, P])
                w_sb = sb("w_sb", [HC, D])
                b_sb = sb("b_sb", [P, D])
                psT = [pb(f"psT{i}") for i in range(2)]
                psP = [pb(f"psP{i}") for i in range(2)]
                fin_in = [sem(f"fin_in{g}") for g in range(NG)]
                w_in, cut_in, fins, weights_wanted, weights_ready, comb = (sem(n) for n in (
                    "w_in", "cut_in", "fins", "weights_wanted", "weights_ready", "comb"))
                combined, hs_ready, turned, hT_ready, product, projected = (sem(n) for n in (
                    "combined", "hs_ready", "turned", "hT_ready", "product", "projected"))
                stored, scattered, cut_got, cut_done = (sem(n) for n in ("stored", "scattered", "cut_got", "cut_done"))
                if last:
                    sg = sb("sg", [P, 2, D])
                    yh = sb("yh", [P, 2, D])
                    yS = sb("yS", [P, 2, KC, P])
                    gs = sb("gs", [P, 2, EXPERTS])
                    wr = sb("wr", [P, KC, EXPERTS])
                    br = sb("br", [P, EXPERTS])
                    bo8 = sb("bo8", [EXPERTS, D])
                    red = sb("red", [P, NT])
                    gT = sb("gT", [EXPERTS, 2, P])
                    psY = [pb(f"psY{i}") for i in range(2)]
                    psR = [pb(f"psR{i}") for i in range(2)]
                    (squashed, added, stats_done, aggregated, rooted, y_ready, y_turned, yT_ready, routed, scored,
                     smax, gap_ready, exp_ready, gs_ready, g_turned, gT_ready, biased, bias_added) = (sem(n) for n in (
                        "squashed", "added", "stats_done", "aggregated", "rooted", "y_ready", "y_turned", "yT_ready",
                        "routed", "scored", "smax", "gap_ready", "exp_ready", "gs_ready", "g_turned", "gT_ready", "biased", "bias_added"))
                block = phase.enter_context(nc.Block())

                @block.sync
                def _(sp):
                    sp.dma_start(cut[:, :], sum_t[2 * (HALF - 1)].partition_broadcast(P)).then_inc(cut_in, 16)
                    w_name, b_name = ("wo", "bo") if last else ("proj2_w", "proj2_b")
                    sp.dma_start(w_sb[:, :], d[w_name]).then_inc(w_in, 16)
                    sp.dma_start(b_sb[:, :], d[b_name].partition_broadcast(P)).then_inc(w_in, 16)
                    if last:
                        sp.dma_start(wr[:, :, :], d["wr"].rearrange("(k p) e -> p k e", p=P)).then_inc(w_in, 16)
                        sp.dma_start(br[:, :], d["br"].partition_broadcast(P)).then_inc(w_in, 16)
                        sp.dma_start(bo8[:, :], d["bo8"]).then_inc(w_in, 16)
                        sp.wait_ge(w_in, 16 * 5)
                    else:
                        store_tables(sp, projected, stored)

                @block.gpsimd
                def _(pool):
                    for g in range(NG):
                        for i in range(G * g, G * (g + 1)):
                            pool.indirect_dma_start(fin[:, i, :], None, sum_t,
                                                    bass.IndirectOffsetOnAxis(end_row[:, i:i + 1], 0),
                                                    bounds_check=EP - 1, oob_is_err=False).then_inc(fin_in[g], 16)
                    for g in range(NG):
                        pool.wait_ge(fin_in[g], 16 * G)
                        pool.sem_inc(fins, 1)
                    if not last:
                        scatter_q(pool, scattered, projected)
                        scatter_cut(pool, scattered, stored, cut_got, cut_done)

                @block.tensor
                def _(pe):
                    pe.wait_ge(w_in, 16 * (5 if last else 2))
                    def group(g):
                        for k in range(G + 1):
                            if k < G:
                                t = G * g + k
                                pe.wait_ge(hs_ready, t + 1)
                                pe.wait_ge(hT_ready, t if k == 0 else t - 1)
                                pe.matmul(psT[k % 2][0:HC, 0:P], hs[:, k % 2, :], identity[:, :],
                                          start=True, stop=True).then_inc(turned, 1)
                            if k >= 1:
                                u, t = k - 1, G * g + k - 1
                                pe.wait_ge(hT_ready, t + 1)
                                pe.wait_ge(projected, t if u == 0 else t - 1)
                                pe.matmul(psP[u % 2][:, 0:D], hT[:, u % 2, :], w_sb[:, :],
                                          start=True, stop=True).then_inc(product, 1)
                    each_group(pe, group)
                    if not last:
                        return
                    def group(g):
                        for k in range(G + 1):
                            if k < G:
                                t = G * g + k
                                pe.wait_ge(y_ready, t + 1)
                                pe.wait_ge(yT_ready, 2 * t if k == 0 else 2 * t - 2)
                                for c in range(KC):
                                    ins = pe.transpose(psY[k % 2][:, P * c:P * (c + 1)], yh[:, k % 2, P * c:P * (c + 1)], identity[:, :])
                                ins.then_inc(y_turned, 1)
                            if k >= 1:
                                u, t = k - 1, G * g + k - 1
                                pe.wait_ge(yT_ready, 2 * t + 2)
                                pe.wait_ge(scored, t if u == 0 else t - 1)
                                for c in range(KC):
                                    ins = pe.matmul(psR[u % 2][:, 0:EXPERTS], yS[:, u % 2, c, :], wr[:, c, :],
                                                    start=(c == 0), stop=(c == KC - 1))
                                ins.then_inc(routed, 1)
                    each_group(pe, group)
                    def group(g):
                        for k in range(G + 1):
                            if k < G:
                                t = G * g + k
                                pe.wait_ge(gs_ready, t + 1)
                                pe.wait_ge(gT_ready, t if k == 0 else t - 1)
                                pe.transpose(psT[k % 2][0:EXPERTS, 0:P], gs[:, k % 2, :], identity[:, :]).then_inc(g_turned, 1)
                            if k >= 1:
                                u, t = k - 1, G * g + k - 1
                                pe.wait_ge(gT_ready, t + 1)
                                pe.wait_ge(bias_added, t if u == 0 else t - 1)
                                pe.matmul(psP[u % 2][:, 0:D], gT[:, u % 2, :], bo8[:, :],
                                          start=True, stop=True).then_inc(biased, 1)

                    each_group(pe, group)
                @block.scalar
                def _(act):
                    with act.Fori(0, NG) as g:
                        act.wait_ge(weights_wanted, g + 1)
                        act.activation(wx[:, :, :, :].rearrange("p i m h -> p (i m h)"),
                                       wt[:, :, :, :].rearrange("p i m h -> p (i m h)"), ACT.Exp).then_inc(weights_ready, 1)
                    def group(g):
                        act.wait_ge(combined, g + 1)
                        for k in range(G + 2):
                            if k < G:
                                t = G * g + k
                                act.wait_ge(turned, t if k == 0 else t - 1)
                                act.activation(hs[:, k % 2, :], h[:, t, :], ACT.Copy).then_inc(hs_ready, 1)
                                act.wait_ge(turned, t + 1)
                                act.wait_ge(product, t if k == 0 else t - 1)
                                act.activation(hT[:, k % 2, :], psT[k % 2][0:HC, 0:P], ACT.Copy).then_inc(hT_ready, 1)
                            if last and k >= 2:
                                t = G * g + k - 2
                                act.wait_ge(projected, t + 1)
                                act.activation(sg[:, k % 2, :], sg[:, k % 2, :], ACT.Sigmoid).then_inc(squashed, 1)
                    each_group(act, group)
                    if not last:
                        return
                    root_variance(act, aggregated, rooted)
                    def group(g):
                        for k in range(G):
                            t = G * g + k
                            act.wait_ge(y_turned, t + 1)
                            act.wait_ge(routed, t if k == 0 else t - 1)
                            act.activation(yT[:, :, ts(t, P)], psY[k % 2][:, 0:D].rearrange("p (c n) -> p c n", c=KC),
                                           ACT.Copy).then_inc(yT_ready, 1)
                            act.activation(yS[:, k % 2, :, :].rearrange("p c n -> p (c n)"), psY[k % 2][:, 0:D],
                                           ACT.Copy).then_inc(yT_ready, 1)
                    each_group(act, group)
                    act.wait_ge(gap_ready, 1)
                    act.activation(gate[:, :, :].rearrange("p i e -> p (i e)"),
                                   gate[:, :, :].rearrange("p i e -> p (i e)"), ACT.Exp).then_inc(exp_ready, 1)
                    act.wait_ge(gap_ready, 2)
                    def group(g):
                        for k in range(G):
                            t = G * g + k
                            act.wait_ge(g_turned, t if k == 0 else t - 1)
                            act.activation(gs[:, k % 2, :], gate[:, t, :], ACT.Copy).then_inc(gs_ready, 1)
                            act.wait_ge(g_turned, t + 1)
                            act.wait_ge(biased, t if k == 0 else t - 1)
                            act.activation(gT[:, k % 2, :], psT[k % 2][0:EXPERTS, 0:P], ACT.Copy).then_inc(gT_ready, 1)

                    each_group(act, group)
                @block.vector
                def _(dve):
                    dve.wait_ge(cut_in, 16)
                    dve.wait_ge(w_in, 16 * (5 if last else 2))
                    COMB = 14
                    all4 = [P, G, HEADS]
                    all64 = [P, G, HEADS, CH]

                    def by_head(a):
                        return a.rearrange("p i (h c) -> p i h c", c=CH)

                    with dve.Fori(0, NG) as g:
                        step = Steps(dve, comb, COMB * g)
                        of = ts(g, G)
                        dve.wait_ge(fins, g + 1)
                        step(dve.tensor_tensor(mb[:, :, :], span_bias[:, of].unsqueeze(2).to_broadcast(all4),
                                               cut[:, MAX:MAX + HEADS].unsqueeze(1).to_broadcast(all4), ALU.add))
                        step(dve.tensor_tensor(mm[:, :, :], mb[:, :, :], fin[:, of, MAX:MAX + HEADS], ALU.max))
                        step(dve.tensor_tensor(wt[:, :, 0, :], fin[:, of, MAX:MAX + HEADS], mm[:, :, :], ALU.subtract))
                        step(dve.tensor_tensor(wt[:, :, 1, :], mb[:, :, :], mm[:, :, :], ALU.subtract))
                        dve.sem_inc(weights_wanted, 1)
                        dve.wait_ge(weights_ready, g + 1)
                        step(dve.tensor_tensor(den[:, :, :], fin[:, of, DEN:DEN + HEADS], wx[:, :, 0, :], ALU.mult))
                        step(dve.tensor_tensor(part[:, :, :], cut[:, DEN:DEN + HEADS].unsqueeze(1).to_broadcast(all4),
                                               wx[:, :, 1, :], ALU.mult))
                        step(dve.scalar_tensor_tensor(den[:, :, :].rearrange("p i h -> p (i h)"), den[:, :, :].rearrange("p i h -> p (i h)"),
                                                      DEN_EPS, part[:, :, :].rearrange("p i h -> p (i h)"), ALU.add, ALU.add))
                        step(dve.reciprocal(den[:, :, :], den[:, :, :]))
                        step(dve.tensor_tensor(den[:, :, :], den[:, :, :], present[:, of].unsqueeze(2).to_broadcast(all4), ALU.mult))
                        step(dve.tensor_tensor(wx[:, :, :, :], wx[:, :, :, :], den[:, :, :].unsqueeze(2).to_broadcast([P, G, 2, HEADS]), ALU.mult))
                        step(dve.tensor_tensor(by_head(h[:, of, :]), by_head(fin[:, of, 0:HC]),
                                               wx[:, :, 0, :].unsqueeze(3).to_broadcast(all64), ALU.mult))
                        step(dve.tensor_tensor(by_head(ov[:, :, :]), wx[:, :, 1, :].unsqueeze(3).to_broadcast(all64),
                                               cut[:, 0:HC].rearrange("p (h c) -> p h c", c=CH).unsqueeze(1).to_broadcast(all64), ALU.mult))
                        step(dve.tensor_tensor(h[:, of, :], h[:, of, :], ov[:, :, :], ALU.add))
                        step(dve.tensor_tensor(ov[:, :, :], h[:, of, :], proj[:, of, S0:S0 + HC], ALU.add))
                        dve.tensor_scalar(h[:, of, :], ov[:, :, :], 0.0, None, ALU.max).then_inc(combined, 1)
                    if not last:
                        with dve.Fori(0, NG) as g:
                            for k in range(G):
                                t = G * g + k
                                dve.wait_ge(product, t + 1)
                                dve.tensor_tensor(proj[:, t, :], psP[k % 2][:, 0:PROJ], b_sb[:, :], ALU.add).then_inc(projected, 1)
                        return
                    def group(g):
                        for k in range(G + 2):
                            if k >= 2:
                                t = G * g + k - 2
                                dve.wait_ge(squashed, t + 1)
                                dve.tensor_tensor(x_sb[:, t, :], x_sb[:, t, :], sg[:, k % 2, :], ALU.add).then_inc(added, 1)
                            if k < G:
                                t = G * g + k
                                dve.wait_ge(product, t + 1)
                                dve.wait_ge(added, t if k == 0 else t - 1)
                                dve.tensor_tensor(sg[:, k % 2, :], psP[k % 2][:, 0:D], b_sb[:, :], ALU.add).then_inc(projected, 1)
                    each_group(dve, group)
                    dve.wait_ge(added, NT)
                    layer_norm_stats(dve, stats_done, aggregated, rooted)
                    def group(g):
                        for k in range(G + 2):
                            if k < G:
                                t = G * g + k
                                dve.wait_ge(y_turned, t if k == 0 else t - 1)
                                dve.tensor_scalar(yh[:, k % 2, :], x_sb[:, t, :], mv[:, t, 0:1], rstd[:, ts(t, 1)],
                                                  ALU.subtract, ALU.mult).then_inc(y_ready, 1)
                            if k >= 2:
                                t = G * g + k - 2
                                dve.wait_ge(routed, t + 1)
                                dve.tensor_tensor(gate[:, t, :], psR[(k - 2) % 2][:, 0:EXPERTS], br[:, :], ALU.add).then_inc(scored, 1)
                    each_group(dve, group)
                    every = [P, NT, EXPERTS]
                    step = Steps(dve, smax)
                    dve.wait_ge(scored, NT)
                    step(dve.tensor_reduce(red[:, :], gate[:, :, :], AX.X, ALU.max))
                    dve.tensor_tensor(gate[:, :, :], gate[:, :, :], red[:, :].unsqueeze(2).to_broadcast(every), ALU.subtract).then_inc(gap_ready, 1)
                    dve.wait_ge(exp_ready, 1)
                    step(dve.tensor_reduce(red[:, :], gate[:, :, :], AX.X, ALU.add))
                    step(dve.reciprocal(red[:, :], red[:, :]))
                    dve.tensor_tensor(gate[:, :, :], gate[:, :, :], red[:, :].unsqueeze(2).to_broadcast(every), ALU.mult).then_inc(gap_ready, 1)
                    with dve.Fori(0, NG) as g:
                        for k in range(G):
                            t = G * g + k
                            dve.wait_ge(biased, t + 1)
                            dve.tensor_tensor(x_sb[:, t, :], x_sb[:, t, :], psP[k % 2][:, 0:D], ALU.add).then_inc(bias_added, 1)

        def expert_phase():
            with ExitStack() as phase:
                def sb(name, shape, dt=F32):
                    return phase.enter_context(nc.sbuf_tensor(name, shape, dt))

                def pb(name):
                    return phase.enter_context(nc.psum_tensor(name, [P, 512], F32))

                def sem(name):
                    return whole.enter_context(nc.semaphore(name))

                LH, LO = HID // P, EXPERTS * HID // P
                w = [sb(f"expert_w{n}", [P, EXPERTS, KC, HID]) for n in range(3)]
                bn = sb("bn", [P, 2, 5, LO])
                scale = sb("scale", [P, 2, LO])
                offset = sb("offset", [P, 2, LO])
                hid = [sb(f"hid{n}", [P, 2, LH, GROUP * P]) for n in range(2)]
                bn_eps = sb("bn_eps", [P, 1])
                psH = [pb(f"psH{i}") for i in range(6)]
                psO = [pb(f"psO{i}") for i in range(2)]
                w_in = [sem(f"expert_w_in{n}") for n in range(3)]
                bn_in, eps_ready, rooted, bn_step, folded = (sem(n) for n in ("bn_in", "bn_eps_set", "bn_rooted", "bn_step", "folded"))
                formed, relued, out_formed, added, stored = (sem(n) for n in (
                    "hid_formed", "hid_relued", "out_formed", "out_added", "out_stored"))
                block = phase.enter_context(nc.Block())

                order = [(0, 0)] + [z for e in range(EXPERTS) for z in ((e, 1), (e + 1, 0))][:-1]
                place = {z: 4 * n for n, z in enumerate(order)}
                PER = 4 * len(order)

                @block.sync
                def _(sp):
                    sp.dma_start(bn[:, :, :, :], d["bn"]).then_inc(bn_in, 16)
                    for n in range(3):
                        sp.dma_start(w[n][:, :, :, :], d[f"expert_w{n}"].rearrange("e (k p) c -> p e k c", p=P)).then_inc(w_in[n], 16)
                    with sp.Fori(0, NG) as g:
                        sp.wait_ge(added, EXPERTS * GROUP * (g + 1))
                        sp.dma_start(d["out"].rearrange("(i p) c -> p i c", p=P)[:, ts(g, GROUP), :],
                                     x_sb[:, ts(g, GROUP), :]).then_inc(stored, 16)
                    sp.wait_ge(stored, 16 * NG)

                @block.tensor
                def _(pe):
                    for n in range(3):
                        pe.wait_ge(w_in[n], 16)
                    def group(g):
                        def hidden(e, layer):
                            for m in range(LH):
                                for half in range(2):
                                    n = place[e, layer] + 2 * m + half
                                    bank = psH[n % 6]
                                    if n >= 6:
                                        pe.wait_ge(relued, PER * g + n - 5)
                                    else:
                                        pe.wait_ge(relued, PER * g)
                                    if layer == 1:
                                        pe.wait_ge(relued, PER * g + place[e, 0] + 3 + half)
                                    for c in range(KC):
                                        if layer == 0:
                                            rhs = yT[:, c, bass.ds(GROUP * P * g + HTOK * half, HTOK)]
                                        else:
                                            rhs = hid[0][:, e % 2, c, HTOK * half:HTOK * (half + 1)]
                                        ins = pe.matmul(bank[:, 0:HTOK], w[layer][:, e, c, P * m:P * (m + 1)], rhs,
                                                        start=(c == 0), stop=(c == KC - 1))
                                    ins.then_inc(formed, 1)

                        def outputs(e):
                            pe.wait_ge(relued, PER * g + place[e, 1] + 4)
                            for u in range(GROUP):
                                n = GROUP * e + u
                                if n >= 2:
                                    pe.wait_ge(added, EXPERTS * GROUP * g + n - 1)
                                else:
                                    pe.wait_ge(added, EXPERTS * GROUP * g)
                                for c in range(KC):
                                    ins = pe.matmul(psO[n % 2][:, 0:D], hid[1][:, e % 2, c, P * u:P * (u + 1)], w[2][:, e, c, :],
                                                    start=(c == 0), stop=(c == KC - 1))
                                ins.then_inc(out_formed, 1)

                        hidden(0, 0)
                        for e in range(EXPERTS):
                            if e >= 1:
                                outputs(e - 1)
                            hidden(e, 1)
                            if e + 1 < EXPERTS:
                                hidden(e + 1, 0)
                        outputs(EXPERTS - 1)

                    each_group(pe, group)
                @block.scalar
                def _(act):
                    act.wait_ge(eps_ready, 1)
                    act.wait_ge(bn_in, 16)
                    act.activation(scale[:, :, :], bn[:, :, 4, :], ACT.Sqrt, bias=bn_eps[:, 0:1]).then_inc(rooted, 1)
                    act.wait_ge(folded, 1)
                    def group(g):
                        for e, layer in order:
                            for m in range(LH):
                                for half in range(2):
                                    n = place[e, layer] + 2 * m + half
                                    act.wait_ge(formed, PER * g + n + 1)
                                    if layer == 1 and m == 0 and half == 0:
                                        if e >= 2:
                                            act.wait_ge(out_formed, EXPERTS * GROUP * g + GROUP * (e - 1))
                                        else:
                                            act.wait_ge(out_formed, EXPERTS * GROUP * g)
                                    at = LH * e + m
                                    act.activation(hid[layer][:, e % 2, m, HTOK * half:HTOK * (half + 1)], psH[n % 6][:, 0:HTOK],
                                                   ACT.Relu, bias=offset[:, layer, at:at + 1],
                                                   scale=scale[:, layer, at:at + 1]).then_inc(relued, 1)

                    each_group(act, group)
                @block.vector
                def _(dve):
                    dve.memset(bn_eps[:, :], BN_EPS).then_inc(eps_ready, 1)
                    step = Steps(dve, bn_step)
                    dve.wait_ge(rooted, 1)
                    step(dve.reciprocal(scale[:, :, :], scale[:, :, :]))
                    step(dve.tensor_tensor(scale[:, :, :], scale[:, :, :], bn[:, :, 1, :], ALU.mult))
                    step(dve.tensor_tensor(offset[:, :, :], bn[:, :, 0, :], bn[:, :, 3, :], ALU.subtract))
                    step(dve.tensor_tensor(offset[:, :, :], offset[:, :, :], scale[:, :, :], ALU.mult))
                    step(dve.tensor_tensor(offset[:, :, :], offset[:, :, :], bn[:, :, 2, :], ALU.add))
                    dve.sem_inc(folded, 1)
                    def group(g):
                        for e in range(EXPERTS):
                            for u in range(GROUP):
                                n = GROUP * e + u
                                dve.wait_ge(out_formed, EXPERTS * GROUP * g + n + 1)
                                if e >= 1:
                                    dve.wait_ge(added, EXPERTS * GROUP * g + n - GROUP + 1)
                                t = GROUP * g + u
                                dve.scalar_tensor_tensor(x_sb[:, t, :], psO[n % 2][:, 0:D], gate[:, t, e:e + 1], x_sb[:, t, :],
                                                         ALU.mult, ALU.add).then_inc(added, 1)

                    each_group(dve, group)
        edge_phase(0)
        node_phase(0)
        edge_phase(1)
        node_phase(1)
        expert_phase()


def kernel(**inputs):
    import concourse.bacc as bacc
    from concourse.bass_utils import run_bass_kernel_spmd

    a = {k: np.asarray(v) for k, v in inputs.items()}
    g, f = "L0_gnn_", "L0_ffn_"

    def side_by_side(kind, n):
        q, k, v, skip = (a[f"{g}{kind}{z}{n}"].T for z in "qkvs")
        pairs = np.stack([k, v], axis=-1).reshape(*k.shape[:-1], 2 * HC)
        return np.ascontiguousarray(np.concatenate([q, pairs, skip], axis=-1))

    x = np.zeros((NP, D), np.float32)
    x[:N] = a["x"]
    src = np.zeros(EP, np.int32)
    src[:E] = a["src"]
    dst = np.full(EP, N, np.int32)
    dst[:E] = a["dst"]
    arrays = {
        "x": x,
        "src": np.ascontiguousarray(src.reshape(STREAMS, BLOCKS, TPB, P).transpose(1, 3, 2, 0).reshape(BLOCKS, P, TPB * STREAMS)),
        "dst": dst,
        "prev": np.concatenate([np.full(1, -1, np.int32), dst[:-1]]),
        "samples": np.ascontiguousarray(dst[:E:SCOLS]),
        "edge_rows": dst[:E].reshape(SROWS, SCOLS).copy(),
        "cut": dst[HALF:HALF + 16].reshape(16, 1).copy(),
        "proj1_w": side_by_side("W", 1), "proj1_b": side_by_side("b", 1),
        "proj2_w": side_by_side("W", 2), "proj2_b": side_by_side("b", 2),
        "wo": np.ascontiguousarray(a[g + "Wo"].T), "bo": a[g + "bo"],
        "wr": a[f + "Wr"], "br": a[f + "br"],
        "expert_w0": a[f + "W1"], "expert_w1": a[f + "W2"], "expert_w2": a[f + "Wo"], "bo8": a[f + "bo"],
        "bn": np.ascontiguousarray(np.stack([[a[f"{f}{k}{n}"] for k in ("b", "g", "be", "m", "v")] for n in (1, 2)])
                                   .reshape(2, 5, EXPERTS * HID // P, P).transpose(3, 0, 1, 2)),
    }
    nc = bacc.Bacc("TRN2", target_bir_lowering=False, num_devices=1)
    d, feed = {}, {}
    for name, v in arrays.items():
        d[name] = nc.dram_tensor(f"in_{name}", v.shape, mybir.dt.from_np(v.dtype), kind="ExternalInput").ap()
        feed[f"in_{name}"] = v
    d["out"] = nc.dram_tensor("out", (NP, D), F32, kind="ExternalOutput").ap()
    build(nc, d)
    r = run_bass_kernel_spmd(nc, [feed], core_ids=[0])
    return r.results[0]["out"][:N]
```

```python
from contextlib import ExitStack

import numpy as np

import concourse.bass as bass
from concourse import mybir

F32 = mybir.dt.float32
F32R = mybir.dt.float32r
BF16 = mybir.dt.bfloat16
I32 = mybir.dt.int32
ALU = mybir.AluOpType
ACT = mybir.ActivationFunctionType
AX = mybir.AxisListType
ts = bass.ts

P = 128
N, E, D = 6250, 106250, 256
HEADS, CH = 4, 16
HC = HEADS * CH
EXPERTS, HID = 8, 256
EXPERT_LAYERS = ("W1", "W2", "Wo")
KC = D // P
LN_EPS, BN_EPS, DEN_EPS = 1e-5, 1e-3, 1e-16

NT = -(-N // P)
NP = NT * P
GROUP = 7
NG = NT // GROUP
assert NG * GROUP == NT

STREAMS = 2
STEP = 512
TPB = STEP // P
UNROLL = 4
BLOCKS = -(-E // (STREAMS * STEP * UNROLL)) * UNROLL
STEPS = BLOCKS // UNROLL
HALF = BLOCKS * STEP
EP = STREAMS * HALF
ROW = HC + 2 * HEADS
DEN, MAX = HC, HC + HEADS

SROWS, SCOLS = 425, 250
assert SROWS * SCOLS == E
NEG = -3.0e38
SKIP = float(1 << 22)

Q0, K0, S0 = 0, HC, 3 * HC
PROJ = 4 * HC
HTOK = GROUP * P // 2
GTOK = GROUP * P
assert STEPS - 2 == len(EXPERT_LAYERS) * EXPERTS


def each_group(eng, body):
    body(0)
    with eng.Fori(1, NG) as g:
        body(g)


class Steps:

    def __init__(self, eng, done, at=0):
        self.eng, self.done, self.at = eng, done, at

    def __call__(self, instruction):
        self.at = self.at + 1
        instruction.then_inc(self.done, 1)
        self.eng.wait_ge(self.done, self.at)


def build(nc, d):
    kv_t = nc.dram_tensor("kv_table", [NP, 2 * HC], F32, kind="Internal").ap()
    q_t = nc.dram_tensor("q_table", [NP, HC], F32, kind="Internal").ap()
    qz_t = nc.dram_tensor("q_at_starts", [EP, HC], F32, kind="Internal").ap()
    sum_t = nc.dram_tensor("running_sums", [EP, ROW], F32, kind="Internal").ap()
    mask_t = nc.dram_tensor("masks", [STREAMS, BLOCKS, 2 * STEP], BF16, kind="Internal").ap()
    qz_blocks = qz_t.rearrange("(b j p s) c -> b p j (s c)", j=TPB, p=P, s=STREAMS)
    sum_blocks = sum_t.rearrange("(b j p s) c -> b p j (s c)", j=TPB, p=P, s=STREAMS)
    kv_nodes = kv_t.rearrange("(i p) c -> p i c", p=P)
    q_nodes = q_t.rearrange("(i p) c -> p i c", p=P)

    with ExitStack() as whole:
        def keep(name, shape, dt=F32):
            return whole.enter_context(nc.sbuf_tensor(name, shape, dt))

        first = whole.enter_context(ExitStack())
        identity = keep("identity", [P, P])
        head_sum = keep("head_sum", [P, P])
        pick = keep("pick", [P, STREAMS * HEADS])
        start_row = keep("start_row", [P, NT], I32)
        end_row = keep("end_row", [P, NT], I32)
        span_bias = keep("span_bias", [P, NT])
        present = keep("present", [P, NT])
        cut_ix = keep("cut_ix", [16, 1], I32)
        cut_q = keep("cut_q", [16, HC])
        eps = keep("eps", [P, 1])
        skip = keep("skip", [P, NT, HC])
        proj = first.enter_context(nc.sbuf_tensor("proj", [P, NT, PROJ], F32))

        def scatter_q(pool, done, projected):
            for i in range(NT):
                pool.wait_ge(projected, i + 1)
                pool.indirect_dma_start(qz_t, bass.IndirectOffsetOnAxis(start_row[:, i:i + 1], 0),
                                        proj[:, i, Q0:Q0 + HC], None,
                                        bounds_check=EP - 1, oob_is_err=False).then_inc(done, 16)

        def scatter_cut(pool, done, stored, got, cut_done):
            pool.wait_ge(stored, 16 * 2 * NG)
            pool.indirect_dma_start(cut_q[:, :], None, q_t, bass.IndirectOffsetOnAxis(cut_ix[:, :], 0),
                                    bounds_check=NP - 1, oob_is_err=False).then_inc(got, 16)
            pool.wait_ge(got, 16)
            pool.wait_ge(done, 16 * NT)
            pool.dma_start(qz_t[1:2, :], cut_q[0:1, :]).then_inc(cut_done, 16)
            pool.wait_ge(cut_done, 16)

        def store_tables(sp, projected, stored):
            with sp.Fori(0, NG) as g:
                sp.wait_ge(projected, GROUP * g + GROUP)
                sp.dma_start(kv_nodes[:, ts(g, GROUP), :], proj[:, ts(g, GROUP), K0:S0]).then_inc(stored, 16)
                sp.dma_start(q_nodes[:, ts(g, GROUP), :], proj[:, ts(g, GROUP), Q0:K0]).then_inc(stored, 16)
            sp.wait_ge(stored, 16 * 2 * NG)

        def layer_norm_moments(step, mean, var, stat):
            step(step.eng.tensor_tensor(mean, stat[:, :, 1], stat[:, :, 4], ALU.subtract))
            step(step.eng.tensor_tensor(var, mean, mean, ALU.mult))
            step(step.eng.scalar_tensor_tensor(var, var, D / 4.0, stat[:, :, 2], ALU.mult, ALU.add))
            step(step.eng.tensor_tensor(var, var, stat[:, :, 5], ALU.add))
            step(step.eng.tensor_scalar(var, var, 1.0 / D, None, ALU.mult))
            step(step.eng.tensor_tensor(mean, stat[:, :, 1], stat[:, :, 4], ALU.add))
            step(step.eng.tensor_scalar(mean, mean, 0.5, None, ALU.mult))

        with ExitStack() as phase:
            def sb(name, shape, dt=F32):
                return phase.enter_context(nc.sbuf_tensor(name, shape, dt))

            def pb(name):
                return phase.enter_context(nc.psum_tensor(name, [P, 512], F32))

            def sem(name):
                return whole.enter_context(nc.semaphore(name))

            x_sb = sb("x_sb", [P, NT, D])
            mv = sb("mv", [P, NT, 2])
            rstd = sb("rstd", [P, NT])
            stat = sb("stat", [P, NT, 6])
            node_i = sb("node_i", [P, NT], I32)
            node = sb("node", [P, NT])
            samples_i = sb("samples_i", [P, SROWS], I32)
            samples = sb("samples", [P, SROWS])
            below = sb("below", [P, GROUP, SROWS], BF16)
            found = sb("found", [P, NT])
            chunk_no = sb("chunk_no", [P, NT])
            chunk_ix = sb("chunk_ix", [P, NT], I32)
            chunk = sb("chunk", [P, NT, SCOLS], I32)
            start = sb("start", [P, NT + 1])
            nxt = sb("nxt", [P, NT])
            t0 = sb("t0", [P, NT])
            t1 = sb("t1", [P, NT])
            shift = sb("shift", [P, P])
            wrap = sb("wrap", [P, P])
            zeros = sb("zeros", [P, EP * HC // P // 32])
            dst_b = sb("dst_b", [BLOCKS, STREAMS, STEP], I32)
            prev_b = sb("prev_b", [BLOCKS, STREAMS, STEP], I32)
            mask_b = sb("mask_b", [BLOCKS, STREAMS, 2, STEP], BF16)
            w1t = sb("w1t", [P, KC, PROJ])
            b1 = sb("b1", [P, PROJ])
            xh = sb("xh", [P, 2, D])
            xT = sb("xT", [P, 2, KC, P])
            psT = [pb(f"psT{i}") for i in range(2)]
            psP = [pb(f"psP{i}") for i in range(2)]
            psN = pb("psN")

            x_in, w_in, edges_in, samples_in, cut_in = (sem(n) for n in (
                "x_in", "w_in", "edges_in", "samples_in", "cut_in"))
            zeroed, filled, constants, numbered, made = (sem(n) for n in (
                "zeroed", "filled", "constants", "numbered", "made"))
            chunk_in = [sem(f"chunk_in{g}") for g in range(NG)]
            chunk_wanted, chunk_ready, started, shifted = (sem(n) for n in (
                "chunk_wanted", "chunk_ready", "started", "shifted"))
            dve_step, stats_done, aggregated, rooted, eps_set = (sem(n) for n in (
                "dve_step", "stats_done", "aggregated", "rooted", "eps_set"))
            rows_ready, masks_made, masks_out = sem("rows_ready"), sem("masks_made"), sem("masks_out")
            xhat_ready, turned, xT_ready, product, projected = (sem(n) for n in (
                "xhat_ready", "turned", "xT_ready", "product", "projected"))
            stored, scattered, cut_got, cut_done = (sem(n) for n in ("stored", "scattered", "cut_got", "cut_done"))
            block = phase.enter_context(nc.Block())

            @block.sync
            def _(sp):
                sp.dma_start(samples_i[:, :], d["samples"].partition_broadcast(P)).then_inc(samples_in, 16)
                sp.dma_start(x_sb[:, :, :], d["x"].rearrange("(i p) c -> p i c", p=P)).then_inc(x_in, 16)
                sp.dma_start(w1t[:, :, :], d["proj1_w"].rearrange("(k p) c -> p k c", p=P)).then_inc(w_in, 16)
                sp.dma_start(b1[:, :], d["proj1_b"].partition_broadcast(P)).then_inc(w_in, 16)
                sp.dma_start(dst_b[:, :, :], d["dst"].rearrange("(s b c) -> b s c", s=STREAMS, c=STEP)).then_inc(edges_in, 16)
                sp.dma_start(prev_b[:, :, :], d["prev"].rearrange("(s b c) -> b s c", s=STREAMS, c=STEP)).then_inc(edges_in, 16)
                sp.dma_start(cut_ix[:, :], d["cut"]).then_inc(cut_in, 16)
                sp.wait_ge(masks_made, 1)
                for s in range(STREAMS):
                    sp.dma_start(mask_t[s], mask_b[:, s, :, :].rearrange("b m c -> b (m c)")).then_inc(masks_out, 16)
                store_tables(sp, projected, stored)
                sp.wait_ge(masks_out, 16 * STREAMS)

            @block.gpsimd
            def _(pool):
                pool.iota(node_i[:, :], pattern=[[P, NT]], base=0, channel_multiplier=1).then_inc(numbered, 1)
                pool.memset(zeros[:, :], 0.0).then_inc(zeroed, 1)
                for m, v in ((identity, 0.0), (shift, 0.0), (wrap, 0.0), (head_sum, CH ** -0.5), (pick, 0.0)):
                    pool.memset(m[:, :], v).then_inc(made, 1)
                pool.wait_ge(made, 5)
                pool.affine_select(out=identity[:, :], in_=identity[:, :], compare_op=ALU.not_equal, fill=1.0,
                                   base=0, pattern=[[-1, P]], channel_multiplier=1).then_inc(constants, 1)
                pool.affine_select(out=shift[:, :], in_=shift[:, :], compare_op=ALU.not_equal, fill=1.0,
                                   base=-1, pattern=[[-1, P]], channel_multiplier=1).then_inc(constants, 1)
                pool.memset(wrap[0:1, P - 1:P], 1.0).then_inc(constants, 1)
                pool.affine_select(out=pick[:, :], in_=pick[:, :], compare_op=ALU.not_equal, fill=1.0,
                                   base=0, pattern=[[-CH, STREAMS * HEADS]], channel_multiplier=1).then_inc(constants, 1)
                blocks = head_sum[:, :].rearrange("p (j c) -> p j c", c=CH)
                pool.affine_select(out=blocks, in_=blocks, compare_op=ALU.is_ge, fill=0.0, base=0,
                                   pattern=[[-CH, P // CH], [0, CH]], channel_multiplier=1).then_inc(made, 1)
                pool.wait_ge(made, 6)
                pool.affine_select(out=blocks, in_=blocks, compare_op=ALU.is_ge, fill=0.0, base=CH - 1,
                                   pattern=[[CH, P // CH], [0, CH]], channel_multiplier=-1).then_inc(constants, 1)
                for g in range(NG):
                    pool.wait_ge(chunk_wanted, g + 1)
                    for i in range(GROUP * g, GROUP * (g + 1)):
                        pool.indirect_dma_start(chunk[:, i, :], None, d["edge_rows"],
                                                bass.IndirectOffsetOnAxis(chunk_ix[:, i:i + 1], 0),
                                                bounds_check=SROWS - 1, oob_is_err=False).then_inc(chunk_in[g], 16)
                pool.wait_ge(rows_ready, 1)
                pool.wait_ge(filled, 16 * 4)
                scatter_q(pool, scattered, projected)
                pool.wait_ge(cut_in, 16)
                scatter_cut(pool, scattered, stored, cut_got, cut_done)

            @block.scalar
            def _(act):
                act.wait_ge(zeroed, 1)
                fill = qz_t.rearrange("(p r) c -> p (r c)", p=P).rearrange("p (m k n) -> m p k n", m=4, k=8)
                for m in range(4):
                    act.dma_start(fill[m], zeros[:, :].unsqueeze(1).to_broadcast([P, 8, EP * HC // P // 32])).then_inc(filled, 16)
                act.wait_ge(eps_set, 1)
                act.wait_ge(aggregated, 1)
                act.activation(rstd[:, :], mv[:, :, 1], ACT.Sqrt, bias=eps[:, 0:1]).then_inc(rooted, 1)
                def group(g):
                    for u in range(GROUP):
                        t = GROUP * g + u
                        act.wait_ge(turned, t + 1)
                        act.wait_ge(product, t if u == 0 else t - 1)
                        act.activation(xT[:, u % 2, :, :].rearrange("p k n -> p (k n)"), psT[u % 2][:, 0:D],
                                       ACT.Copy).then_inc(xT_ready, 1)
                each_group(act, group)
                act.wait_ge(filled, 16 * 4)

            @block.tensor
            def _(pe):
                pe.wait_ge(constants, 5)
                pe.wait_ge(started, 1)
                pe.matmul(psN[:, 0:NT], shift[:, :], start[:, 0:NT], start=True, stop=False)
                pe.matmul(psN[:, 0:NT], wrap[:, :], start[:, 1:NT + 1], start=False, stop=True).then_inc(shifted, 1)
                pe.wait_ge(w_in, 32)
                def group(g):
                    for k in range(GROUP + 1):
                        if k < GROUP:
                            t = GROUP * g + k
                            pe.wait_ge(xhat_ready, t + 1)
                            pe.wait_ge(xT_ready, t if k == 0 else t - 1)
                            for c in range(KC):
                                ins = pe.transpose(psT[k % 2][:, P * c:P * (c + 1)], xh[:, k % 2, P * c:P * (c + 1)], identity[:, :])
                            ins.then_inc(turned, 1)
                        if k >= 1:
                            u, t = k - 1, GROUP * g + k - 1
                            pe.wait_ge(xT_ready, t + 1)
                            pe.wait_ge(projected, t if u == 0 else t - 1)
                            for c in range(KC):
                                ins = pe.matmul(psP[u % 2][:, 0:PROJ], xT[:, u % 2, c, :], w1t[:, c, :],
                                                start=(c == 0), stop=(c == KC - 1))
                            ins.then_inc(product, 1)

                each_group(pe, group)
            @block.vector
            def _(dve):
                dve.memset(eps[:, :], LN_EPS).then_inc(eps_set, 1)
                step = Steps(dve, dve_step)
                dve.wait_ge(numbered, 1)
                step(dve.tensor_copy(node[:, :], node_i[:, :]))
                dve.wait_ge(samples_in, 16)
                step(dve.tensor_copy(samples[:, :], samples_i[:, :]))
                for g in range(NG):
                    of = slice(GROUP * g, GROUP * (g + 1))
                    step(dve.tensor_tensor(below[:, :, :], samples[:, :].unsqueeze(1).to_broadcast([P, GROUP, SROWS]),
                                           node[:, of].unsqueeze(2).to_broadcast([P, GROUP, SROWS]), ALU.is_lt))
                    step(dve.tensor_reduce(found[:, of], below[:, :, :], AX.X, ALU.add))
                    step(dve.tensor_scalar(chunk_no[:, of], found[:, of], -1.0, 0.0, ALU.add, ALU.max))
                    dve.tensor_copy(chunk_ix[:, of], chunk_no[:, of]).then_inc(chunk_wanted, 1)
                dve.wait_ge(edges_in, 32)
                step(dve.tensor_tensor(mask_b[:, :, 0, :], dst_b[:, :, :], prev_b[:, :, :], ALU.is_equal))
                step(dve.memset(mask_b[0:1, 1, 0, 0:1], 0.0))
                step(dve.tensor_scalar(mask_b[:, :, 1, :], mask_b[:, :, 0, :], -NEG, NEG, ALU.mult, ALU.add))
                dve.sem_inc(masks_made, 1)
                dve.wait_ge(x_in, 16)
                with dve.Fori(0, NG) as g:
                    for u in range(GROUP):
                        ins = dve.bn_stats(stat[:, ts(GROUP * g + u, 1), :].rearrange("p i c -> p (i c)"), x_sb[:, GROUP * g + u, :])
                    ins.then_inc(stats_done, 1)
                dve.wait_ge(stats_done, NG)
                step_norm = Steps(dve, stats_done, NG)
                layer_norm_moments(step_norm, mv[:, :, 0], mv[:, :, 1], stat)
                dve.sem_inc(aggregated, 1)
                dve.wait_ge(rooted, 1)
                step_norm(dve.reciprocal(rstd[:, :], rstd[:, :]))
                for g in range(NG):
                    of = slice(GROUP * g, GROUP * (g + 1))
                    dve.wait_ge(chunk_in[g], 16 * GROUP)
                    step(dve.tensor_tensor(below[:, :, 0:SCOLS], chunk[:, of, :],
                                           node[:, of].unsqueeze(2).to_broadcast([P, GROUP, SCOLS]), ALU.is_lt))
                    step(dve.tensor_reduce(found[:, of], below[:, :, 0:SCOLS], AX.X, ALU.add))
                step(dve.memset(start[:, NT:NT + 1], float(E)))
                step(dve.scalar_tensor_tensor(start[:, 0:NT], chunk_no[:, :], float(SCOLS), found[:, :], ALU.mult, ALU.add))
                dve.sem_inc(started, 1)
                dve.wait_ge(shifted, 1)
                step(dve.tensor_copy(nxt[:, :], psN[:, 0:NT]))
                first = start[:, 0:NT]
                step(dve.tensor_tensor(present[:, :], nxt[:, :], first, ALU.is_gt))
                step(dve.tensor_scalar(t0[:, :], first, float(HALF), 1.0 - 2 * HALF, ALU.is_ge, ALU.mult))
                step(dve.scalar_tensor_tensor(t0[:, :], first, 2.0, t0[:, :], ALU.mult, ALU.add))
                step(dve.tensor_scalar(t1[:, :], present[:, :], -SKIP, SKIP, ALU.mult, ALU.add))
                step(dve.tensor_tensor(start_row[:, :], t0[:, :], t1[:, :], ALU.add))
                dve.sem_inc(rows_ready, 1)
                step(dve.tensor_scalar(t0[:, :], first, float(HALF), None, ALU.is_lt))
                step(dve.scalar_tensor_tensor(t0[:, :], nxt[:, :], float(HALF), t0[:, :], ALU.is_gt, ALU.mult))
                step(dve.tensor_scalar(span_bias[:, :], t0[:, :], -NEG, NEG, ALU.mult, ALU.add))
                step(dve.tensor_scalar(nxt[:, :], nxt[:, :], -1.0, 0.0, ALU.add, ALU.max))
                step(dve.tensor_scalar(t0[:, :], nxt[:, :], float(HALF), 1.0 - 2 * HALF, ALU.is_ge, ALU.mult))
                step(dve.scalar_tensor_tensor(end_row[:, :], nxt[:, :], 2.0, t0[:, :], ALU.mult, ALU.add))
                dve.wait_ge(w_in, 32)
                def group(g):
                    for k in range(GROUP + 2):
                        if k < GROUP:
                            t = GROUP * g + k
                            dve.wait_ge(turned, t if k == 0 else t - 1)
                            dve.tensor_scalar(xh[:, k % 2, :], x_sb[:, t, :], mv[:, t, 0:1], rstd[:, ts(t, 1)],
                                              ALU.subtract, ALU.mult).then_inc(xhat_ready, 1)
                        if k >= 2:
                            t = GROUP * g + k - 2
                            dve.wait_ge(product, t + 1)
                            dve.tensor_tensor(proj[:, t, :], psP[(k - 2) % 2][:, 0:PROJ], b1[:, :],
                                              ALU.add).then_inc(projected, 1)

                each_group(dve, group)
        def edge_sem(name):
            return whole.enter_context(nc.semaphore(name))

        ix_in = [edge_sem(f"ix_in{u}") for u in range(UNROLL)]
        kv_in = [edge_sem(f"kv_in{u}") for u in range(UNROLL)]
        q_in = [edge_sem(f"q_in{u}") for u in range(UNROLL)]
        mask_in = [edge_sem(f"mask_in{u}") for u in range(UNROLL)]
        rows_out = [edge_sem(f"rows_out{i}") for i in range(2)]
        cleared, kq_turned, v_turned, out_turned = (edge_sem(n) for n in ("cleared", "kq_turned", "v_turned", "out_turned"))
        q_held, kq_ready, logits_ready, carried, top_ready = (edge_sem(n) for n in (
            "q_held", "kq_ready", "logits_ready", "carried", "top_ready"))
        grown, gaps_ready, ex_ready, weighted, v_summed, d_summed, copied, gathering = (edge_sem(n) for n in (
            "grown", "gaps_ready", "ex_ready", "weighted", "v_summed", "d_summed", "copied", "gathering"))

        w_in, w_high, w_parted = (edge_sem(n) for n in ("expert_w_in", "expert_w_high", "expert_w_parted"))

        def edge_phase(layer):
            with ExitStack() as phase:
                def sb(name, shape, dt=F32):
                    return phase.enter_context(nc.sbuf_tensor(f"{name}_{layer}", shape, dt))

                def pb(name):
                    return phase.enter_context(nc.psum_tensor(f"{name}_{layer}", [P, STEP], F32))

                U = UNROLL
                ix = sb("ix", [P, U, TPB * STREAMS], I32)
                kv = sb("kv", [P, U, TPB, STREAMS * 2 * HC])
                qz = sb("qz", [P, U, TPB, STREAMS * HC])
                mask = sb("mask", [P, U, 2, STEP], BF16)
                held_q = sb("held_q", [P, 2, STEP])
                kq = sb("kq", [P, 2, STEP])
                top = sb("top", [P, U, 1 + STEP])
                gap = sb("gap", [P, 2, 2, STEP])
                ex = sb("ex", [P, 2, 2, STEP])
                wv = sb("wv", [P, 2, STEP])
                run_v = sb("run_v", [P, U, STEP])
                run_d = sb("run_d", [P, U, STEP])
                rows = sb("rows", [P, 2, TPB, STREAMS, ROW])
                if layer == 1:
                    w_raw = sb("w_raw", [P, KC * HID])
                kT = [pb(f"kT{i}") for i in range(2)]
                qT = [pb(f"qT{i}") for i in range(2)]
                vT, logit, outT = pb("vT"), pb("logit"), pb("outT")
                restT = pb("restT")[:, 0:2 * TPB * STREAMS * HEADS].rearrange("p (m j h) -> p m j h", m=2, j=TPB)

                block = phase.enter_context(nc.Block())

                past = STEPS * layer
                peeled = 2

                def each_step(eng, body):
                    for i in range(past, past + peeled):
                        body(i)
                    with eng.Fori(past + peeled, past + STEPS) as i:
                        body(i)

                def each_block(eng, stages, before=None, after=None):
                    def body(i):
                        if before and layer == 1 and not isinstance(i, int):
                            before(i - past - peeled)
                        blocks(i)
                        if after and layer == 1 and not isinstance(i, int):
                            after(i - past - peeled)

                    def blocks(i):
                        for u in range(U):
                            for lag, stage in enumerate(stages):
                                b = U * i + u - lag
                                if not isinstance(i, int) or b >= U * past:
                                    stage(b, (u - lag) % U, i if u >= lag else i - 1)
                    each_step(eng, body)
                    for late in range(1, len(stages)):
                        for lag in range(late, len(stages)):
                            b = U * (past + STEPS) + late - 1 - lag
                            stages[lag](b, b % U, b // U)

                def wait_past(eng, done, count):
                    if not isinstance(count, int) or count >= 1:
                        eng.wait_ge(done, count)

                @block.sync
                def _(sp):
                    def body(i):
                        for u in range(U):
                            b = U * i + u
                            wait_past(sp, kq_turned, b - U + 1)
                            wait_past(sp, gaps_ready, b - U + 1)
                            wait_past(sp, v_turned, b - U + 1)
                            sp.dma_start(ix[:, u, :], d["src"][b - BLOCKS * layer]).then_inc(ix_in[u], 16)
                            sp.dma_start(qz[:, u, :, :], qz_blocks[b - BLOCKS * layer]).then_inc(q_in[u], 16)
                            for s in range(STREAMS):
                                sp.dma_start(mask[HC * s:HC * (s + 1), u, :, :].rearrange("p m c -> p (m c)"),
                                             mask_t[s, b - BLOCKS * layer].partition_broadcast(HC)).then_inc(mask_in[u], 16)
                    def with_weights(i):
                        body(i)
                        if layer == 1 and not isinstance(i, int):
                            n = i - past - peeled
                            sp.wait_ge(w_parted, n + 1)
                            sp.dma_start(w_raw[:, :], d["expert_w"][n]).then_inc(w_in, 16)
                    each_step(sp, with_weights)

                @block.gpsimd
                def _(pool):
                    def body(i):
                        for u in range(U):
                            pool.wait_ge(ix_in[u], 16 * i + 16)
                            pool.sem_inc(gathering, 1)
                            for j in range(TPB):
                                for s in range(STREAMS):
                                    n = STREAMS * j + s
                                    pool.indirect_dma_start(kv[:, u, j, 2 * HC * s:2 * HC * (s + 1)], None, kv_t,
                                                            bass.IndirectOffsetOnAxis(ix[:, u, n:n + 1], 0),
                                                            bounds_check=NP - 1, oob_is_err=False).then_inc(kv_in[u], 16)
                    each_step(pool, body)

                @block.tensor
                def _(pe):
                    def turn_kq(b, u, i):
                        pe.wait_ge(kv_in[u], 16 * TPB * STREAMS * (i + 1))
                        pe.wait_ge(q_in[u], 16 * i + 16)
                        wait_past(pe, kq_ready, b - 1)
                        for j in range(TPB):
                            pe.transpose(kT[u % 2][:, P * j:P * (j + 1)], kv[:, u, j, 0::2], identity[:, :])
                            ins = pe.transpose(qT[u % 2][:, P * j:P * (j + 1)], qz[:, u, j, :], identity[:, :])
                        ins.then_inc(kq_turned, 1)

                    def logits(b, u, i):
                        pe.wait_ge(kq_ready, b + 1)
                        wait_past(pe, gaps_ready, b)
                        pe.matmul(logit[:, :], head_sum[:, :], kq[:, u % 2, :], start=True, stop=True)\
                            .then_inc(logits_ready, 1)

                    def turn_v(b, u, i):
                        wait_past(pe, weighted, b)
                        for j in range(TPB):
                            ins = pe.transpose(vT[:, P * j:P * (j + 1)], kv[:, u, j, 1::2], identity[:, :])
                        ins.then_inc(v_turned, 1)

                    def turn_results(b, u, i):
                        pe.wait_ge(v_summed, b + 1)
                        pe.wait_ge(d_summed, b + 1)
                        wait_past(pe, copied, 3 * b)
                        for j in range(TPB):
                            of = slice(P * j, P * (j + 1))
                            pe.transpose(outT[:, of], run_v[:, u, of], identity[:, :])
                            pe.matmul(restT[:, 0, j, :], run_d[:, u, of], pick[:, :], start=True, stop=True)
                            ins = pe.matmul(restT[:, 1, j, :], top[:, u, 1 + P * j:1 + P * (j + 1)], pick[:, :],
                                            start=True, stop=True)
                        ins.then_inc(out_turned, 1)

                    each_block(pe, [turn_kq, logits, turn_v, turn_results])

                @block.vector
                def _(dve):
                    dve.memset(held_q[:, 1, STEP - 1:STEP], 0.0).then_inc(cleared, 1)
                    dve.memset(top[:, U - 1, STEP:STEP + 1], 0.0).then_inc(cleared, 1)
                    dve.memset(run_v[:, U - 1, STEP - 1:STEP], 0.0).then_inc(cleared, 1)
                    dve.memset(run_d[:, U - 1, STEP - 1:STEP], 0.0).then_inc(cleared, 1)
                    dve.wait_ge(cleared, 4 * layer + 4)
                    if layer == 1:
                        dve.sem_inc(w_parted, 1)

                    def part_low(n):
                        dve.wait_ge(w_high, n + 1)
                        dve.tensor_tensor(w_lo[:, n, :], w_raw[:, :], w_hi[:, n, :].bitcast(F32),
                                          ALU.subtract).then_inc(w_parted, 1)

                    def hold_q(b, u, i):
                        h = u % 2
                        dve.wait_ge(kq_turned, b + 1)
                        dve.wait_ge(mask_in[u], 32 * i + 32)
                        wait_past(dve, q_held, b)
                        dve.tensor_tensor_scan(held_q[:, h, :], mask[:, u, 0, :], qT[h][:, :],
                                               held_q[:, 1 - h, STEP - 1:STEP], ALU.mult, ALU.add).then_inc(q_held, 1)
                        dve.wait_ge(q_held, b + 1)
                        wait_past(dve, logits_ready, b - 1)
                        dve.tensor_tensor(kq[:, h, :], kT[h][:, :], held_q[:, h, :], ALU.mult).then_inc(kq_ready, 1)

                    def maximum(b, u, i):
                        h = u % 2
                        before, now = top[:, u, 0:STEP], top[:, u, 1:1 + STEP]
                        last = top[:, (u - 1) % U, STEP:STEP + 1]
                        wait_past(dve, top_ready, b)
                        wait_past(dve, out_turned, b - U + 1)
                        dve.tensor_copy(top[:, u, 0:1], last).then_inc(carried, 1)
                        dve.wait_ge(logits_ready, b + 1)
                        dve.tensor_tensor_scan(now, mask[:, u, 1, :], logit[:, :], last,
                                               ALU.add, ALU.max).then_inc(top_ready, 1)
                        dve.wait_ge(top_ready, b + 1)
                        dve.wait_ge(carried, b + 1)
                        wait_past(dve, ex_ready, b - 1)
                        dve.tensor_tensor(gap[:, h, 1, :], before, now, ALU.subtract).then_inc(grown, 1)
                        dve.tensor_tensor(gap[:, h, 0, :], logit[:, :], now, ALU.subtract).then_inc(grown, 1)
                        dve.wait_ge(grown, 2 * b + 2)
                        dve.tensor_tensor(gap[:, h, 1, :], gap[:, h, 1, :], mask[:, u, 1, :], ALU.add).then_inc(gaps_ready, 1)

                    def sums(b, u, i):
                        h = u % 2
                        dve.wait_ge(ex_ready, b + 1)
                        dve.wait_ge(v_turned, b + 1)
                        dve.tensor_tensor(wv[:, h, :], vT[:, :], ex[:, h, 0, :], ALU.mult).then_inc(weighted, 1)
                        wait_past(dve, out_turned, b - U + 1)
                        wait_past(dve, d_summed, b)
                        dve.tensor_tensor_scan(run_d[:, u, :], ex[:, h, 1, :], ex[:, h, 0, :],
                                               run_d[:, (u - 1) % U, STEP - 1:STEP], ALU.mult, ALU.add).then_inc(d_summed, 1)
                        dve.wait_ge(weighted, b + 1)
                        wait_past(dve, v_summed, b)
                        dve.tensor_tensor_scan(run_v[:, u, :], ex[:, h, 1, :], wv[:, h, :],
                                               run_v[:, (u - 1) % U, STEP - 1:STEP], ALU.mult, ALU.add).then_inc(v_summed, 1)

                    each_block(dve, [hold_q, maximum, sums], after=part_low)

                @block.scalar
                def _(act):
                    def weights(b, u, i):
                        h = u % 2
                        act.wait_ge(gaps_ready, b + 1)
                        wait_past(act, v_summed, b - 1)
                        act.activation(ex[:, h, :, :].rearrange("p m c -> p (m c)"),
                                       gap[:, h, :, :].rearrange("p m c -> p (m c)"), ACT.Exp).then_inc(ex_ready, 1)

                    def store(b, u, i):
                        h = u % 2
                        act.wait_ge(out_turned, b + 1)
                        wait_past(act, rows_out[h], 16 * (U // 2 * i + u // 2))
                        flat = rows[:, h, :, :, :].rearrange("p j s c -> p (j s) c")
                        act.activation(flat[:, :, 0:HC], outT[:, :].rearrange("p (r c) -> p r c", c=HC),
                                       ACT.Copy).then_inc(copied, 1)
                        for m, at in enumerate((DEN, MAX)):
                            act.activation(flat[:, :, at:at + HEADS],
                                           restT[:, m, :, :].rearrange("p j (s h) -> p (j s) h", h=HEADS),
                                           ACT.Copy).then_inc(copied, 1)
                        act.wait_ge(copied, 3 * b + 3)
                        act.dma_start(sum_blocks[b - BLOCKS * layer], rows[:, h, :, :, :].rearrange("p j s c -> p j (s c)"))\
                            .then_inc(rows_out[h], 16)

                    def part_high(n):
                        act.wait_ge(w_in, 16 * n + 16)
                        act.activation(w_hi[:, n, :], w_raw[:, :], ACT.Copy).then_inc(w_high, 1)

                    each_block(act, [weights, lambda b, u, i: None, store], before=part_high)
                    for h in range(2):
                        act.wait_ge(rows_out[h], 16 * BLOCKS // 2 * (layer + 1))

        def node_phase():
            with ExitStack() as phase:
                def sb(name, shape, dt=F32):
                    return phase.enter_context(nc.sbuf_tensor(f"{name}_n", shape, dt))

                def pb(name):
                    return phase.enter_context(nc.psum_tensor(f"{name}_n", [P, 512], F32))

                def sem(name):
                    return whole.enter_context(nc.semaphore(f"{name}_n"))

                G = GROUP
                fin = sb("fin", [P, NT, ROW])
                cut = sb("cut", [P, ROW])
                h = sb("h", [P, NT, HC])
                mb = sb("mb", [P, G, HEADS])
                mm = sb("mm", [P, G, HEADS])
                wt = sb("wt", [P, G, 2, HEADS])
                wx = sb("wx", [P, G, 2, HEADS])
                den = sb("den", [P, G, HEADS])
                part = sb("part", [P, G, HEADS])
                ov = sb("ov", [P, G, HC])
                hs = sb("hs", [P, 2, HC])
                hT = sb("hT", [HC, 2, P])
                w_sb = sb("w_sb", [HC, D])
                b_sb = sb("b_sb", [P, D])
                psT = [pb(f"psT{i}") for i in range(2)]
                psP = [pb(f"psP{i}") for i in range(2)]
                fin_in = [sem(f"fin_in{g}") for g in range(NG)]
                w_in, cut_in, fins, weights_wanted, weights_ready, comb = (sem(n) for n in (
                    "w_in", "cut_in", "fins", "weights_wanted", "weights_ready", "comb"))
                combined, hs_ready, turned, hT_ready, product, projected = (sem(n) for n in (
                    "combined", "hs_ready", "turned", "hT_ready", "product", "projected"))
                stored, scattered, cut_got, cut_done = (sem(n) for n in ("stored", "scattered", "cut_got", "cut_done"))
                skipped = sem("skipped")
                block = phase.enter_context(nc.Block())

                @block.sync
                def _(sp):
                    sp.dma_start(cut[:, :], sum_t[2 * (HALF - 1)].partition_broadcast(P)).then_inc(cut_in, 16)
                    sp.dma_start(w_sb[:, :], d["proj2_w"]).then_inc(w_in, 16)
                    sp.dma_start(b_sb[:, :], d["proj2_b"].partition_broadcast(P)).then_inc(w_in, 16)
                    store_tables(sp, projected, stored)

                @block.gpsimd
                def _(pool):
                    for g in range(NG):
                        for i in range(G * g, G * (g + 1)):
                            pool.indirect_dma_start(fin[:, i, :], None, sum_t,
                                                    bass.IndirectOffsetOnAxis(end_row[:, i:i + 1], 0),
                                                    bounds_check=EP - 1, oob_is_err=False).then_inc(fin_in[g], 16)
                    for g in range(NG):
                        pool.wait_ge(fin_in[g], 16 * G)
                        pool.sem_inc(fins, 1)
                    scatter_q(pool, scattered, projected)
                    scatter_cut(pool, scattered, stored, cut_got, cut_done)

                @block.tensor
                def _(pe):
                    pe.wait_ge(w_in, 16 * 2)
                    def group(g):
                        for k in range(G + 1):
                            if k < G:
                                t = G * g + k
                                pe.wait_ge(hs_ready, t + 1)
                                pe.wait_ge(hT_ready, t if k == 0 else t - 1)
                                pe.matmul(psT[k % 2][0:HC, 0:P], hs[:, k % 2, :], identity[:, :],
                                          start=True, stop=True).then_inc(turned, 1)
                            if k >= 1:
                                u, t = k - 1, G * g + k - 1
                                pe.wait_ge(hT_ready, t + 1)
                                pe.wait_ge(projected, t if u == 0 else t - 1)
                                pe.wait_ge(skipped, t if u == 0 else t - 1)
                                pe.matmul(psP[u % 2][:, 0:D], hT[:, u % 2, :], w_sb[:, :],
                                          start=True, stop=True).then_inc(product, 1)
                    each_group(pe, group)

                @block.scalar
                def _(act):
                    with act.Fori(0, NG) as g:
                        act.wait_ge(weights_wanted, g + 1)
                        act.activation(wx[:, :, :, :].rearrange("p i m h -> p (i m h)"),
                                       wt[:, :, :, :].rearrange("p i m h -> p (i m h)"), ACT.Exp).then_inc(weights_ready, 1)
                    def group(g):
                        act.wait_ge(combined, g + 1)
                        for k in range(G):
                                t = G * g + k
                                act.wait_ge(turned, t if k == 0 else t - 1)
                                act.activation(hs[:, k % 2, :], h[:, t, :], ACT.Copy).then_inc(hs_ready, 1)
                                act.wait_ge(turned, t + 1)
                                act.wait_ge(product, t if k == 0 else t - 1)
                                act.activation(hT[:, k % 2, :], psT[k % 2][0:HC, 0:P], ACT.Copy).then_inc(hT_ready, 1)
                    each_group(act, group)

                @block.vector
                def _(dve):
                    dve.wait_ge(cut_in, 16)
                    dve.wait_ge(w_in, 16 * 2)
                    COMB = 14
                    all4 = [P, G, HEADS]
                    all64 = [P, G, HEADS, CH]

                    def by_head(a):
                        return a.rearrange("p i (h c) -> p i h c", c=CH)

                    with dve.Fori(0, NG) as g:
                        step = Steps(dve, comb, COMB * g)
                        of = ts(g, G)
                        dve.wait_ge(fins, g + 1)
                        step(dve.tensor_tensor(mb[:, :, :], span_bias[:, of].unsqueeze(2).to_broadcast(all4),
                                               cut[:, MAX:MAX + HEADS].unsqueeze(1).to_broadcast(all4), ALU.add))
                        step(dve.tensor_tensor(mm[:, :, :], mb[:, :, :], fin[:, of, MAX:MAX + HEADS], ALU.max))
                        step(dve.tensor_tensor(wt[:, :, 0, :], fin[:, of, MAX:MAX + HEADS], mm[:, :, :], ALU.subtract))
                        step(dve.tensor_tensor(wt[:, :, 1, :], mb[:, :, :], mm[:, :, :], ALU.subtract))
                        dve.sem_inc(weights_wanted, 1)
                        dve.wait_ge(weights_ready, g + 1)
                        step(dve.tensor_tensor(den[:, :, :], fin[:, of, DEN:DEN + HEADS], wx[:, :, 0, :], ALU.mult))
                        step(dve.tensor_tensor(part[:, :, :], cut[:, DEN:DEN + HEADS].unsqueeze(1).to_broadcast(all4),
                                               wx[:, :, 1, :], ALU.mult))
                        step(dve.scalar_tensor_tensor(den[:, :, :].rearrange("p i h -> p (i h)"), den[:, :, :].rearrange("p i h -> p (i h)"),
                                                      DEN_EPS, part[:, :, :].rearrange("p i h -> p (i h)"), ALU.add, ALU.add))
                        step(dve.reciprocal(den[:, :, :], den[:, :, :]))
                        step(dve.tensor_tensor(den[:, :, :], den[:, :, :], present[:, of].unsqueeze(2).to_broadcast(all4), ALU.mult))
                        step(dve.tensor_tensor(wx[:, :, :, :], wx[:, :, :, :], den[:, :, :].unsqueeze(2).to_broadcast([P, G, 2, HEADS]), ALU.mult))
                        step(dve.tensor_tensor(by_head(h[:, of, :]), by_head(fin[:, of, 0:HC]),
                                               wx[:, :, 0, :].unsqueeze(3).to_broadcast(all64), ALU.mult))
                        step(dve.tensor_tensor(by_head(ov[:, :, :]), wx[:, :, 1, :].unsqueeze(3).to_broadcast(all64),
                                               cut[:, 0:HC].rearrange("p (h c) -> p h c", c=CH).unsqueeze(1).to_broadcast(all64), ALU.mult))
                        step(dve.tensor_tensor(h[:, of, :], h[:, of, :], ov[:, :, :], ALU.add))
                        step(dve.tensor_tensor(ov[:, :, :], h[:, of, :], proj[:, of, S0:S0 + HC], ALU.add))
                        dve.tensor_scalar(h[:, of, :], ov[:, :, :], 0.0, None, ALU.max).then_inc(combined, 1)
                    with dve.Fori(0, NG) as g:
                        for k in range(G):
                            t = G * g + k
                            dve.wait_ge(product, t + 1)
                            dve.tensor_tensor(proj[:, t, 0:S0], psP[k % 2][:, 0:S0], b_sb[:, 0:S0], ALU.add).then_inc(projected, 1)
                            dve.tensor_tensor(skip[:, t, :], psP[k % 2][:, S0:PROJ], b_sb[:, S0:PROJ], ALU.add).then_inc(skipped, 1)

        def expert_phase():
            with ExitStack() as phase:
                def sb(name, shape, dt=F32):
                    return phase.enter_context(nc.sbuf_tensor(f"{name}_x", shape, dt))

                def pb(name):
                    return phase.enter_context(nc.psum_tensor(f"{name}_x", [P, 512], F32))

                def sem(name):
                    return whole.enter_context(nc.semaphore(f"{name}_x"))

                G = GROUP
                LH, LO = HID // P, EXPERTS * HID // P
                fin = sb("fin", [P, G, ROW])
                cut = sb("cut", [P, ROW])
                mb = sb("mb", [P, G, HEADS])
                mm = sb("mm", [P, G, HEADS])
                wt = sb("wt", [P, G, 2, HEADS])
                wx = sb("wx", [P, G, 2, HEADS])
                den = sb("den", [P, G, HEADS])
                part = sb("part", [P, G, HEADS])
                ov = sb("ov", [P, G, HC])
                h = sb("h", [P, G, HC])
                hT = sb("hT", [HC + 1, GTOK])
                wo = sb("wo", [HC + 1, D])
                x = sb("x", [P, G, D])
                y = sb("y", [P, G, D])
                stat = sb("stat", [P, G, 6])
                mv = sb("mv", [P, G, 2])
                rstd = sb("rstd", [P, G])
                y_hi = sb("y_hi", [P, KC, GTOK], F32R)
                y_lo = sb("y_lo", [P, KC, GTOK], F32R)
                wr = sb("wr", [P, KC, EXPERTS])
                wr_hi = sb("wr_hi", [P, KC, EXPERTS], F32R)
                wr_lo = sb("wr_lo", [P, KC, EXPERTS], F32R)
                br = sb("br", [P, EXPERTS])
                gate = sb("gate", [P, G, EXPERTS])
                red = sb("red", [P, G])
                gT = sb("gT", [EXPERTS, GTOK])
                bo8 = sb("bo8", [EXPERTS, D])
                bn = sb("bn", [P, 2, 5, LO])
                scale = sb("scale", [P, 2, LO])
                offset = sb("offset", [P, 2, LO])
                bn_eps = sb("bn_eps", [P, 1])
                full = sb("full", [P, 4, HTOK])
                hid_hi = [sb(f"hid_hi{n}", [P, LH, GTOK], F32R) for n in range(2)]
                hid_lo = [sb(f"hid_lo{n}", [P, LH, GTOK], F32R) for n in range(2)]
                total = sb("total", [P, G, D])
                psH = [pb(f"psH{i}") for i in range(4)]
                psO = [pb(f"psO{i}") for i in range(2)]
                psA = [pb(f"psA{i}") for i in range(2)]

                consts_in, bn_in, bn_eps_set, bn_rooted, bn_step, folded, wr_split = (sem(n) for n in (
                    "consts_in", "bn_in", "bn_eps_set", "bn_rooted", "bn_step", "folded", "wr_split"))
                fin_in, x_in, combined, weights_wanted, weights_ready, comb = (sem(n) for n in (
                    "fin_in", "x_in", "combined", "weights_wanted", "weights_ready", "comb"))
                residual, stats_done, aggregated, rooted, norm, y_ready, y_high = (sem(n) for n in (
                    "residual", "stats_done", "aggregated", "rooted", "norm", "y_ready", "y_high"))
                smax, gap_ready, exp_ready, gate_ready, bias_added = (sem(n) for n in (
                    "smax", "gap_ready", "exp_ready", "gate_ready", "bias_added"))
                ones = sem("ones")
                in_bank, bank_read = sem("in_bank"), [sem(f"bank_read{i}") for i in range(2)]
                formed, relued, parted, out_formed, added, stored = (sem(n) for n in (
                    "hid_formed", "hid_relued", "hid_parted", "out_formed", "out_added", "out_stored"))
                block = phase.enter_context(nc.Block())

                TURN_H, PROJECT, TURN_Y = 0, 2, 6
                ROUTE, TURN_GATE, BIAS = 10, 11, 13
                USES = 17

                def bank_of(use):
                    return psA[use % 2]

                def reads_before(p, use):
                    return (9 if use % 2 == 0 else 8) * p + use // 2

                def wait_free(pe, p, use):
                    count = reads_before(p, use)
                    if not isinstance(count, int) or count >= 1:
                        pe.wait_ge(bank_read[use % 2], count)

                def wait_read(eng, p, use):
                    eng.wait_ge(bank_read[use % 2], reads_before(p, use) + 1)

                def wait_in_bank(eng, p, use):
                    eng.wait_ge(in_bank, USES * p + use + 1)

                def pairs(use_of_kind):
                    return slice(2 * use_of_kind, min(2 * use_of_kind + 2, G))

                QUADS = (slice(0, 4), slice(4, G))

                order = [(0, 0)] + [z for e in range(EXPERTS) for z in ((e, 1), (e + 1, 0))][:-1]
                place = {z: 4 * n for n, z in enumerate(order)}
                PER = 4 * len(order)
                OUTS = EXPERTS * G
                FREE_RELUED, FREE_PARTED, FREE_OUT, FREE_ADDED = 2 * 4, 4, G, 2

                def all_groups(eng, before, experts):
                    for slot in sorted(before(0)):
                        before(0)[slot]()
                    with eng.Fori(0, NG - 1) as g:
                        experts(g, before(g + 1))
                    experts(NG - 1, {})

                def run(pieces, e, n):
                    if (e, n) in pieces:
                        pieces[e, n]()

                @block.sync
                def _(sp):
                    sp.sem_inc(stored, 16)
                    sp.dma_start(bn[:, :, :, :], d["bn"]).then_inc(bn_in, 16)
                    for to, name in ((wo[:, :], d["wo_bo"]),
                                     (wr[:, :, :], d["wr"].rearrange("(k p) e -> p k e", p=P)),
                                     (br[:, :], d["br"].partition_broadcast(P)), (bo8[:, :], d["bo8"]),
                                     (cut[:, :], sum_t[2 * (HALF - 1)].partition_broadcast(P))):
                        sp.dma_start(to, name).then_inc(consts_in, 16)
                    with sp.Fori(0, NG) as g:
                        sp.wait_ge(added, FREE_ADDED + OUTS * (g + 1))
                        sp.dma_start(d["out"].rearrange("(i p) c -> p i c", p=P)[:, ts(g, G), :],
                                     total[:, :, :]).then_inc(stored, 16)
                    sp.wait_ge(stored, 16 * (NG + 1))

                @block.gpsimd
                def _(pool):
                    features = d["x"].rearrange("(i p) c -> p i c", p=P)
                    for p in range(NG):
                        if p >= 1:
                            pool.wait_ge(combined, p)
                        for i in range(G):
                            pool.indirect_dma_start(fin[:, i, :], None, sum_t,
                                                    bass.IndirectOffsetOnAxis(end_row[:, G * p + i:G * p + i + 1], 0),
                                                    bounds_check=EP - 1, oob_is_err=False).then_inc(fin_in, 16)
                        if p >= 1:
                            pool.wait_ge(added, FREE_ADDED + OUTS * (p - 1) + G)
                        pool.dma_start(x[:, :, :], features[:, G * p:G * (p + 1), :]).then_inc(x_in, 16)
                    pool.wait_ge(x_in, 16 * NG)

                @block.tensor
                def _(pe):
                    pe.sem_inc(out_formed, FREE_OUT)
                    pe.wait_ge(consts_in, 16 * 5)

                    def before(p):
                        def turn_h():
                            pe.wait_ge(combined, p + 1)
                            for n, tiles in enumerate(QUADS):
                                wait_free(pe, p, TURN_H + n)
                                for k, u in enumerate(range(tiles.start, tiles.stop)):
                                    ins = pe.matmul(bank_of(TURN_H + n)[0:HC, P * k:P * (k + 1)], h[:, u, :], identity[:, :],
                                                    start=True, stop=True)
                                ins.then_inc(in_bank, 1)

                        def project(uses):
                            def go():
                                wait_read(pe, p, TURN_H)
                                wait_read(pe, p, TURN_H + 1)
                                for n in uses:
                                    wait_free(pe, p, PROJECT + n)
                                    for k, u in enumerate(range(pairs(n).start, pairs(n).stop)):
                                        ins = pe.matmul(bank_of(PROJECT + n)[:, D * k:D * (k + 1)], hT[:, P * u:P * (u + 1)], wo[:, :],
                                                        start=True, stop=True)
                                    ins.then_inc(in_bank, 1)
                            return go

                        def turn_y(uses):
                            def go():
                                pe.wait_ge(y_ready, p + 1)
                                for n in uses:
                                    wait_free(pe, p, TURN_Y + n)
                                    for k, u in enumerate(range(pairs(n).start, pairs(n).stop)):
                                        for c in range(KC):
                                            at = 2 * P * c + P * k
                                            ins = pe.transpose(bank_of(TURN_Y + n)[:, at:at + P], y[:, u, P * c:P * (c + 1)], identity[:, :])
                                    ins.then_inc(in_bank, 1)
                            return go

                        return {(2, 0): turn_h, (2, 1): project((0, 1)), (3, 0): project((2, 3)),
                                (6, 1): turn_y((0, 1)), (7, 0): turn_y((2, 3))}

                    def product(out, first, last, *operands):
                        (a_hi, a_lo), (b_hi, b_lo) = operands
                        pe.matmul(out, a_hi, b_hi, start=first, stop=False)
                        pe.matmul(out, a_hi, b_lo, start=False, stop=False)
                        return pe.matmul(out, a_lo, b_hi, start=False, stop=last)

                    def experts(g, pieces):
                        def hidden(e, layer):
                            n0 = place[e, layer]
                            for m in range(LH):
                                for half in range(2):
                                    n, of = n0 + 2 * m + half, slice(HTOK * half, HTOK * (half + 1))
                                    pe.wait_ge(relued, 2 * (PER * g + n + 1))
                                    if layer == 1:
                                        pe.wait_ge(parted, FREE_PARTED + PER * g + place[e, 0] + 3 + half)
                                    for c in range(KC):
                                        hi, lo = (y_hi, y_lo) if layer == 0 else (hid_hi[0], hid_lo[0])
                                        w_at = slice(HID * c + P * m, HID * c + P * (m + 1))
                                        ins = product(psH[n % 4][:, 0:HTOK], c == 0, c == KC - 1,
                                                      (w_hi[:, EXPERTS * layer + e, w_at], w_lo[:, EXPERTS * layer + e, w_at]),
                                                      (hi[:, c, of], lo[:, c, of]))
                                    ins.then_inc(formed, 1)

                        def outputs(e):
                            pe.wait_ge(parted, FREE_PARTED + PER * g + place[e, 1] + 4)
                            for u in range(G):
                                n, of = G * e + u, slice(P * u, P * (u + 1))
                                pe.wait_ge(added, OUTS * g + n + 1)
                                for c in range(KC):
                                    w_at = slice(HID * c, HID * (c + 1))
                                    ins = product(psO[n % 2][:, 0:D], c == 0, c == KC - 1,
                                                  (hid_hi[1][:, c, of], hid_lo[1][:, c, of]),
                                                  (w_hi[:, EXPERTS * 2 + e, w_at], w_lo[:, EXPERTS * 2 + e, w_at]))
                                ins.then_inc(out_formed, 1)

                        def route():
                            wait_free(pe, g, ROUTE)
                            for u in range(G):
                                of = slice(P * u, P * (u + 1))
                                for c in range(KC):
                                    ins = product(bank_of(ROUTE)[:, EXPERTS * u:EXPERTS * (u + 1)], c == 0, c == KC - 1,
                                                  (y_hi[:, c, of], y_lo[:, c, of]), (wr_hi[:, c, :], wr_lo[:, c, :]))
                            ins.then_inc(in_bank, 1)

                        def turn_gate():
                            pe.wait_ge(gate_ready, g + 1)
                            for n, tiles in enumerate(QUADS):
                                wait_free(pe, g, TURN_GATE + n)
                                for k, u in enumerate(range(tiles.start, tiles.stop)):
                                    ins = pe.transpose(bank_of(TURN_GATE + n)[0:EXPERTS, P * k:P * (k + 1)], gate[:, u, :], identity[:, :])
                                ins.then_inc(in_bank, 1)

                        def biases(uses):
                            wait_read(pe, g, TURN_GATE)
                            wait_read(pe, g, TURN_GATE + 1)
                            for n in uses:
                                wait_free(pe, g, BIAS + n)
                                for k, u in enumerate(range(pairs(n).start, pairs(n).stop)):
                                    ins = pe.matmul(bank_of(BIAS + n)[:, D * k:D * (k + 1)], gT[:, P * u:P * (u + 1)], bo8[:, :],
                                                    start=True, stop=True)
                                ins.then_inc(in_bank, 1)

                        wait_read(pe, g, TURN_Y + 2)
                        wait_read(pe, g, TURN_Y + 3)
                        hidden(0, 0)
                        route()
                        for e in range(EXPERTS):
                            hidden(e, 1)
                            if e == 1:
                                biases((0, 1))
                            run(pieces, e, 0)
                            if e + 1 < EXPERTS:
                                hidden(e + 1, 0)
                            if e == 0:
                                turn_gate()
                            if e == 1:
                                biases((2, 3))
                            run(pieces, e, 1)
                            outputs(e)

                    pe.wait_ge(ones, 1)
                    pe.wait_ge(wr_split, 2)
                    all_groups(pe, before, experts)

                @block.scalar
                def _(act):
                    act.sem_inc(relued, FREE_RELUED)
                    act.wait_ge(bn_eps_set, 1)
                    act.wait_ge(bn_in, 16)
                    act.activation(scale[:, :, :], bn[:, :, 4, :], ACT.Sqrt, bias=bn_eps[:, 0:1]).then_inc(bn_rooted, 1)

                    def before(p):
                        def merge_weights():
                            act.wait_ge(weights_wanted, p + 1)
                            act.activation(wx[:, :, :, :].rearrange("p i m h -> p (i m h)"),
                                           wt[:, :, :, :].rearrange("p i m h -> p (i m h)"), ACT.Exp).then_inc(weights_ready, 1)

                        def take_h():
                            for n, tiles in enumerate(QUADS):
                                wait_in_bank(act, p, TURN_H + n)
                                act.activation(hT[0:HC, P * tiles.start:P * tiles.stop],
                                               bank_of(TURN_H + n)[0:HC, 0:P * (tiles.stop - tiles.start)],
                                               ACT.Copy).then_inc(bank_read[(TURN_H + n) % 2], 1)

                        def squash(uses):
                            def go():
                                for n in uses:
                                    wait_in_bank(act, p, PROJECT + n)
                                    tiles = pairs(n)
                                    act.activation(y[:, tiles, :], bank_of(PROJECT + n)[:, 0:D * (tiles.stop - tiles.start)]
                                                   .rearrange("p (u c) -> p u c", c=D), ACT.Sigmoid).then_inc(bank_read[(PROJECT + n) % 2], 1)
                            return go

                        def root():
                            act.wait_ge(aggregated, p + 1)
                            act.activation(rstd[:, :], mv[:, :, 1], ACT.Sqrt, bias=eps[:, 0:1]).then_inc(rooted, 1)

                        def high_y(uses):
                            def go():
                                for n in uses:
                                    wait_in_bank(act, p, TURN_Y + n)
                                    width = P * (pairs(n).stop - pairs(n).start)
                                    at = P * pairs(n).start
                                    act.activation(y_hi[:, :, at:at + width],
                                                   bank_of(TURN_Y + n)[:, :].rearrange("p (c n) -> p c n", c=KC)[:, :, 0:width],
                                                   ACT.Copy).then_inc(y_high, 1)
                            return go

                        return {(0, 1): merge_weights, (2, 0): take_h, (2, 1): squash((0, 1)), (3, 1): squash((2, 3)), (5, 1): root,
                                (6, 1): high_y((0, 1)), (7, 0): high_y((2, 3))}

                    def experts(g, pieces):
                        def hidden(e, layer):
                            for m in range(LH):
                                for half in range(2):
                                    n, of = place[e, layer] + 2 * m + half, slice(HTOK * half, HTOK * (half + 1))
                                    act.wait_ge(formed, PER * g + n + 1)
                                    act.wait_ge(parted, PER * g + n + 1)
                                    if layer == 1 and m == 0 and half == 0:
                                        act.wait_ge(out_formed, OUTS * g + G * e + G)
                                    at = LH * e + m
                                    for to in (full[:, n % 4, :], hid_hi[layer][:, m, of]):
                                        act.activation(to, psH[n % 4][:, 0:HTOK], ACT.Relu, bias=offset[:, layer, at:at + 1],
                                                       scale=scale[:, layer, at:at + 1]).then_inc(relued, 1)

                        def exponentials():
                            act.wait_ge(gap_ready, g + 1)
                            act.activation(gate[:, :, :].rearrange("p i e -> p (i e)"),
                                           gate[:, :, :].rearrange("p i e -> p (i e)"), ACT.Exp).then_inc(exp_ready, 1)

                        def take_gate():
                            for n, tiles in enumerate(QUADS):
                                wait_in_bank(act, g, TURN_GATE + n)
                                act.activation(gT[:, P * tiles.start:P * tiles.stop],
                                               bank_of(TURN_GATE + n)[0:EXPERTS, 0:P * (tiles.stop - tiles.start)],
                                               ACT.Copy).then_inc(bank_read[(TURN_GATE + n) % 2], 1)

                        hidden(0, 0)
                        exponentials()
                        for e in range(EXPERTS):
                            hidden(e, 1)
                            run(pieces, e, 0)
                            if e + 1 < EXPERTS:
                                hidden(e + 1, 0)
                            if e == 0:
                                take_gate()
                            run(pieces, e, 1)

                    act.wait_ge(folded, 1)
                    all_groups(act, before, experts)

                @block.vector
                def _(dve):
                    dve.sem_inc(parted, FREE_PARTED)
                    dve.sem_inc(added, FREE_ADDED)
                    dve.memset(hT[HC:HC + 1, :], 1.0).then_inc(ones, 1)
                    dve.memset(bn_eps[:, :], BN_EPS).then_inc(bn_eps_set, 1)
                    step = Steps(dve, bn_step)
                    dve.wait_ge(bn_rooted, 1)
                    step(dve.reciprocal(scale[:, :, :], scale[:, :, :]))
                    step(dve.tensor_tensor(scale[:, :, :], scale[:, :, :], bn[:, :, 1, :], ALU.mult))
                    step(dve.tensor_tensor(offset[:, :, :], bn[:, :, 0, :], bn[:, :, 3, :], ALU.subtract))
                    step(dve.tensor_tensor(offset[:, :, :], offset[:, :, :], scale[:, :, :], ALU.mult))
                    step(dve.tensor_tensor(offset[:, :, :], offset[:, :, :], bn[:, :, 2, :], ALU.add))
                    dve.sem_inc(folded, 1)
                    dve.wait_ge(consts_in, 16 * 5)
                    dve.tensor_copy(wr_hi[:, :, :], wr[:, :, :]).then_inc(wr_split, 1)
                    dve.wait_ge(wr_split, 1)
                    dve.tensor_tensor(wr_lo[:, :, :], wr[:, :, :], wr_hi[:, :, :].bitcast(F32), ALU.subtract).then_inc(wr_split, 1)

                    all4 = [P, G, HEADS]
                    all64 = [P, G, HEADS, CH]
                    every = [P, G, EXPERTS]
                    COMB, NORM, SMAX = 14, 8, 5

                    def by_head(a):
                        return a.rearrange("p i (h c) -> p i h c", c=CH)

                    def before(p):
                        of = ts(p, G)

                        def distances():
                            step = Steps(dve, comb, COMB * p)
                            dve.wait_ge(fin_in, 16 * G * (p + 1))
                            step(dve.tensor_tensor(mb[:, :, :], span_bias[:, of].unsqueeze(2).to_broadcast(all4),
                                                   cut[:, MAX:MAX + HEADS].unsqueeze(1).to_broadcast(all4), ALU.add))
                            step(dve.tensor_tensor(mm[:, :, :], mb[:, :, :], fin[:, :, MAX:MAX + HEADS], ALU.max))
                            step(dve.tensor_tensor(wt[:, :, 0, :], fin[:, :, MAX:MAX + HEADS], mm[:, :, :], ALU.subtract))
                            step(dve.tensor_tensor(wt[:, :, 1, :], mb[:, :, :], mm[:, :, :], ALU.subtract))
                            dve.sem_inc(weights_wanted, 1)

                        def sum_parts():
                            step = Steps(dve, comb, COMB * p + 4)
                            dve.wait_ge(weights_ready, p + 1)
                            step(dve.tensor_tensor(den[:, :, :], fin[:, :, DEN:DEN + HEADS], wx[:, :, 0, :], ALU.mult))
                            step(dve.tensor_tensor(part[:, :, :], cut[:, DEN:DEN + HEADS].unsqueeze(1).to_broadcast(all4),
                                                   wx[:, :, 1, :], ALU.mult))
                            step(dve.scalar_tensor_tensor(den[:, :, :].rearrange("p i h -> p (i h)"), den[:, :, :].rearrange("p i h -> p (i h)"),
                                                          DEN_EPS, part[:, :, :].rearrange("p i h -> p (i h)"), ALU.add, ALU.add))
                            step(dve.reciprocal(den[:, :, :], den[:, :, :]))
                            step(dve.tensor_tensor(den[:, :, :], den[:, :, :], present[:, of].unsqueeze(2).to_broadcast(all4), ALU.mult))
                            step(dve.tensor_tensor(wx[:, :, :, :], wx[:, :, :, :], den[:, :, :].unsqueeze(2).to_broadcast([P, G, 2, HEADS]), ALU.mult))

                            step(dve.tensor_tensor(by_head(h[:, :, :]), by_head(fin[:, :, 0:HC]),
                                                   wx[:, :, 0, :].unsqueeze(3).to_broadcast(all64), ALU.mult))
                            step(dve.tensor_tensor(by_head(ov[:, :, :]), wx[:, :, 1, :].unsqueeze(3).to_broadcast(all64),
                                                   cut[:, 0:HC].rearrange("p (h c) -> p h c", c=CH).unsqueeze(1).to_broadcast(all64), ALU.mult))

                        def finish():
                            step = Steps(dve, comb, COMB * p + 12)
                            step(dve.tensor_tensor(h[:, :, :], h[:, :, :], ov[:, :, :], ALU.add))
                            step(dve.tensor_tensor(ov[:, :, :], h[:, :, :], skip[:, of, :], ALU.add))
                            dve.tensor_scalar(h[:, :, :], ov[:, :, :], 0.0, None, ALU.max).then_inc(combined, 1)

                        def add_x(uses):
                            def go():
                                if uses[0] == 0:
                                    dve.wait_ge(x_in, 16 * p + 16)
                                tiles = slice(pairs(uses[0]).start, pairs(uses[-1]).stop)
                                for n in uses:
                                    wait_read(dve, p, PROJECT + n)
                                dve.tensor_tensor(x[:, tiles, :], x[:, tiles, :], y[:, tiles, :], ALU.add).then_inc(residual, 1)
                            return go

                        def statistics():
                            dve.wait_ge(residual, 2 * p + 2)
                            for u in range(G):
                                ins = dve.bn_stats(stat[:, u, :], x[:, u, :])
                            ins.then_inc(stats_done, 1)

                        def moments():
                            dve.wait_ge(stats_done, p + 1)
                            layer_norm_moments(Steps(dve, norm, NORM * p), mv[:, :, 0], mv[:, :, 1], stat)
                            dve.sem_inc(aggregated, 1)

                        def normalise():
                            dve.wait_ge(rooted, p + 1)
                            Steps(dve, norm, NORM * p + 7)(dve.reciprocal(rstd[:, :], rstd[:, :]))
                            for u in range(G):
                                ins = dve.tensor_scalar(y[:, u, :], x[:, u, :], mv[:, u, 0:1], rstd[:, u:u + 1], ALU.subtract, ALU.mult)
                            ins.then_inc(y_ready, 1)

                        def low_y(uses):
                            def go():
                                for n in uses:
                                    dve.wait_ge(y_high, 4 * p + n + 1)
                                    width = P * (pairs(n).stop - pairs(n).start)
                                    at = P * pairs(n).start
                                    dve.tensor_tensor(y_lo[:, :, at:at + width],
                                                      bank_of(TURN_Y + n)[:, :].rearrange("p (c n) -> p c n", c=KC)[:, :, 0:width],
                                                      y_hi[:, :, at:at + width].bitcast(F32), ALU.subtract).then_inc(bank_read[(TURN_Y + n) % 2], 1)
                            return go

                        return {(0, 1): lambda: (distances(), sum_parts()), (1, 0): finish,
                                (3, 0): add_x((0, 1)), (4, 0): add_x((2, 3)), (4, 1): statistics, (5, 0): moments,
                                (6, 0): normalise, (6, 1): low_y((0, 1)), (7, 0): low_y((2, 3))}

                    def experts(g, pieces):
                        def low_parts(e, layer):
                            for m in range(LH):
                                for half in range(2):
                                    n, of = place[e, layer] + 2 * m + half, slice(HTOK * half, HTOK * (half + 1))
                                    dve.wait_ge(relued, FREE_RELUED + 2 * (PER * g + n + 1))
                                    dve.tensor_tensor(hid_lo[layer][:, m, of], full[:, n % 4, :], hid_hi[layer][:, m, of].bitcast(F32),
                                                      ALU.subtract).then_inc(parted, 1)

                        def score():
                            step = Steps(dve, smax, SMAX * g)
                            dve.wait_ge(added, FREE_ADDED + OUTS * g)
                            wait_in_bank(dve, g, ROUTE)
                            step(dve.tensor_tensor(gate[:, :, :], bank_of(ROUTE)[:, 0:G * EXPERTS].rearrange("p (u e) -> p u e", e=EXPERTS),
                                                   br[:, :].unsqueeze(1).to_broadcast(every), ALU.add))
                            dve.sem_inc(bank_read[ROUTE % 2], 1)
                            step(dve.tensor_reduce(red[:, :], gate[:, :, :], AX.X, ALU.max))
                            step(dve.tensor_tensor(gate[:, :, :], gate[:, :, :], red[:, :].unsqueeze(2).to_broadcast(every), ALU.subtract))
                            dve.sem_inc(gap_ready, 1)

                        def weigh():
                            step = Steps(dve, smax, SMAX * g + 3)
                            dve.wait_ge(exp_ready, g + 1)
                            step(dve.tensor_reduce(red[:, :], gate[:, :, :], AX.X, ALU.add))
                            step(dve.reciprocal(red[:, :], red[:, :]))
                            dve.tensor_tensor(gate[:, :, :], gate[:, :, :], red[:, :].unsqueeze(2).to_broadcast(every), ALU.mult).then_inc(gate_ready, 1)

                        def add_biases(e, uses):
                            dve.wait_ge(added, FREE_ADDED + OUTS * g + G * e)
                            for n in uses:
                                tiles = pairs(n)
                                wait_in_bank(dve, g, BIAS + n)
                                dve.tensor_tensor(total[:, tiles, :], total[:, tiles, :],
                                                  bank_of(BIAS + n)[:, 0:(tiles.stop - tiles.start) * D].rearrange("p (u c) -> p u c", c=D),
                                                  ALU.add).then_inc(bias_added, 1)
                            dve.wait_ge(bias_added, 4 * g + uses[-1] + 1)
                            for n in uses:
                                dve.sem_inc(bank_read[(BIAS + n) % 2], 1)

                        def add_outputs(e):
                            if e == 0:
                                dve.wait_ge(stored, 16 * g + 16)
                                dve.wait_ge(gate_ready, g + 1)
                            for u in range(G):
                                n = G * e + u
                                so_far = x if e == 0 else total
                                dve.wait_ge(out_formed, FREE_OUT + OUTS * g + n + 1)
                                if e >= 1:
                                    dve.wait_ge(added, FREE_ADDED + OUTS * g + n - G + 1)
                                dve.scalar_tensor_tensor(total[:, u, :], psO[n % 2][:, 0:D], gate[:, u, e:e + 1], so_far[:, u, :],
                                                         ALU.mult, ALU.add).then_inc(added, 1)

                        low_parts(0, 0)
                        score()
                        for e in range(EXPERTS):
                            low_parts(e, 1)
                            if e == 0:
                                weigh()
                            if e == 1:
                                add_biases(1, (0, 1))
                            run(pieces, e, 0)
                            if e + 1 < EXPERTS:
                                low_parts(e + 1, 0)
                            add_outputs(e)
                            if e == 1:
                                add_biases(2, (2, 3))
                            run(pieces, e, 1)

                    all_groups(dve, before, experts)

        edge_phase(0)
        node_phase()
        first.close()
        pieces = [P, len(EXPERT_LAYERS) * EXPERTS, KC * HID]
        w_hi = whole.enter_context(nc.sbuf_tensor("expert_w_hi", pieces, F32R))
        w_lo = whole.enter_context(nc.sbuf_tensor("expert_w_lo", pieces, F32R))
        edge_phase(1)
        expert_phase()


def kernel(**inputs):
    import concourse.bacc as bacc
    from concourse.bass_utils import run_bass_kernel_spmd

    a = {k: np.asarray(v) for k, v in inputs.items()}
    g, f = "L0_gnn_", "L0_ffn_"

    def side_by_side(kind, n):
        q, k, v, skip = (a[f"{g}{kind}{z}{n}"].T for z in "qkvs")
        pairs = np.stack([k, v], axis=-1).reshape(*k.shape[:-1], 2 * HC)
        return np.ascontiguousarray(np.concatenate([q, pairs, skip], axis=-1))

    x = np.zeros((NP, D), np.float32)
    x[:N] = a["x"]
    src = np.zeros(EP, np.int32)
    src[:E] = a["src"]
    dst = np.full(EP, N, np.int32)
    dst[:E] = a["dst"]
    arrays = {
        "x": x,
        "src": np.ascontiguousarray(src.reshape(STREAMS, BLOCKS, TPB, P).transpose(1, 3, 2, 0).reshape(BLOCKS, P, TPB * STREAMS)),
        "dst": dst,
        "prev": np.concatenate([np.full(1, -1, np.int32), dst[:-1]]),
        "samples": np.ascontiguousarray(dst[:E:SCOLS]),
        "edge_rows": dst[:E].reshape(SROWS, SCOLS).copy(),
        "cut": dst[HALF:HALF + 16].reshape(16, 1).copy(),
        "proj1_w": side_by_side("W", 1), "proj1_b": side_by_side("b", 1),
        "proj2_w": side_by_side("W", 2), "proj2_b": side_by_side("b", 2),
        "wo_bo": np.concatenate([a[g + "Wo"].T, a[g + "bo"][None]]),
        "wr": a[f + "Wr"], "br": a[f + "br"],
        "expert_w": np.ascontiguousarray(np.stack([a[f + n] for n in EXPERT_LAYERS]).reshape(-1, KC, P, HID)
                                         .transpose(0, 2, 1, 3).reshape(-1, P, KC * HID)),
        "bo8": a[f + "bo"],
        "bn": np.ascontiguousarray(np.stack([[a[f"{f}{k}{n}"] for k in ("b", "g", "be", "m", "v")] for n in (1, 2)])
                                   .reshape(2, 5, EXPERTS * HID // P, P).transpose(3, 0, 1, 2)),
    }
    nc = bacc.Bacc("TRN2", target_bir_lowering=False, num_devices=1)
    d, feed = {}, {}
    for name, v in arrays.items():
        d[name] = nc.dram_tensor(f"in_{name}", v.shape, mybir.dt.from_np(v.dtype), kind="ExternalInput").ap()
        feed[f"in_{name}"] = v
    d["out"] = nc.dram_tensor("out", (NP, D), F32, kind="ExternalOutput").ap()
    build(nc, d)
    r = run_bass_kernel_spmd(nc, [feed], core_ids=[0])
    return r.results[0]["out"][:N]
```

```python
from contextlib import ExitStack

import numpy as np

import concourse.bass as bass
from concourse import mybir

F32 = mybir.dt.float32
F32R = mybir.dt.float32r
BF16 = mybir.dt.bfloat16
I32 = mybir.dt.int32
ALU = mybir.AluOpType
ACT = mybir.ActivationFunctionType
AX = mybir.AxisListType
ts = bass.ts

P = 128
N, E, D = 6250, 106250, 256
HEADS, CH = 4, 16
HC = HEADS * CH
EXPERTS, HID = 8, 256
EXPERT_LAYERS = ("W1", "W2", "Wo")
KC = D // P
LN_EPS, BN_EPS, DEN_EPS = 1e-5, 1e-3, 1e-16

NT = -(-N // P)
NP = NT * P
GROUP = 7
NG = NT // GROUP
assert NG * GROUP == NT and NG % 2 == 1

STREAMS = 2
STEP = 512
TPB = STEP // P
UNROLL = 4
BLOCKS = -(-E // (STREAMS * STEP * UNROLL)) * UNROLL
STEPS = BLOCKS // UNROLL
HALF = BLOCKS * STEP
EP = STREAMS * HALF
ROW = HC + 2 * HEADS
DEN, MAX = HC, HC + HEADS

SCOLS = 128
SROWS = -(-E // SCOLS)
NEG = -3.0e38
SKIP = float(1 << 22)

Q0, K0, S0 = 0, HC, 3 * HC
PROJ = 4 * HC
HTOK = GROUP * P // 2
GTOK = GROUP * P
assert STEPS - 2 == len(EXPERT_LAYERS) * EXPERTS


def each_group(eng, body):
    body(0)
    with eng.Fori(1, NG) as g:
        body(g)


def wait_past(eng, done, count):
    if not isinstance(count, int) or count >= 1:
        eng.wait_ge(done, count)


class Steps:

    def __init__(self, eng, done, at=0):
        self.eng, self.done, self.at = eng, done, at

    def __call__(self, instruction):
        self.at = self.at + 1
        instruction.then_inc(self.done, 1)
        self.eng.wait_ge(self.done, self.at)


def build(nc, d):
    kv_t = nc.dram_tensor("kv_table", [NP, 2 * HC], F32, kind="Internal").ap()
    q_t = nc.dram_tensor("q_table", [NP, HC], F32, kind="Internal").ap()
    qz_t = nc.dram_tensor("q_at_starts", [EP, HC], F32, kind="Internal").ap()
    sum_t = nc.dram_tensor("running_sums", [EP, ROW], F32, kind="Internal").ap()
    mask_t = nc.dram_tensor("masks", [STREAMS, BLOCKS, 2 * STEP], BF16, kind="Internal").ap()
    qz_blocks = qz_t.rearrange("(b j p s) c -> b p j (s c)", j=TPB, p=P, s=STREAMS)
    sum_blocks = sum_t.rearrange("(b j p s) c -> b p j (s c)", j=TPB, p=P, s=STREAMS)
    kv_nodes = kv_t.rearrange("(i p) c -> p i c", p=P)
    q_nodes = q_t.rearrange("(i p) c -> p i c", p=P)

    with ExitStack() as whole:
        def keep(name, shape, dt=F32):
            return whole.enter_context(nc.sbuf_tensor(name, shape, dt))

        first = whole.enter_context(ExitStack())
        identity = keep("identity", [P, P])
        head_sum = keep("head_sum", [P, P])
        pick = keep("pick", [P, STREAMS * HEADS])
        start_row = keep("start_row", [P, NT], I32)
        end_row = keep("end_row", [P, NT], I32)
        span_bias = keep("span_bias", [P, NT])
        present = keep("present", [P, NT])
        cut_ix = keep("cut_ix", [16, 1], I32)
        cut_q = keep("cut_q", [16, HC])
        eps = keep("eps", [P, 1])
        skip = keep("skip", [P, NT, HC])
        proj = first.enter_context(nc.sbuf_tensor("proj", [P, NT, PROJ], F32))

        def scatter_q(pool, done, g):
            for i in range(GROUP * g, GROUP * (g + 1)):
                pool.indirect_dma_start(qz_t, bass.IndirectOffsetOnAxis(start_row[:, i:i + 1], 0),
                                        proj[:, i, Q0:Q0 + HC], None,
                                        bounds_check=EP - 1, oob_is_err=False).then_inc(done, 16)

        def scatter_cut(pool, done, stored, got, cut_done):
            pool.wait_ge(stored, 16 * 2 * NG)
            pool.indirect_dma_start(cut_q[:, :], None, q_t, bass.IndirectOffsetOnAxis(cut_ix[:, :], 0),
                                    bounds_check=NP - 1, oob_is_err=False).then_inc(got, 16)
            pool.wait_ge(got, 16)
            pool.wait_ge(done, 16 * NT)
            pool.dma_start(qz_t[1:2, :], cut_q[0:1, :]).then_inc(cut_done, 16)
            pool.wait_ge(cut_done, 16)

        def store_tables(sp, projected, per_group, stored):
            with sp.Fori(0, NG) as g:
                sp.wait_ge(projected, per_group * g + per_group)
                sp.dma_start(kv_nodes[:, ts(g, GROUP), :], proj[:, ts(g, GROUP), K0:S0]).then_inc(stored, 16)
                sp.dma_start(q_nodes[:, ts(g, GROUP), :], proj[:, ts(g, GROUP), Q0:K0]).then_inc(stored, 16)
            sp.wait_ge(stored, 16 * 2 * NG)

        def layer_norm_moments(step, mean, var, stat):
            step(step.eng.tensor_tensor(mean, stat[:, :, 1], stat[:, :, 4], ALU.subtract))
            step(step.eng.tensor_tensor(var, mean, mean, ALU.mult))
            step(step.eng.scalar_tensor_tensor(var, var, D / 4.0, stat[:, :, 2], ALU.mult, ALU.add))
            step(step.eng.tensor_tensor(var, var, stat[:, :, 5], ALU.add))
            step(step.eng.tensor_scalar(var, var, 1.0 / D, None, ALU.mult))
            step(step.eng.tensor_tensor(mean, stat[:, :, 1], stat[:, :, 4], ALU.add))
            step(step.eng.tensor_scalar(mean, mean, 0.5, None, ALU.mult))

        with ExitStack() as phase:
            def sb(name, shape, dt=F32):
                return phase.enter_context(nc.sbuf_tensor(name, shape, dt))

            def pb(name):
                return phase.enter_context(nc.psum_tensor(name, [P, 512], F32))

            def sem(name):
                return whole.enter_context(nc.semaphore(name))

            FILLS = 16
            fill = qz_t.rearrange("(p r) c -> p (r c)", p=P).rearrange("p (m k n) -> m p k n", m=FILLS, k=32 // FILLS)
            x_sb = sb("x_sb", [P, NT, D])
            mv = sb("mv", [P, NT, 2])
            rstd = sb("rstd", [P, NT])
            stat = sb("stat", [P, NT, 6])
            node_i = sb("node_i", [P, NT], I32)
            node = sb("node", [P, NT])
            samples_i = sb("samples_i", [P, SROWS], I32)
            samples = sb("samples", [P, SROWS])
            signs = sb("signs", [P, GROUP, SROWS], BF16)
            below = sb("below", [P, GROUP, SCOLS], BF16)
            half_less = sb("half_less", [P, NT])
            balance = sb("balance", [P, NT])
            found = sb("found", [P, NT])
            chunk_no = sb("chunk_no", [P, NT])
            chunk_ix = sb("chunk_ix", [P, NT], I32)
            chunk = sb("chunk", [P, NT, SCOLS], I32)
            start = sb("start", [P, NT + 1])
            nxt = sb("nxt", [P, NT])
            t0 = sb("t0", [P, NT])
            t1 = sb("t1", [P, NT])
            shift = sb("shift", [P, P])
            wrap = sb("wrap", [P, P])
            zeros = sb("zeros", [P, EP * HC // P // 32])
            dst_b = sb("dst_b", [BLOCKS, STREAMS, STEP], I32)
            prev_b = sb("prev_b", [BLOCKS, STREAMS, STEP], I32)
            mask_b = sb("mask_b", [BLOCKS, STREAMS, 2, STEP], BF16)
            w1t = sb("w1t", [P, KC, PROJ])
            b1 = sb("b1", [P, PROJ])
            mean_less = sb("mean_less", [P, NT])
            xh = sb("xh", [P, 2, D])
            xT = sb("xT", [P, 2, KC, P])
            psT = [pb(f"psT{i}") for i in range(2)]
            psP = [pb(f"psP{i}") for i in range(4)]
            psN = pb("psN")

            x_in, w_in, edges_in, samples_in, cut_in = (sem(n) for n in (
                "x_in", "w_in", "edges_in", "samples_in", "cut_in"))
            zeroed, constants, numbered, made = (sem(n) for n in ("zeroed", "constants", "numbered", "made"))
            filled = [sem(f"filled{n}") for n in range(4)]
            chunk_in = [sem(f"chunk_in{g}") for g in range(NG)]
            pool_step, started, shifted = (sem(n) for n in (
                "pool_step", "started", "shifted"))
            dve_step, stats_done, aggregated, rooted, eps_set = (sem(n) for n in (
                "dve_step", "stats_done", "aggregated", "rooted", "eps_set"))
            rows_ready, masks_made, masks_out = sem("rows_ready"), sem("masks_made"), sem("masks_out")
            xhat_ready, turned, xT_ready, product, projected = (sem(n) for n in (
                "xhat_ready", "turned", "xT_ready", "product", "projected"))
            stored, scattered, cut_got, cut_done = (sem(n) for n in ("stored", "scattered", "cut_got", "cut_done"))
            samples_ready, counted, chunks, normed, row_step = (sem(n) for n in (
                "samples_ready", "counted", "chunks", "normed", "row_step"))
            block = phase.enter_context(nc.Block())

            @block.sync
            def _(sp):
                sp.dma_start(samples_i[:, :], d["samples"].partition_broadcast(P)).then_inc(samples_in, 16)
                sp.dma_start(dst_b[:, :, :], d["dst"].rearrange("(s b c) -> b s c", s=STREAMS, c=STEP)).then_inc(edges_in, 16)
                sp.dma_start(prev_b[:, :, :], d["prev"].rearrange("(s b c) -> b s c", s=STREAMS, c=STEP)).then_inc(edges_in, 16)
                sp.dma_start(x_sb[:, :, :], d["x"].rearrange("(i p) c -> p i c", p=P)).then_inc(x_in, 16)
                sp.dma_start(w1t[:, :, :], d["proj1_w"].rearrange("(k p) c -> p k c", p=P)).then_inc(w_in, 16)
                sp.dma_start(b1[:, :], d["proj1_b"].partition_broadcast(P)).then_inc(w_in, 16)
                sp.dma_start(cut_ix[:, :], d["cut"]).then_inc(cut_in, 16)
                sp.wait_ge(zeroed, 1)
                for m in range(FILLS):
                    if m >= len(filled):
                        sp.wait_ge(filled[m % len(filled)], 16 * (m // len(filled)))
                    if m == 2:
                        sp.wait_ge(masks_made, 1)
                        for s in range(STREAMS):
                            sp.dma_start(mask_t[s], mask_b[:, s, :, :].rearrange("b m c -> b (m c)")).then_inc(masks_out, 16)
                    sp.dma_start(fill[m], zeros[:, :].unsqueeze(1).to_broadcast([P, 32 // FILLS, EP * HC // P // 32])).then_inc(filled[m % len(filled)], 16)
                store_tables(sp, projected, GROUP, stored)
                sp.wait_ge(masks_out, 16 * STREAMS)

            @block.gpsimd
            def _(pool):
                pool.iota(node_i[:, :], pattern=[[P, NT]], base=0, channel_multiplier=1).then_inc(numbered, 1)
                pool.memset(zeros[:, :], 0.0).then_inc(zeroed, 1)
                for m, v in ((identity, 0.0), (shift, 0.0), (wrap, 0.0), (head_sum, CH ** -0.5), (pick, 0.0)):
                    pool.memset(m[:, :], v).then_inc(made, 1)
                pool.wait_ge(made, 5)
                pool.affine_select(out=identity[:, :], in_=identity[:, :], compare_op=ALU.not_equal, fill=1.0,
                                   base=0, pattern=[[-1, P]], channel_multiplier=1).then_inc(constants, 1)
                pool.affine_select(out=shift[:, :], in_=shift[:, :], compare_op=ALU.not_equal, fill=1.0,
                                   base=-1, pattern=[[-1, P]], channel_multiplier=1).then_inc(constants, 1)
                pool.memset(wrap[0:1, P - 1:P], 1.0).then_inc(constants, 1)
                pool.affine_select(out=pick[:, :], in_=pick[:, :], compare_op=ALU.not_equal, fill=1.0,
                                   base=0, pattern=[[-CH, STREAMS * HEADS]], channel_multiplier=1).then_inc(constants, 1)
                blocks = head_sum[:, :].rearrange("p (j c) -> p j c", c=CH)
                pool.affine_select(out=blocks, in_=blocks, compare_op=ALU.is_ge, fill=0.0, base=0,
                                   pattern=[[-CH, P // CH], [0, CH]], channel_multiplier=1).then_inc(made, 1)
                pool.wait_ge(made, 6)
                pool.affine_select(out=blocks, in_=blocks, compare_op=ALU.is_ge, fill=0.0, base=CH - 1,
                                   pattern=[[CH, P // CH], [0, CH]], channel_multiplier=-1).then_inc(constants, 1)
                step = Steps(pool, pool_step)
                for g in range(NG):
                    of = slice(GROUP * g, GROUP * (g + 1))
                    pool.wait_ge(counted, GROUP * (g + 1))
                    step(pool.tensor_scalar(chunk_no[:, of], balance[:, of], 0.5, SROWS / 2.0 - 1, ALU.mult, ALU.add))
                    step(pool.tensor_scalar(chunk_no[:, of], chunk_no[:, of], 0.0, None, ALU.max))
                    step(pool.tensor_copy(chunk_ix[:, of], chunk_no[:, of]))
                    for i in range(GROUP * g, GROUP * (g + 1)):
                        pool.indirect_dma_start(chunk[:, i, :], None, d["edge_rows"],
                                                bass.IndirectOffsetOnAxis(chunk_ix[:, i:i + 1], 0),
                                                bounds_check=SROWS - 1, oob_is_err=False).then_inc(chunk_in[g], 16)
                for g in range(NG):
                    pool.wait_ge(chunk_in[g], 16 * GROUP)
                    pool.sem_inc(chunks, 1)
                pool.wait_ge(rows_ready, 1)
                for fill_part in filled:
                    pool.wait_ge(fill_part, 16 * FILLS // len(filled))
                for g in range(NG):
                    pool.wait_ge(projected, GROUP * (g + 1))
                    scatter_q(pool, scattered, g)
                pool.wait_ge(cut_in, 16)
                scatter_cut(pool, scattered, stored, cut_got, cut_done)

            @block.scalar
            def _(act):
                act.wait_ge(samples_ready, 1)
                def group(g):
                    for u in range(GROUP):
                        t = GROUP * g + u
                        wait_past(act, counted, t - GROUP + 1)
                        act.activation(signs[:, u, :], samples[:, :], ACT.Sign, bias=half_less[:, ts(t, 1)], scale=-1.0,
                                       accum_out=balance[:, ts(t, 1)]).then_inc(counted, 1)
                each_group(act, group)
                act.wait_ge(eps_set, 1)
                act.wait_ge(aggregated, 1)
                act.activation(rstd[:, :], mv[:, :, 1], ACT.Sqrt, bias=eps[:, 0:1]).then_inc(rooted, 1)
                act.wait_ge(normed, 1)
                def group(g):
                    for k in range(GROUP + 1):
                        if k < GROUP:
                            t = GROUP * g + k
                            wait_past(act, turned, t if k == 0 else t - 1)
                            act.activation(xh[:, k % 2, :], x_sb[:, t, :], ACT.Identity, bias=mean_less[:, ts(t, 1)],
                                           scale=rstd[:, ts(t, 1)]).then_inc(xhat_ready, 1)
                        if k >= 1:
                            u, t = k - 1, GROUP * g + k - 1
                            act.wait_ge(turned, t + 1)
                            wait_past(act, product, t if u == 0 else t - 1)
                            act.activation(xT[:, u % 2, :, :].rearrange("p k n -> p (k n)"), psT[u % 2][:, 0:D],
                                           ACT.Copy).then_inc(xT_ready, 1)
                each_group(act, group)

            @block.tensor
            def _(pe):
                pe.wait_ge(constants, 5)
                pe.wait_ge(w_in, 32)
                def group(g):
                    for k in range(GROUP + 1):
                        if k < GROUP:
                            t = GROUP * g + k
                            pe.wait_ge(xhat_ready, t + 1)
                            pe.wait_ge(xT_ready, t if k == 0 else t - 1)
                            for c in range(KC):
                                ins = pe.transpose(psT[k % 2][:, P * c:P * (c + 1)], xh[:, k % 2, P * c:P * (c + 1)], identity[:, :])
                            ins.then_inc(turned, 1)
                        if k >= 1:
                            u, t = k - 1, GROUP * g + k - 1
                            pe.wait_ge(xT_ready, t + 1)
                            before = 4 if u >= 4 else GROUP - 4 if u < 3 else GROUP
                            wait_past(pe, projected, t - before + 1)
                            for c in range(KC):
                                ins = pe.matmul(psP[u % 4][:, 0:PROJ], xT[:, u % 2, c, :], w1t[:, c, :],
                                                start=(c == 0), stop=(c == KC - 1))
                            ins.then_inc(product, 1)

                group(0)
                with pe.Fori(1, NG // 2 + 1) as g:
                    group(g)
                pe.wait_ge(started, 1)
                pe.matmul(psN[:, 0:NT], shift[:, :], start[:, 0:NT], start=True, stop=False)
                pe.matmul(psN[:, 0:NT], wrap[:, :], start[:, 1:NT + 1], start=False, stop=True).then_inc(shifted, 1)
                with pe.Fori(NG // 2 + 1, NG) as g:
                    group(g)

            @block.vector
            def _(dve):
                dve.memset(eps[:, :], LN_EPS).then_inc(eps_set, 1)
                step = Steps(dve, dve_step)
                dve.wait_ge(numbered, 1)
                step(dve.tensor_copy(node[:, :], node_i[:, :]))
                dve.wait_ge(samples_in, 16)
                step(dve.tensor_copy(samples[:, :], samples_i[:, :]))
                step(dve.tensor_scalar(half_less[:, :], node[:, :], -0.5, None, ALU.add))
                dve.sem_inc(samples_ready, 1)
                dve.wait_ge(edges_in, 32)
                step(dve.tensor_tensor(mask_b[:, :, 0, :], dst_b[:, :, :], prev_b[:, :, :], ALU.is_equal))
                step(dve.memset(mask_b[0:1, 1, 0, 0:1], 0.0))
                step(dve.tensor_scalar(mask_b[:, :, 1, :], mask_b[:, :, 0, :], -NEG, NEG, ALU.mult, ALU.add))
                dve.sem_inc(masks_made, 1)
                dve.wait_ge(x_in, 16)
                with dve.Fori(0, NG) as g:
                    for u in range(GROUP):
                        ins = dve.bn_stats(stat[:, ts(GROUP * g + u, 1), :].rearrange("p i c -> p (i c)"), x_sb[:, GROUP * g + u, :])
                    ins.then_inc(stats_done, 1)
                dve.wait_ge(stats_done, NG)
                step_norm = Steps(dve, stats_done, NG)
                layer_norm_moments(step_norm, mv[:, :, 0], mv[:, :, 1], stat)
                dve.sem_inc(aggregated, 1)
                dve.wait_ge(rooted, 1)
                step_norm(dve.reciprocal(rstd[:, :], rstd[:, :]))
                step_norm(dve.scalar_tensor_tensor(mean_less[:, :], mv[:, :, 0], -1.0, rstd[:, :], ALU.mult, ALU.mult))
                dve.sem_inc(normed, 1)
                dve.wait_ge(w_in, 32)

                def add_bias(g):
                    for k in range(GROUP):
                        t = GROUP * g + k
                        dve.wait_ge(product, t + 1)
                        dve.tensor_tensor(proj[:, t, :], psP[k % 4][:, 0:PROJ], b1[:, :], ALU.add).then_inc(projected, 1)

                def search(g):
                    of = ts(g, GROUP)
                    step_row = Steps(dve, row_step, 2 * g)
                    dve.wait_ge(chunks, g + 1)
                    step_row(dve.tensor_tensor(below[:, :, :], chunk[:, of, :],
                                               node[:, of].unsqueeze(2).to_broadcast([P, GROUP, SCOLS]), ALU.is_lt))
                    step_row(dve.tensor_reduce(found[:, of], below[:, :, :], AX.X, ALU.add))

                with dve.Fori(0, NG // 2) as g:
                    add_bias(g)
                    search(2 * g)
                    search(2 * g + 1)
                add_bias(NG // 2)
                search(NG - 1)
                step(dve.memset(start[:, NT:NT + 1], float(E)))
                step(dve.scalar_tensor_tensor(start[:, 0:NT], chunk_no[:, :], float(SCOLS), found[:, :], ALU.mult, ALU.add))
                dve.sem_inc(started, 1)
                dve.wait_ge(shifted, 1)
                step(dve.tensor_copy(nxt[:, :], psN[:, 0:NT]))
                first = start[:, 0:NT]
                step(dve.tensor_tensor(present[:, :], nxt[:, :], first, ALU.is_gt))
                step(dve.tensor_scalar(t0[:, :], first, float(HALF), 1.0 - 2 * HALF, ALU.is_ge, ALU.mult))
                step(dve.scalar_tensor_tensor(t0[:, :], first, 2.0, t0[:, :], ALU.mult, ALU.add))
                step(dve.tensor_scalar(t1[:, :], present[:, :], -SKIP, SKIP, ALU.mult, ALU.add))
                step(dve.tensor_tensor(start_row[:, :], t0[:, :], t1[:, :], ALU.add))
                dve.sem_inc(rows_ready, 1)
                step(dve.tensor_scalar(t0[:, :], first, float(HALF), None, ALU.is_lt))
                step(dve.scalar_tensor_tensor(t0[:, :], nxt[:, :], float(HALF), t0[:, :], ALU.is_gt, ALU.mult))
                step(dve.tensor_scalar(span_bias[:, :], t0[:, :], -NEG, NEG, ALU.mult, ALU.add))
                step(dve.tensor_scalar(nxt[:, :], nxt[:, :], -1.0, 0.0, ALU.add, ALU.max))
                step(dve.tensor_scalar(t0[:, :], nxt[:, :], float(HALF), 1.0 - 2 * HALF, ALU.is_ge, ALU.mult))
                step(dve.scalar_tensor_tensor(end_row[:, :], nxt[:, :], 2.0, t0[:, :], ALU.mult, ALU.add))
                with dve.Fori(NG // 2 + 1, NG) as g:
                    add_bias(g)

        def edge_sem(name):
            return whole.enter_context(nc.semaphore(name))

        ix_in = [edge_sem(f"ix_in{u}") for u in range(UNROLL)]
        kv_in = [edge_sem(f"kv_in{u}") for u in range(UNROLL)]
        q_in = [edge_sem(f"q_in{u}") for u in range(UNROLL)]
        mask_in = [edge_sem(f"mask_in{u}") for u in range(UNROLL)]
        rows_out = [edge_sem(f"rows_out{i}") for i in range(2)]
        cleared, kq_turned, v_turned, out_turned = (edge_sem(n) for n in ("cleared", "kq_turned", "v_turned", "out_turned"))
        q_held, kq_ready, logits_ready, carried, top_ready = (edge_sem(n) for n in (
            "q_held", "kq_ready", "logits_ready", "carried", "top_ready"))
        grown, gaps_ready, ex_ready, weighted, v_summed, d_summed, copied, gathering = (edge_sem(n) for n in (
            "grown", "gaps_ready", "ex_ready", "weighted", "v_summed", "d_summed", "copied", "gathering"))

        w_in, w_high, w_parted = (edge_sem(n) for n in ("expert_w_in", "expert_w_high", "expert_w_parted"))

        def edge_phase(layer):
            with ExitStack() as phase:
                def sb(name, shape, dt=F32):
                    return phase.enter_context(nc.sbuf_tensor(f"{name}_{layer}", shape, dt))

                def pb(name):
                    return phase.enter_context(nc.psum_tensor(f"{name}_{layer}", [P, STEP], F32))

                U = UNROLL
                ix = sb("ix", [P, U, TPB * STREAMS], I32)
                kv = sb("kv", [P, U, TPB, STREAMS * 2 * HC])
                qz = sb("qz", [P, U, TPB, STREAMS * HC])
                mask = sb("mask", [P, U, 2, STEP], BF16)
                held_q = sb("held_q", [P, 2, STEP])
                kq = sb("kq", [P, 2, STEP])
                top = sb("top", [P, U, 1 + STEP])
                gap = sb("gap", [P, 2, 2, STEP])
                ex = sb("ex", [P, 2, 2, STEP])
                wv = sb("wv", [P, 2, STEP])
                run_v = sb("run_v", [P, U, STEP])
                run_d = sb("run_d", [P, U, STEP])
                rows = sb("rows", [P, 2, TPB, STREAMS, ROW])
                if layer == 1:
                    w_raw = sb("w_raw", [P, KC * HID])
                kT = [pb(f"kT{i}") for i in range(2)]
                qT = [pb(f"qT{i}") for i in range(2)]
                vT, logit, outT = pb("vT"), pb("logit"), pb("outT")
                restT = pb("restT")[:, 0:2 * TPB * STREAMS * HEADS].rearrange("p (m j h) -> p m j h", m=2, j=TPB)

                block = phase.enter_context(nc.Block())

                past = STEPS * layer
                peeled = 2

                def each_step(eng, body):
                    for i in range(past, past + peeled):
                        body(i)
                    with eng.Fori(past + peeled, past + STEPS) as i:
                        body(i)

                def each_block(eng, stages, before=None, after=None):
                    def body(i):
                        if before and layer == 1 and not isinstance(i, int):
                            before(i - past - peeled)
                        blocks(i)
                        if after and layer == 1 and not isinstance(i, int):
                            after(i - past - peeled)

                    def blocks(i):
                        for u in range(U):
                            for lag, stage in enumerate(stages):
                                b = U * i + u - lag
                                if not isinstance(i, int) or b >= U * past:
                                    stage(b, (u - lag) % U, i if u >= lag else i - 1)
                    each_step(eng, body)
                    for late in range(1, len(stages)):
                        for lag in range(late, len(stages)):
                            b = U * (past + STEPS) + late - 1 - lag
                            stages[lag](b, b % U, b // U)

                @block.sync
                def _(sp):
                    def body(i):
                        for u in range(U):
                            b = U * i + u
                            wait_past(sp, kq_turned, b - U + 1)
                            wait_past(sp, gaps_ready, b - U + 1)
                            sp.dma_start(ix[:, u, :], d["src"][b - BLOCKS * layer]).then_inc(ix_in[u], 16)
                            sp.dma_start(qz[:, u, :, :], qz_blocks[b - BLOCKS * layer]).then_inc(q_in[u], 16)
                            for s in range(STREAMS):
                                sp.dma_start(mask[HC * s:HC * (s + 1), u, :, :].rearrange("p m c -> p (m c)"),
                                             mask_t[s, b - BLOCKS * layer].partition_broadcast(HC)).then_inc(mask_in[u], 16)
                    def with_weights(i):
                        body(i)
                        if layer == 1 and not isinstance(i, int):
                            n = i - past - peeled
                            sp.wait_ge(w_parted, n + 1)
                            sp.dma_start(w_raw[:, :], d["expert_w"][n]).then_inc(w_in, 16)
                    each_step(sp, with_weights)

                @block.gpsimd
                def _(pool):
                    def body(i):
                        for u in range(U):
                            b = U * i + u
                            pool.wait_ge(ix_in[u], 16 * i + 16)
                            wait_past(pool, v_turned, b - U + 1)
                            pool.sem_inc(gathering, 1)
                            for j in range(TPB):
                                for s in range(STREAMS):
                                    n = STREAMS * j + s
                                    pool.indirect_dma_start(kv[:, u, j, 2 * HC * s:2 * HC * (s + 1)], None, kv_t,
                                                            bass.IndirectOffsetOnAxis(ix[:, u, n:n + 1], 0),
                                                            bounds_check=NP - 1, oob_is_err=False).then_inc(kv_in[u], 16)
                    each_step(pool, body)

                @block.tensor
                def _(pe):
                    def turn_kq(b, u, i):
                        pe.wait_ge(kv_in[u], 16 * TPB * STREAMS * (i + 1))
                        pe.wait_ge(q_in[u], 16 * i + 16)
                        wait_past(pe, kq_ready, b - 1)
                        for j in range(TPB):
                            pe.transpose(kT[u % 2][:, P * j:P * (j + 1)], kv[:, u, j, 0::2], identity[:, :])
                            ins = pe.transpose(qT[u % 2][:, P * j:P * (j + 1)], qz[:, u, j, :], identity[:, :])
                        ins.then_inc(kq_turned, 1)

                    def logits(b, u, i):
                        pe.wait_ge(kq_ready, b + 1)
                        wait_past(pe, gaps_ready, b)
                        pe.matmul(logit[:, :], head_sum[:, :], kq[:, u % 2, :], start=True, stop=True)\
                            .then_inc(logits_ready, 1)

                    def turn_v(b, u, i):
                        wait_past(pe, weighted, b)
                        for j in range(TPB):
                            ins = pe.transpose(vT[:, P * j:P * (j + 1)], kv[:, u, j, 1::2], identity[:, :])
                        ins.then_inc(v_turned, 1)

                    def turn_results(b, u, i):
                        pe.wait_ge(v_summed, b + 1)
                        pe.wait_ge(d_summed, b + 1)
                        wait_past(pe, copied, 3 * b)
                        for j in range(TPB):
                            of = slice(P * j, P * (j + 1))
                            pe.transpose(outT[:, of], run_v[:, u, of], identity[:, :])
                            pe.matmul(restT[:, 0, j, :], run_d[:, u, of], pick[:, :], start=True, stop=True)
                            ins = pe.matmul(restT[:, 1, j, :], top[:, u, 1 + P * j:1 + P * (j + 1)], pick[:, :],
                                            start=True, stop=True)
                        ins.then_inc(out_turned, 1)

                    each_block(pe, [turn_kq, logits, turn_v, turn_results])

                @block.vector
                def _(dve):
                    dve.memset(held_q[:, 1, STEP - 1:STEP], 0.0).then_inc(cleared, 1)
                    dve.memset(top[:, U - 1, STEP:STEP + 1], 0.0).then_inc(cleared, 1)
                    dve.memset(run_v[:, U - 1, STEP - 1:STEP], 0.0).then_inc(cleared, 1)
                    dve.memset(run_d[:, U - 1, STEP - 1:STEP], 0.0).then_inc(cleared, 1)
                    dve.wait_ge(cleared, 4 * layer + 4)
                    if layer == 1:
                        dve.sem_inc(w_parted, 1)

                    def part_low(n):
                        dve.wait_ge(w_high, n + 1)
                        dve.tensor_tensor(w_lo[:, n, :], w_raw[:, :], w_hi[:, n, :].bitcast(F32),
                                          ALU.subtract).then_inc(w_parted, 1)

                    def hold_q(b, u, i):
                        h = u % 2
                        dve.wait_ge(kq_turned, b + 1)
                        dve.wait_ge(mask_in[u], 32 * i + 32)
                        wait_past(dve, q_held, b)
                        dve.tensor_tensor_scan(held_q[:, h, :], mask[:, u, 0, :], qT[h][:, :],
                                               held_q[:, 1 - h, STEP - 1:STEP], ALU.mult, ALU.add).then_inc(q_held, 1)
                        dve.wait_ge(q_held, b + 1)
                        wait_past(dve, logits_ready, b - 1)
                        dve.tensor_tensor(kq[:, h, :], kT[h][:, :], held_q[:, h, :], ALU.mult).then_inc(kq_ready, 1)

                    def maximum(b, u, i):
                        h = u % 2
                        before, now = top[:, u, 0:STEP], top[:, u, 1:1 + STEP]
                        last = top[:, (u - 1) % U, STEP:STEP + 1]
                        wait_past(dve, top_ready, b)
                        wait_past(dve, out_turned, b - U + 1)
                        dve.tensor_copy(top[:, u, 0:1], last).then_inc(carried, 1)
                        dve.wait_ge(logits_ready, b + 1)
                        dve.tensor_tensor_scan(now, mask[:, u, 1, :], logit[:, :], last,
                                               ALU.add, ALU.max).then_inc(top_ready, 1)
                        dve.wait_ge(top_ready, b + 1)
                        dve.wait_ge(carried, b + 1)
                        wait_past(dve, ex_ready, b - 1)
                        dve.tensor_tensor(gap[:, h, 1, :], before, now, ALU.subtract).then_inc(grown, 1)
                        dve.tensor_tensor(gap[:, h, 0, :], logit[:, :], now, ALU.subtract).then_inc(grown, 1)
                        dve.wait_ge(grown, 2 * b + 2)
                        dve.tensor_tensor(gap[:, h, 1, :], gap[:, h, 1, :], mask[:, u, 1, :], ALU.add).then_inc(gaps_ready, 1)

                    def sums(b, u, i):
                        h = u % 2
                        dve.wait_ge(ex_ready, b + 1)
                        dve.wait_ge(v_turned, b + 1)
                        dve.tensor_tensor(wv[:, h, :], vT[:, :], ex[:, h, 0, :], ALU.mult).then_inc(weighted, 1)
                        wait_past(dve, out_turned, b - U + 1)
                        wait_past(dve, d_summed, b)
                        dve.tensor_tensor_scan(run_d[:, u, :], ex[:, h, 1, :], ex[:, h, 0, :],
                                               run_d[:, (u - 1) % U, STEP - 1:STEP], ALU.mult, ALU.add).then_inc(d_summed, 1)
                        dve.wait_ge(weighted, b + 1)
                        wait_past(dve, v_summed, b)
                        dve.tensor_tensor_scan(run_v[:, u, :], ex[:, h, 1, :], wv[:, h, :],
                                               run_v[:, (u - 1) % U, STEP - 1:STEP], ALU.mult, ALU.add).then_inc(v_summed, 1)

                    each_block(dve, [hold_q, maximum, sums], after=part_low)

                @block.scalar
                def _(act):
                    def weights(b, u, i):
                        h = u % 2
                        act.wait_ge(gaps_ready, b + 1)
                        wait_past(act, v_summed, b - 1)
                        act.activation(ex[:, h, :, :].rearrange("p m c -> p (m c)"),
                                       gap[:, h, :, :].rearrange("p m c -> p (m c)"), ACT.Exp).then_inc(ex_ready, 1)

                    def store(b, u, i):
                        h = u % 2
                        act.wait_ge(out_turned, b + 1)
                        wait_past(act, rows_out[h], 16 * (U // 2 * i + u // 2))
                        flat = rows[:, h, :, :, :].rearrange("p j s c -> p (j s) c")
                        act.activation(flat[:, :, 0:HC], outT[:, :].rearrange("p (r c) -> p r c", c=HC),
                                       ACT.Copy).then_inc(copied, 1)
                        for m, at in enumerate((DEN, MAX)):
                            act.activation(flat[:, :, at:at + HEADS],
                                           restT[:, m, :, :].rearrange("p j (s h) -> p (j s) h", h=HEADS),
                                           ACT.Copy).then_inc(copied, 1)
                        act.wait_ge(copied, 3 * b + 3)
                        act.dma_start(sum_blocks[b - BLOCKS * layer], rows[:, h, :, :, :].rearrange("p j s c -> p j (s c)"))\
                            .then_inc(rows_out[h], 16)

                    def part_high(n):
                        act.wait_ge(w_in, 16 * n + 16)
                        act.activation(w_hi[:, n, :], w_raw[:, :], ACT.Copy).then_inc(w_high, 1)

                    each_block(act, [weights, lambda b, u, i: None, store], before=part_high)
                    for h in range(2):
                        act.wait_ge(rows_out[h], 16 * BLOCKS // 2 * (layer + 1))

        all4 = [P, GROUP, HEADS]
        all64 = [P, GROUP, HEADS, CH]

        def by_head(a):
            return a.rearrange("p i (h c) -> p i h c", c=CH)

        class NodeResults:
            DISTANCES, SUMS, FINISH = 4, 8, 2

            def __init__(self, sb):
                self.cut = sb("cut", [P, ROW])
                self.mb = sb("mb", [P, GROUP, HEADS])
                self.mm = sb("mm", [P, GROUP, HEADS])
                self.wt = sb("wt", [P, GROUP, 2, HEADS])
                self.wx = sb("wx", [P, GROUP, 2, HEADS])
                self.den = sb("den", [P, GROUP, HEADS])
                self.part = sb("part", [P, GROUP, HEADS])
                self.ov = sb("ov", [P, GROUP, HC])
                self.h = sb("h", [P, GROUP, HC])

            def distances(self, dve, step, of, fin):
                step(dve.tensor_tensor(self.mb[:, :, :], span_bias[:, of].unsqueeze(2).to_broadcast(all4),
                                       self.cut[:, MAX:MAX + HEADS].unsqueeze(1).to_broadcast(all4), ALU.add))
                step(dve.tensor_tensor(self.mm[:, :, :], self.mb[:, :, :], fin[:, :, MAX:MAX + HEADS], ALU.max))
                step(dve.tensor_tensor(self.wt[:, :, 0, :], fin[:, :, MAX:MAX + HEADS], self.mm[:, :, :], ALU.subtract))
                step(dve.tensor_tensor(self.wt[:, :, 1, :], self.mb[:, :, :], self.mm[:, :, :], ALU.subtract))

            def sum_parts(self, dve, step, of, fin):
                step(dve.tensor_tensor(self.den[:, :, :], fin[:, :, DEN:DEN + HEADS], self.wx[:, :, 0, :], ALU.mult))
                step(dve.tensor_tensor(self.part[:, :, :], self.cut[:, DEN:DEN + HEADS].unsqueeze(1).to_broadcast(all4),
                                       self.wx[:, :, 1, :], ALU.mult))
                step(dve.scalar_tensor_tensor(self.den[:, :, :].rearrange("p i h -> p (i h)"), self.den[:, :, :].rearrange("p i h -> p (i h)"),
                                              DEN_EPS, self.part[:, :, :].rearrange("p i h -> p (i h)"), ALU.add, ALU.add))
                step(dve.reciprocal(self.den[:, :, :], self.den[:, :, :]))
                step(dve.tensor_tensor(self.den[:, :, :], self.den[:, :, :], present[:, of].unsqueeze(2).to_broadcast(all4), ALU.mult))
                step(dve.tensor_tensor(self.wx[:, :, :, :], self.wx[:, :, :, :], self.den[:, :, :].unsqueeze(2).to_broadcast([P, GROUP, 2, HEADS]), ALU.mult))
                step(dve.tensor_tensor(by_head(self.h[:, :, :]), by_head(fin[:, :, 0:HC]),
                                       self.wx[:, :, 0, :].unsqueeze(3).to_broadcast(all64), ALU.mult))
                step(dve.tensor_tensor(by_head(self.ov[:, :, :]), self.wx[:, :, 1, :].unsqueeze(3).to_broadcast(all64),
                                       self.cut[:, 0:HC].rearrange("p (h c) -> p h c", c=CH).unsqueeze(1).to_broadcast(all64), ALU.mult))

            def finish(self, dve, step, skip_path):
                step(dve.tensor_tensor(self.h[:, :, :], self.h[:, :, :], self.ov[:, :, :], ALU.add))
                step(dve.tensor_tensor(self.ov[:, :, :], self.h[:, :, :], skip_path, ALU.add))
                return dve.tensor_scalar(self.h[:, :, :], self.ov[:, :, :], 0.0, None, ALU.max)

        def exponentials_of(act, b):
            return act.activation(b.wx[:, :, :, :].rearrange("p i m h -> p (i m h)"),
                                  b.wt[:, :, :, :].rearrange("p i m h -> p (i m h)"), ACT.Exp)

        def node_phase():
            with ExitStack() as phase:
                def sb(name, shape, dt=F32):
                    return phase.enter_context(nc.sbuf_tensor(f"{name}_n", shape, dt))

                def pb(name):
                    return phase.enter_context(nc.psum_tensor(f"{name}_n", [P, 512], F32))

                def sem(name):
                    return whole.enter_context(nc.semaphore(f"{name}_n"))

                G = GROUP
                AHEAD = 3
                fin = sb("fin", [P, NT, ROW])
                res = NodeResults(sb)
                hT = sb("hT", [HC + 1, G * P])
                w_sb = sb("w_sb", [HC + 1, PROJ])
                psT = [pb(f"psT{i}") for i in range(2)]
                psP = [pb(f"psP{i}") for i in range(4)]
                fin_in = [sem(f"fin_in{g}") for g in range(NG)]
                w_in, cut_in, fins, weights_wanted, weights_ready, comb = (sem(n) for n in (
                    "w_in", "cut_in", "fins", "weights_wanted", "weights_ready", "comb"))
                ones, combined, turned, hT_ready, product, projected, skipped = (sem(n) for n in (
                    "ones", "combined", "turned", "hT_ready", "product", "projected", "skipped"))
                stored, scattered, cut_got, cut_done = (sem(n) for n in ("stored", "scattered", "cut_got", "cut_done"))
                block = phase.enter_context(nc.Block())
                QUADS = (slice(0, 4), slice(4, G))

                def pair(n):
                    return slice(2 * n, min(2 * n + 2, G))

                def by_tile(bank, n):
                    return bank[:, 0:PROJ * (pair(n).stop - pair(n).start)].rearrange("p (u c) -> p u c", c=PROJ)

                @block.sync
                def _(sp):
                    sp.dma_start(res.cut[:, :], sum_t[2 * (HALF - 1)].partition_broadcast(P)).then_inc(cut_in, 16)
                    sp.dma_start(w_sb[:, :], d["proj2"]).then_inc(w_in, 16)
                    store_tables(sp, projected, 4, stored)

                @block.gpsimd
                def _(pool):
                    def gather(g):
                        for i in range(G * g, G * (g + 1)):
                            pool.indirect_dma_start(fin[:, i, :], None, sum_t,
                                                    bass.IndirectOffsetOnAxis(end_row[:, i:i + 1], 0),
                                                    bounds_check=EP - 1, oob_is_err=False).then_inc(fin_in[g], 16)

                    def announce(g):
                        pool.wait_ge(fin_in[g], 16 * G)
                        pool.sem_inc(fins, 1)

                    for g in range(AHEAD):
                        gather(g)
                        if g >= 1:
                            announce(g - 1)
                    for g in range(NG):
                        if g + AHEAD < NG:
                            gather(g + AHEAD)
                        if g + AHEAD - 1 < NG:
                            announce(g + AHEAD - 1)
                        pool.wait_ge(projected, 4 * (g + 1))
                        scatter_q(pool, scattered, g)
                    scatter_cut(pool, scattered, stored, cut_got, cut_done)

                @block.tensor
                def _(pe):
                    pe.wait_ge(w_in, 16)
                    pe.wait_ge(ones, 1)
                    def group(g):
                        pe.wait_ge(combined, g + 1)
                        for n, tiles in enumerate(QUADS):
                            for k, u in enumerate(range(tiles.start, tiles.stop)):
                                ins = pe.matmul(psT[n][0:HC, P * k:P * (k + 1)], res.h[:, u, :], identity[:, :],
                                                start=True, stop=True)
                            ins.then_inc(turned, 1)
                        pe.wait_ge(hT_ready, 2 * g + 2)
                        for n in range(4):
                            wait_past(pe, skipped, 4 * g + n - 3)
                            for k, u in enumerate(range(pair(n).start, pair(n).stop)):
                                ins = pe.matmul(psP[n][:, PROJ * k:PROJ * (k + 1)], hT[:, P * u:P * (u + 1)], w_sb[:, :],
                                                start=True, stop=True)
                            ins.then_inc(product, 1)

                    each_group(pe, group)

                @block.scalar
                def _(act):
                    def weigh(g):
                        act.wait_ge(weights_wanted, g + 1)
                        exponentials_of(act, res).then_inc(weights_ready, 1)

                    def take_h(g):
                        for n, tiles in enumerate(QUADS):
                            act.wait_ge(turned, 2 * g + n + 1)
                            act.activation(hT[0:HC, P * tiles.start:P * tiles.stop], psT[n][0:HC, 0:P * (tiles.stop - tiles.start)],
                                           ACT.Copy).then_inc(hT_ready, 1)

                    def take_skip(g):
                        for n in range(4):
                            act.wait_ge(projected, 4 * g + n + 1)
                            tiles = bass.ds(G * g + pair(n).start, pair(n).stop - pair(n).start)
                            act.activation(skip[:, tiles, :], by_tile(psP[n], n)[:, :, S0:PROJ], ACT.Copy).then_inc(skipped, 1)

                    weigh(0)
                    with act.Fori(0, NG - 1) as g:
                        take_h(g)
                        weigh(g + 1)
                        take_skip(g)
                    take_h(NG - 1)
                    take_skip(NG - 1)

                @block.vector
                def _(dve):
                    dve.memset(hT[HC:HC + 1, :], 1.0).then_inc(ones, 1)
                    dve.wait_ge(cut_in, 16)
                    COMB = res.DISTANCES + res.SUMS + res.FINISH

                    def combine(g):
                        of = ts(g, G)
                        step = Steps(dve, comb, COMB * g)
                        dve.wait_ge(fins, g + 1)
                        res.distances(dve, step, of, fin[:, of, :])
                        dve.sem_inc(weights_wanted, 1)
                        dve.wait_ge(weights_ready, g + 1)
                        wait_past(dve, turned, 2 * g)
                        res.sum_parts(dve, step, of, fin[:, of, :])
                        res.finish(dve, step, proj[:, of, S0:PROJ]).then_inc(combined, 1)

                    def take_projections(g):
                        for n in range(4):
                            dve.wait_ge(product, 4 * g + n + 1)
                            tiles = bass.ds(G * g + pair(n).start, pair(n).stop - pair(n).start)
                            dve.tensor_copy(proj[:, tiles, 0:S0], by_tile(psP[n], n)[:, :, 0:S0]).then_inc(projected, 1)

                    combine(0)
                    with dve.Fori(0, NG - 1) as g:
                        combine(g + 1)
                        take_projections(g)
                    take_projections(NG - 1)

        def expert_phase():
            with ExitStack() as phase:
                def sb(name, shape, dt=F32):
                    return phase.enter_context(nc.sbuf_tensor(f"{name}_x", shape, dt))

                def pb(name):
                    return phase.enter_context(nc.psum_tensor(f"{name}_x", [P, 512], F32))

                def sem(name):
                    return whole.enter_context(nc.semaphore(f"{name}_x"))

                G = GROUP
                LH, LO = HID // P, EXPERTS * HID // P
                fin = sb("fin", [P, G, ROW])
                res = NodeResults(sb)
                hT = sb("hT", [HC + 1, GTOK])
                wo = sb("wo", [HC + 1, D])
                x = sb("x", [P, G, D])
                y = sb("y", [P, G, D])
                stat = sb("stat", [P, G, 6])
                mv = sb("mv", [P, G, 2])
                rstd = sb("rstd", [P, G])
                y_hi = sb("y_hi", [P, KC, GTOK], F32R)
                y_lo = sb("y_lo", [P, KC, GTOK], F32R)
                wr = sb("wr", [P, KC, EXPERTS])
                wr_parts = sb("wr_parts", [P, KC, 2, EXPERTS], F32R)
                br = sb("br", [P, EXPERTS])
                gate = sb("gate", [P, G, EXPERTS])
                red = sb("red", [P, G])
                gT = sb("gT", [EXPERTS, GTOK])
                bo8 = sb("bo8", [EXPERTS, D])
                bn = sb("bn", [P, 2, 5, LO])
                scale = sb("scale", [P, 2, LO])
                offset = sb("offset", [P, 2, LO])
                bn_eps = sb("bn_eps", [P, 1])
                full = sb("full", [P, 4, HTOK])
                hid_hi = [sb(f"hid_hi{n}", [P, LH, GTOK], F32R) for n in range(2)]
                hid_lo = [sb(f"hid_lo{n}", [P, LH, GTOK], F32R) for n in range(2)]
                total = sb("total", [P, G, D])
                psH = [pb(f"psH{i}") for i in range(3)]
                psO = [pb(f"psO{i}") for i in range(3)]
                psA = [pb(f"psA{i}") for i in range(2)]

                consts_in, bn_in, bn_eps_set, bn_rooted, bn_step, folded, wr_split = (sem(n) for n in (
                    "consts_in", "bn_in", "bn_eps_set", "bn_rooted", "bn_step", "folded", "wr_split"))
                fin_in, x_in, combined, weights_wanted, weights_ready, comb = (sem(n) for n in (
                    "fin_in", "x_in", "combined", "weights_wanted", "weights_ready", "comb"))
                residual, stats_done, aggregated, rooted, norm, y_ready, y_high = (sem(n) for n in (
                    "residual", "stats_done", "aggregated", "rooted", "norm", "y_ready", "y_high"))
                smax, gap_ready, exp_ready, gate_ready, bias_added = (sem(n) for n in (
                    "smax", "gap_ready", "exp_ready", "gate_ready", "bias_added"))
                ones = sem("ones")
                in_bank, bank_read = sem("in_bank"), [sem(f"bank_read{i}") for i in range(2)]
                formed, relued, parted, out_formed, added, stored = (sem(n) for n in (
                    "hid_formed", "hid_relued", "hid_parted", "out_formed", "out_added", "out_stored"))
                block = phase.enter_context(nc.Block())

                TURN_H, PROJECT, TURN_Y = 0, 2, 6
                ROUTE, TURN_GATE, BIAS = 10, 11, 13
                USES = 17

                def bank_of(use):
                    return psA[use % 2]

                def reads_before(p, use):
                    return (9 if use % 2 == 0 else 8) * p + use // 2

                def wait_free(pe, p, use):
                    count = reads_before(p, use)
                    if not isinstance(count, int) or count >= 1:
                        pe.wait_ge(bank_read[use % 2], count)

                def wait_read(eng, p, use):
                    eng.wait_ge(bank_read[use % 2], reads_before(p, use) + 1)

                def wait_in_bank(eng, p, use):
                    eng.wait_ge(in_bank, USES * p + use + 1)

                def pairs(use_of_kind):
                    return slice(2 * use_of_kind, min(2 * use_of_kind + 2, G))

                QUADS = (slice(0, 4), slice(4, G))

                order = [(0, 0)] + [z for e in range(EXPERTS) for z in ((e, 1), (e + 1, 0))][:-1]
                place = {z: 4 * n for n, z in enumerate(order)}
                PER = 4 * len(order)
                OUTS = EXPERTS * G
                FREE_RELUED, FREE_PARTED, FREE_OUT, FREE_ADDED = 2 * len(psH), 4, G, len(psO)

                def all_groups(eng, before, experts):
                    for slot in sorted(before(0)):
                        before(0)[slot]()
                    with eng.Fori(0, NG - 1) as g:
                        experts(g, before(g + 1))
                    experts(NG - 1, {})

                def run(pieces, e, n):
                    if (e, n) in pieces:
                        pieces[e, n]()

                @block.sync
                def _(sp):
                    sp.sem_inc(stored, 16)
                    sp.dma_start(bn[:, :, :, :], d["bn"]).then_inc(bn_in, 16)
                    for to, name in ((wo[:, :], d["wo_bo"]),
                                     (wr[:, :, :], d["wr"].rearrange("(k p) e -> p k e", p=P)),
                                     (br[:, :], d["br"].partition_broadcast(P)), (bo8[:, :], d["bo8"]),
                                     (res.cut[:, :], sum_t[2 * (HALF - 1)].partition_broadcast(P))):
                        sp.dma_start(to, name).then_inc(consts_in, 16)
                    with sp.Fori(0, NG) as g:
                        sp.wait_ge(added, FREE_ADDED + OUTS * (g + 1))
                        sp.dma_start(d["out"].rearrange("(i p) c -> p i c", p=P)[:, ts(g, G), :],
                                     total[:, :, :]).then_inc(stored, 16)
                    sp.wait_ge(stored, 16 * (NG + 1))

                @block.gpsimd
                def _(pool):
                    features = d["x"].rearrange("(i p) c -> p i c", p=P)
                    for p in range(NG):
                        if p >= 1:
                            pool.wait_ge(combined, p)
                        for i in range(G):
                            pool.indirect_dma_start(fin[:, i, :], None, sum_t,
                                                    bass.IndirectOffsetOnAxis(end_row[:, G * p + i:G * p + i + 1], 0),
                                                    bounds_check=EP - 1, oob_is_err=False).then_inc(fin_in, 16)
                        if p >= 1:
                            pool.wait_ge(added, FREE_ADDED + OUTS * (p - 1) + G)
                        pool.dma_start(x[:, :, :], features[:, G * p:G * (p + 1), :]).then_inc(x_in, 16)
                    pool.wait_ge(x_in, 16 * NG)

                @block.tensor
                def _(pe):
                    pe.sem_inc(out_formed, FREE_OUT)
                    pe.wait_ge(consts_in, 16 * 5)

                    def before(p):
                        def turn_h():
                            pe.wait_ge(combined, p + 1)
                            for n, tiles in enumerate(QUADS):
                                wait_free(pe, p, TURN_H + n)
                                for k, u in enumerate(range(tiles.start, tiles.stop)):
                                    ins = pe.matmul(bank_of(TURN_H + n)[0:HC, P * k:P * (k + 1)], res.h[:, u, :], identity[:, :],
                                                    start=True, stop=True)
                                ins.then_inc(in_bank, 1)

                        def project(uses):
                            def go():
                                wait_read(pe, p, TURN_H)
                                wait_read(pe, p, TURN_H + 1)
                                for n in uses:
                                    wait_free(pe, p, PROJECT + n)
                                    for k, u in enumerate(range(pairs(n).start, pairs(n).stop)):
                                        ins = pe.matmul(bank_of(PROJECT + n)[:, D * k:D * (k + 1)], hT[:, P * u:P * (u + 1)], wo[:, :],
                                                        start=True, stop=True)
                                    ins.then_inc(in_bank, 1)
                            return go

                        def turn_y(uses):
                            def go():
                                pe.wait_ge(y_ready, p + 1)
                                for n in uses:
                                    wait_free(pe, p, TURN_Y + n)
                                    for k, u in enumerate(range(pairs(n).start, pairs(n).stop)):
                                        for c in range(KC):
                                            at = 2 * P * c + P * k
                                            ins = pe.transpose(bank_of(TURN_Y + n)[:, at:at + P], y[:, u, P * c:P * (c + 1)], identity[:, :])
                                    ins.then_inc(in_bank, 1)
                            return go

                        return {(2, 0): turn_h, (2, 1): project((0, 1)), (3, 0): project((2, 3)),
                                (6, 1): turn_y((0, 1)), (7, 0): turn_y((2, 3))}

                    def product(out, first, last, *operands):
                        (a_hi, a_lo), (b_hi, b_lo) = operands
                        pe.matmul(out, a_hi, b_hi, start=first, stop=False)
                        pe.matmul(out, a_hi, b_lo, start=False, stop=False)
                        return pe.matmul(out, a_lo, b_hi, start=False, stop=last)

                    def experts(g, pieces):
                        def hidden(e, layer):
                            n0 = place[e, layer]
                            for m in range(LH):
                                for half in range(2):
                                    n, of = n0 + 2 * m + half, slice(HTOK * half, HTOK * (half + 1))
                                    pe.wait_ge(relued, FREE_RELUED + 2 * (PER * g + max(0, n + 1 - len(psH))))
                                    if layer == 1:
                                        pe.wait_ge(parted, FREE_PARTED + PER * g + place[e, 0] + 3 + half)
                                    for c in range(KC):
                                        hi, lo = (y_hi, y_lo) if layer == 0 else (hid_hi[0], hid_lo[0])
                                        w_at = slice(HID * c + P * m, HID * c + P * (m + 1))
                                        ins = product(psH[n % len(psH)][:, 0:HTOK], c == 0, c == KC - 1,
                                                      (w_hi[:, EXPERTS * layer + e, w_at], w_lo[:, EXPERTS * layer + e, w_at]),
                                                      (hi[:, c, of], lo[:, c, of]))
                                    ins.then_inc(formed, 1)

                        def outputs(e):
                            pe.wait_ge(parted, FREE_PARTED + PER * g + place[e, 1] + 4)
                            for u in range(G):
                                n, of = G * e + u, slice(P * u, P * (u + 1))
                                pe.wait_ge(added, FREE_ADDED + OUTS * g + max(0, n + 1 - len(psO)))
                                for c in range(KC):
                                    w_at = slice(HID * c, HID * (c + 1))
                                    ins = product(psO[n % len(psO)][:, 0:D], c == 0, c == KC - 1,
                                                  (hid_hi[1][:, c, of], hid_lo[1][:, c, of]),
                                                  (w_hi[:, EXPERTS * 2 + e, w_at], w_lo[:, EXPERTS * 2 + e, w_at]))
                                ins.then_inc(out_formed, 1)

                        def route():
                            wait_free(pe, g, ROUTE)
                            for u in range(G):
                                of = slice(P * u, P * (u + 1))
                                at = 2 * EXPERTS * u
                                both, high = (bank_of(ROUTE)[:, at:at + n * EXPERTS] for n in (2, 1))
                                pe.matmul(both, y_hi[:, 0, of], wr_parts[:, 0, :, :], start=True, stop=False)
                                for c in range(KC):
                                    pe.matmul(high, y_lo[:, c, of], wr_parts[:, c, 0, :], start=False, stop=False)
                                ins = pe.matmul(both, y_hi[:, 1, of], wr_parts[:, 1, :, :], start=False, stop=True)
                            ins.then_inc(in_bank, 1)

                        def turn_gate():
                            pe.wait_ge(gate_ready, g + 1)
                            for n, tiles in enumerate(QUADS):
                                wait_free(pe, g, TURN_GATE + n)
                                for k, u in enumerate(range(tiles.start, tiles.stop)):
                                    ins = pe.transpose(bank_of(TURN_GATE + n)[0:EXPERTS, P * k:P * (k + 1)], gate[:, u, :], identity[:, :])
                                ins.then_inc(in_bank, 1)

                        def biases(uses):
                            wait_read(pe, g, TURN_GATE)
                            wait_read(pe, g, TURN_GATE + 1)
                            for n in uses:
                                wait_free(pe, g, BIAS + n)
                                for k, u in enumerate(range(pairs(n).start, pairs(n).stop)):
                                    ins = pe.matmul(bank_of(BIAS + n)[:, D * k:D * (k + 1)], gT[:, P * u:P * (u + 1)], bo8[:, :],
                                                    start=True, stop=True)
                                ins.then_inc(in_bank, 1)

                        wait_read(pe, g, TURN_Y + 2)
                        wait_read(pe, g, TURN_Y + 3)
                        hidden(0, 0)
                        route()
                        for e in range(EXPERTS):
                            hidden(e, 1)
                            if e == 1:
                                biases((0, 1))
                            run(pieces, e, 0)
                            if e + 1 < EXPERTS:
                                hidden(e + 1, 0)
                            if e == 0:
                                turn_gate()
                            if e == 1:
                                biases((2, 3))
                            run(pieces, e, 1)
                            outputs(e)

                    pe.wait_ge(ones, 1)
                    pe.wait_ge(wr_split, 2)
                    all_groups(pe, before, experts)

                @block.scalar
                def _(act):
                    act.sem_inc(relued, FREE_RELUED)
                    act.wait_ge(bn_eps_set, 1)
                    act.wait_ge(bn_in, 16)
                    act.activation(scale[:, :, :], bn[:, :, 4, :], ACT.Sqrt, bias=bn_eps[:, 0:1]).then_inc(bn_rooted, 1)

                    def before(p):
                        def merge_weights():
                            act.wait_ge(weights_wanted, p + 1)
                            exponentials_of(act, res).then_inc(weights_ready, 1)

                        def take_h():
                            for n, tiles in enumerate(QUADS):
                                wait_in_bank(act, p, TURN_H + n)
                                act.activation(hT[0:HC, P * tiles.start:P * tiles.stop],
                                               bank_of(TURN_H + n)[0:HC, 0:P * (tiles.stop - tiles.start)],
                                               ACT.Copy).then_inc(bank_read[(TURN_H + n) % 2], 1)

                        def squash(uses):
                            def go():
                                for n in uses:
                                    wait_in_bank(act, p, PROJECT + n)
                                    tiles = pairs(n)
                                    act.activation(y[:, tiles, :], bank_of(PROJECT + n)[:, 0:D * (tiles.stop - tiles.start)]
                                                   .rearrange("p (u c) -> p u c", c=D), ACT.Sigmoid).then_inc(bank_read[(PROJECT + n) % 2], 1)
                            return go

                        def root():
                            act.wait_ge(aggregated, p + 1)
                            act.activation(rstd[:, :], mv[:, :, 1], ACT.Sqrt, bias=eps[:, 0:1]).then_inc(rooted, 1)

                        def high_y(uses):
                            def go():
                                for n in uses:
                                    wait_in_bank(act, p, TURN_Y + n)
                                    width = P * (pairs(n).stop - pairs(n).start)
                                    at = P * pairs(n).start
                                    act.activation(y_hi[:, :, at:at + width],
                                                   bank_of(TURN_Y + n)[:, :].rearrange("p (c n) -> p c n", c=KC)[:, :, 0:width],
                                                   ACT.Copy).then_inc(y_high, 1)
                            return go

                        return {(0, 1): merge_weights, (2, 0): take_h, (2, 1): squash((0, 1)), (3, 1): squash((2, 3)), (5, 1): root,
                                (6, 1): high_y((0, 1)), (7, 0): high_y((2, 3))}

                    def experts(g, pieces):
                        def hidden(e, layer):
                            for m in range(LH):
                                for half in range(2):
                                    n, of = place[e, layer] + 2 * m + half, slice(HTOK * half, HTOK * (half + 1))
                                    act.wait_ge(formed, PER * g + n + 1)
                                    act.wait_ge(parted, PER * g + n + 1)
                                    if layer == 1 and m == 0 and half == 0:
                                        act.wait_ge(out_formed, OUTS * g + G * e + G)
                                    at = LH * e + m
                                    for to in (full[:, n % 4, :], hid_hi[layer][:, m, of]):
                                        act.activation(to, psH[n % len(psH)][:, 0:HTOK], ACT.Relu, bias=offset[:, layer, at:at + 1],
                                                       scale=scale[:, layer, at:at + 1]).then_inc(relued, 1)

                        def exponentials():
                            act.wait_ge(gap_ready, g + 1)
                            act.activation(gate[:, :, :].rearrange("p i e -> p (i e)"),
                                           gate[:, :, :].rearrange("p i e -> p (i e)"), ACT.Exp).then_inc(exp_ready, 1)

                        def take_gate():
                            for n, tiles in enumerate(QUADS):
                                wait_in_bank(act, g, TURN_GATE + n)
                                act.activation(gT[:, P * tiles.start:P * tiles.stop],
                                               bank_of(TURN_GATE + n)[0:EXPERTS, 0:P * (tiles.stop - tiles.start)],
                                               ACT.Copy).then_inc(bank_read[(TURN_GATE + n) % 2], 1)

                        hidden(0, 0)
                        exponentials()
                        for e in range(EXPERTS):
                            hidden(e, 1)
                            run(pieces, e, 0)
                            if e + 1 < EXPERTS:
                                hidden(e + 1, 0)
                            if e == 0:
                                take_gate()
                            run(pieces, e, 1)

                    act.wait_ge(folded, 1)
                    all_groups(act, before, experts)

                @block.vector
                def _(dve):
                    dve.sem_inc(parted, FREE_PARTED)
                    dve.sem_inc(added, FREE_ADDED)
                    dve.memset(hT[HC:HC + 1, :], 1.0).then_inc(ones, 1)
                    dve.memset(bn_eps[:, :], BN_EPS).then_inc(bn_eps_set, 1)
                    step = Steps(dve, bn_step)
                    dve.wait_ge(bn_rooted, 1)
                    step(dve.reciprocal(scale[:, :, :], scale[:, :, :]))
                    step(dve.tensor_tensor(scale[:, :, :], scale[:, :, :], bn[:, :, 1, :], ALU.mult))
                    step(dve.tensor_tensor(offset[:, :, :], bn[:, :, 0, :], bn[:, :, 3, :], ALU.subtract))
                    step(dve.tensor_tensor(offset[:, :, :], offset[:, :, :], scale[:, :, :], ALU.mult))
                    step(dve.tensor_tensor(offset[:, :, :], offset[:, :, :], bn[:, :, 2, :], ALU.add))
                    dve.sem_inc(folded, 1)
                    dve.wait_ge(consts_in, 16 * 5)
                    dve.tensor_copy(wr_parts[:, :, 0, :], wr[:, :, :]).then_inc(wr_split, 1)
                    dve.wait_ge(wr_split, 1)
                    dve.tensor_tensor(wr_parts[:, :, 1, :], wr[:, :, :], wr_parts[:, :, 0, :].bitcast(F32), ALU.subtract).then_inc(wr_split, 1)

                    every = [P, G, EXPERTS]
                    COMB, NORM, SMAX = res.DISTANCES + res.SUMS + res.FINISH, 8, 6

                    def before(p):
                        of = ts(p, G)

                        def sum_parts():
                            dve.wait_ge(fin_in, 16 * G * (p + 1))
                            res.distances(dve, Steps(dve, comb, COMB * p), of, fin)
                            dve.sem_inc(weights_wanted, 1)
                            dve.wait_ge(weights_ready, p + 1)
                            res.sum_parts(dve, Steps(dve, comb, COMB * p + res.DISTANCES), of, fin)

                        def finish():
                            step = Steps(dve, comb, COMB * p + res.DISTANCES + res.SUMS)
                            res.finish(dve, step, skip[:, of, :]).then_inc(combined, 1)

                        def add_x(uses):
                            def go():
                                if uses[0] == 0:
                                    dve.wait_ge(x_in, 16 * p + 16)
                                tiles = slice(pairs(uses[0]).start, pairs(uses[-1]).stop)
                                for n in uses:
                                    wait_read(dve, p, PROJECT + n)
                                dve.tensor_tensor(x[:, tiles, :], x[:, tiles, :], y[:, tiles, :], ALU.add).then_inc(residual, 1)
                            return go

                        def statistics():
                            dve.wait_ge(residual, 2 * p + 2)
                            for u in range(G):
                                ins = dve.bn_stats(stat[:, u, :], x[:, u, :])
                            ins.then_inc(stats_done, 1)

                        def moments():
                            dve.wait_ge(stats_done, p + 1)
                            layer_norm_moments(Steps(dve, norm, NORM * p), mv[:, :, 0], mv[:, :, 1], stat)
                            dve.sem_inc(aggregated, 1)

                        def normalise():
                            dve.wait_ge(rooted, p + 1)
                            Steps(dve, norm, NORM * p + 7)(dve.reciprocal(rstd[:, :], rstd[:, :]))
                            for u in range(G):
                                ins = dve.tensor_scalar(y[:, u, :], x[:, u, :], mv[:, u, 0:1], rstd[:, u:u + 1], ALU.subtract, ALU.mult)
                            ins.then_inc(y_ready, 1)

                        def low_y(uses):
                            def go():
                                for n in uses:
                                    dve.wait_ge(y_high, 4 * p + n + 1)
                                    width = P * (pairs(n).stop - pairs(n).start)
                                    at = P * pairs(n).start
                                    dve.tensor_tensor(y_lo[:, :, at:at + width],
                                                      bank_of(TURN_Y + n)[:, :].rearrange("p (c n) -> p c n", c=KC)[:, :, 0:width],
                                                      y_hi[:, :, at:at + width].bitcast(F32), ALU.subtract).then_inc(bank_read[(TURN_Y + n) % 2], 1)
                            return go

                        return {(0, 1): sum_parts, (1, 0): finish,
                                (3, 0): add_x((0, 1)), (4, 0): add_x((2, 3)), (4, 1): statistics, (5, 0): moments,
                                (6, 0): normalise, (6, 1): low_y((0, 1)), (7, 0): low_y((2, 3))}

                    def experts(g, pieces):
                        def low_part(e, layer, k):
                            m, half = divmod(k, 2)
                            n, of = place[e, layer] + k, slice(HTOK * half, HTOK * (half + 1))
                            dve.wait_ge(relued, FREE_RELUED + 2 * (PER * g + n + 1))
                            dve.tensor_tensor(hid_lo[layer][:, m, of], full[:, n % 4, :], hid_hi[layer][:, m, of].bitcast(F32),
                                              ALU.subtract).then_inc(parted, 1)

                        def low_parts(e, layer):
                            for k in range(2 * LH):
                                low_part(e, layer, k)

                        def score():
                            step = Steps(dve, smax, SMAX * g)
                            dve.wait_ge(added, FREE_ADDED + OUTS * g)
                            wait_in_bank(dve, g, ROUTE)
                            scores = bank_of(ROUTE)[:, 0:G * 2 * EXPERTS].rearrange("p (u n e) -> p u n e", n=2, e=EXPERTS)
                            step(dve.tensor_tensor(gate[:, :, :], scores[:, :, 1, :], br[:, :].unsqueeze(1).to_broadcast(every), ALU.add))
                            step(dve.tensor_tensor(gate[:, :, :], gate[:, :, :], scores[:, :, 0, :], ALU.add))
                            dve.sem_inc(bank_read[ROUTE % 2], 1)
                            step(dve.tensor_reduce(red[:, :], gate[:, :, :], AX.X, ALU.max))
                            step(dve.tensor_tensor(gate[:, :, :], gate[:, :, :], red[:, :].unsqueeze(2).to_broadcast(every), ALU.subtract))
                            dve.sem_inc(gap_ready, 1)

                        def weigh():
                            step = Steps(dve, smax, SMAX * g + 4)
                            dve.wait_ge(exp_ready, g + 1)
                            step(dve.tensor_reduce(red[:, :], gate[:, :, :], AX.X, ALU.add))
                            step(dve.reciprocal(red[:, :], red[:, :]))
                            dve.tensor_tensor(gate[:, :, :], gate[:, :, :], red[:, :].unsqueeze(2).to_broadcast(every), ALU.mult).then_inc(gate_ready, 1)

                        def add_biases(e, uses):
                            dve.wait_ge(added, FREE_ADDED + OUTS * g + G * e)
                            for n in uses:
                                tiles = pairs(n)
                                wait_in_bank(dve, g, BIAS + n)
                                dve.tensor_tensor(total[:, tiles, :], total[:, tiles, :],
                                                  bank_of(BIAS + n)[:, 0:(tiles.stop - tiles.start) * D].rearrange("p (u c) -> p u c", c=D),
                                                  ALU.add).then_inc(bias_added, 1)
                            dve.wait_ge(bias_added, 4 * g + uses[-1] + 1)
                            for n in uses:
                                dve.sem_inc(bank_read[(BIAS + n) % 2], 1)

                        def add_output(e, u):
                            n = G * e + u
                            so_far = x if e == 0 else total
                            dve.wait_ge(out_formed, FREE_OUT + OUTS * g + n + 1)
                            if e >= 1:
                                dve.wait_ge(added, FREE_ADDED + OUTS * g + n - G + 1)
                            dve.scalar_tensor_tensor(total[:, u, :], psO[n % len(psO)][:, 0:D], gate[:, u, e:e + 1], so_far[:, u, :],
                                                     ALU.mult, ALU.add).then_inc(added, 1)

                        def add_outputs(e):
                            if e == 0:
                                dve.wait_ge(stored, 16 * g + 16)
                                dve.wait_ge(gate_ready, g + 1)
                            following = e + 1 < EXPERTS
                            if following:
                                low_part(e + 1, 0, 0)
                                low_part(e + 1, 0, 1)
                            for u in range(G):
                                add_output(e, u)
                                if following and u < 2:
                                    low_part(e + 1, 0, 2 + u)

                        low_parts(0, 0)
                        score()
                        for e in range(EXPERTS):
                            low_parts(e, 1)
                            if e == 0:
                                weigh()
                            if e == 1:
                                add_biases(1, (0, 1))
                            run(pieces, e, 0)
                            add_outputs(e)
                            if e == 1:
                                add_biases(2, (2, 3))
                            run(pieces, e, 1)

                    all_groups(dve, before, experts)

        edge_phase(0)
        node_phase()
        first.close()
        pieces = [P, len(EXPERT_LAYERS) * EXPERTS, KC * HID]
        w_hi = whole.enter_context(nc.sbuf_tensor("expert_w_hi", pieces, F32R))
        w_lo = whole.enter_context(nc.sbuf_tensor("expert_w_lo", pieces, F32R))
        edge_phase(1)
        expert_phase()


def kernel(**inputs):
    import concourse.bacc as bacc
    from concourse.bass_utils import run_bass_kernel_spmd

    a = {k: np.asarray(v) for k, v in inputs.items()}
    g, f = "L0_gnn_", "L0_ffn_"

    def side_by_side(kind, n):
        q, k, v, skip = (a[f"{g}{kind}{z}{n}"].T for z in "qkvs")
        pairs = np.stack([k, v], axis=-1).reshape(*k.shape[:-1], 2 * HC)
        return np.ascontiguousarray(np.concatenate([q, pairs, skip], axis=-1))

    x = np.zeros((NP, D), np.float32)
    x[:N] = a["x"]
    src = np.zeros(EP, np.int32)
    src[:E] = a["src"]
    dst = np.full(EP, N, np.int32)
    dst[:E] = a["dst"]
    arrays = {
        "x": x,
        "src": np.ascontiguousarray(src.reshape(STREAMS, BLOCKS, TPB, P).transpose(1, 3, 2, 0).reshape(BLOCKS, P, TPB * STREAMS)),
        "dst": dst,
        "prev": np.concatenate([np.full(1, -1, np.int32), dst[:-1]]),
        "samples": np.ascontiguousarray(dst[:SROWS * SCOLS:SCOLS]),
        "edge_rows": dst[:SROWS * SCOLS].reshape(SROWS, SCOLS).copy(),
        "cut": dst[HALF:HALF + 16].reshape(16, 1).copy(),
        "proj1_w": side_by_side("W", 1), "proj1_b": side_by_side("b", 1),
        "proj2": np.concatenate([side_by_side("W", 2), side_by_side("b", 2)[None]]),
        "wo_bo": np.concatenate([a[g + "Wo"].T, a[g + "bo"][None]]),
        "wr": a[f + "Wr"], "br": a[f + "br"],
        "expert_w": np.ascontiguousarray(np.stack([a[f + n] for n in EXPERT_LAYERS]).reshape(-1, KC, P, HID)
                                         .transpose(0, 2, 1, 3).reshape(-1, P, KC * HID)),
        "bo8": a[f + "bo"],
        "bn": np.ascontiguousarray(np.stack([[a[f"{f}{k}{n}"] for k in ("b", "g", "be", "m", "v")] for n in (1, 2)])
                                   .reshape(2, 5, EXPERTS * HID // P, P).transpose(3, 0, 1, 2)),
    }
    nc = bacc.Bacc("TRN2", target_bir_lowering=False, num_devices=1)
    d, feed = {}, {}
    for name, v in arrays.items():
        d[name] = nc.dram_tensor(f"in_{name}", v.shape, mybir.dt.from_np(v.dtype), kind="ExternalInput").ap()
        feed[f"in_{name}"] = v
    d["out"] = nc.dram_tensor("out", (NP, D), F32, kind="ExternalOutput").ap()
    build(nc, d)
    r = run_bass_kernel_spmd(nc, [feed], core_ids=[0])
    return r.results[0]["out"][:N]
```
